# Optimizing a Trainium2 kernel written in Bass

```python
import numpy as np
import jax
import jax.numpy as jnp

def _softmax(x, axis=-1):
    return jax.nn.softmax(x, axis=axis)

def _gelu(x):
    return jax.nn.gelu(x, approximate=True)

def _silu(x):
    return jax.nn.silu(x)

def _sigmoid(x):
    return jax.nn.sigmoid(x)

def _layernorm(x, axis=-1, eps=1e-05):
    m = jnp.mean(x, axis=axis, keepdims=True)
    v = jnp.var(x, axis=axis, keepdims=True)
    return (x - m) / jnp.sqrt(v + eps)

def _scatter_add(tgt, idx, src, axis=0):
    return tgt.at[idx].add(src)

def _segment_sum(src, seg, n):
    return jax.ops.segment_sum(src, seg, n)
kernel_name = 'mk_macaron_d1_jaxref_r8_5b4eb3'

def setup_inputs(seed: int=0):
    np.random.seed(seed)
    _w = jnp.asarray

    def _L0_attn_setup():
        import jax, jax.numpy as jnp
        import numpy as np
        import math
        D_MODEL = 128
        EXPAND = 2
        D_INNER = EXPAND * D_MODEL
        HEADDIM = 16
        NHEADS = D_INNER // (HEADDIM * 2)
        D_STATE = 16
        NGROUPS = 1
        D_CONV = 4
        CHUNK = 32
        D_IN_PROJ = D_INNER + 2 * NGROUPS * D_STATE + NHEADS
        CONV_DIM = D_INNER // 2 + 2 * NGROUPS * D_STATE

        def _segsum(x):
            T = x.shape[-1]
            cs = jnp.cumsum(x, axis=-1)
            seg = cs[..., :, None] - cs[..., None, :]
            mask = jnp.tril(jnp.ones((T, T), dtype=bool))
            return jnp.where(mask, seg, -jnp.inf)

        def _ssd(X, Adt, B, C, chunk):
            b, l, h, p = X.shape
            c = l // chunk
            n = B.shape[-1]
            X = X.reshape(b, c, chunk, h, p)
            A = Adt.reshape(b, c, chunk, h).transpose(0, 3, 1, 2)
            B = B.reshape(b, c, chunk, n)
            C = C.reshape(b, c, chunk, n)
            A_cs = jnp.cumsum(A, axis=-1)
            Lmat = jnp.exp(_segsum(A))
            Y_diag = jnp.einsum('bcln,bcsn,bhcls,bcshp->bclhp', C, B, Lmat, X)
            decay_states = jnp.exp(A_cs[..., -1:] - A_cs)
            states = jnp.einsum('bcln,bhcl,bclhp->bchpn', B, decay_states, X)
            init = jnp.zeros_like(states[:, :1])
            states_cat = jnp.concatenate([init, states], axis=1)
            A_last = jnp.pad(A_cs[..., -1], ((0, 0), (0, 0), (1, 0)))
            decay_chunk = jnp.exp(_segsum(A_last))
            new_states = jnp.einsum('bhzc,bchpn->bzhpn', decay_chunk, states_cat)
            states_in = new_states[:, :-1]
            out_decay = jnp.exp(A_cs)
            Y_off = jnp.einsum('bcln,bchpn,bhcl->bclhp', C, states_in, out_decay)
            return (Y_diag + Y_off).reshape(b, l, h, p)

        def _forward(u, W_in, conv_w, conv_b, dt_bias, A_log, Dskip, ln_w, ln_b, W_out):
            b, l, _ = u.shape
            zxbcdt = jnp.einsum('bld,ed->ble', u, W_in)
            half = D_INNER // 2
            z = zxbcdt[..., :half]
            xBC = zxbcdt[..., half:half + CONV_DIM]
            dt = zxbcdt[..., half + CONV_DIM:]
            dt = jax.nn.softplus(dt + dt_bias)
            xBC_ncl = xBC.transpose(0, 2, 1)
            xBC_ncl = jax.lax.conv_general_dilated(xBC_ncl, conv_w, window_strides=(1,), padding=[(D_CONV - 1, 0)], feature_group_count=CONV_DIM, dimension_numbers=('NCH', 'OIH', 'NCH'))
            xBC = jax.nn.silu(xBC_ncl.transpose(0, 2, 1) + conv_b)
            x = xBC[..., :half]
            Bm = xBC[..., half:half + NGROUPS * D_STATE]
            Cm = xBC[..., half + NGROUPS * D_STATE:]
            A = -jnp.exp(A_log)
            xh = x.reshape(b, l, NHEADS, HEADDIM)
            y = _ssd(xh * dt[..., None], A * dt, Bm, Cm, CHUNK)
            y = y + xh * Dskip[None, None, :, None]
            y = y.reshape(b, l, half)
            y = jnp.concatenate([y, z], axis=-1)
            mu = jnp.mean(y, axis=-1, keepdims=True)
            var = jnp.mean((y - mu) ** 2, axis=-1, keepdims=True)
            y = (y - mu) / jnp.sqrt(var + 1e-05) * ln_w + ln_b
            return jnp.einsum('ble,de->bld', y, W_out)
        key = jax.random.key(seed)
        ks = jax.random.split(key, 10)
        u = jax.random.normal(ks[0], (2, 256, D_MODEL), dtype=jnp.float32)
        W_in = jax.random.normal(ks[1], (D_IN_PROJ, D_MODEL), dtype=jnp.float32) / math.sqrt(D_MODEL)
        conv_w = jax.random.normal(ks[2], (CONV_DIM, 1, D_CONV), dtype=jnp.float32) / math.sqrt(D_CONV)
        conv_b = jnp.zeros((CONV_DIM,), dtype=jnp.float32)
        dt = jnp.exp(jax.random.uniform(ks[3], (NHEADS,)) * (math.log(0.1) - math.log(0.001)) + math.log(0.001))
        dt = jnp.clip(dt, 0.0001, None)
        dt_bias = (dt + jnp.log(-jnp.expm1(-dt))).astype(jnp.float32)
        A_log = jnp.log(jax.random.uniform(ks[4], (NHEADS,), minval=1.0, maxval=16.0)).astype(jnp.float32)
        Dskip = jnp.ones((NHEADS,), dtype=jnp.float32)
        ln_w = jnp.ones((D_INNER,), dtype=jnp.float32)
        ln_b = jnp.zeros((D_INNER,), dtype=jnp.float32)
        W_out = jax.random.normal(ks[5], (D_MODEL, D_INNER), dtype=jnp.float32) / math.sqrt(D_INNER)
        return {'u': u, 'W_in': W_in, 'conv_w': conv_w, 'conv_b': conv_b, 'dt_bias': dt_bias, 'A_log': A_log, 'Dskip': Dskip, 'ln_w': ln_w, 'ln_b': ln_b, 'W_out': W_out}
    _L0_attn_in = _L0_attn_setup()

    def _L0_ffn_setup():
        import jax, jax.numpy as jnp
        import numpy as np
        BEST_K = 2

        def _expert(xf, w1, w3, w2):
            return jax.nn.silu(xf @ w1) * (xf @ w3) @ w2
        key = jax.random.key(seed)
        ks = jax.random.split(key, 9)
        E, S_sh, D, H = (8, 2, 128, 64)
        B, S = (2, 256)
        w = lambda k, shape: jax.random.normal(k, shape, dtype=jnp.float32) * 0.02
        return {'x': jax.random.normal(ks[0], (B, S, D), dtype=jnp.float32), 'router_w': w(ks[1], (D, E)), 'router_b': jnp.zeros((E,), dtype=jnp.float32), 'routed_w1': w(ks[2], (E, D, H)), 'routed_w3': w(ks[3], (E, D, H)), 'routed_w2': w(ks[4], (E, H, D)), 'shared_w1': w(ks[5], (S_sh, D, H)), 'shared_w3': w(ks[6], (S_sh, D, H)), 'shared_w2': w(ks[7], (S_sh, H, D))}
    _L0_ffn_in = _L0_ffn_setup()
    _d = {'L0_attn_u': _L0_attn_in['u'], 'L0_attn_W_in': _L0_attn_in['W_in'], 'L0_attn_conv_w': _L0_attn_in['conv_w'], 'L0_attn_conv_b': _L0_attn_in['conv_b'], 'L0_attn_dt_bias': _L0_attn_in['dt_bias'], 'L0_attn_A_log': _L0_attn_in['A_log'], 'L0_attn_Dskip': _L0_attn_in['Dskip'], 'L0_attn_ln_w': _L0_attn_in['ln_w'], 'L0_attn_ln_b': _L0_attn_in['ln_b'], 'L0_attn_W_out': _L0_attn_in['W_out'], 'L0_ffn_router_w': _L0_ffn_in['router_w'], 'L0_ffn_router_b': _L0_ffn_in['router_b'], 'L0_ffn_routed_w1': _L0_ffn_in['routed_w1'], 'L0_ffn_routed_w3': _L0_ffn_in['routed_w3'], 'L0_ffn_routed_w2': _L0_ffn_in['routed_w2'], 'L0_ffn_shared_w1': _L0_ffn_in['shared_w1'], 'L0_ffn_shared_w3': _L0_ffn_in['shared_w3'], 'L0_ffn_shared_w2': _L0_ffn_in['shared_w2']}
    _x0 = _d['L0_attn_u']
    _d['L0_attn_u'] = jax.random.normal(jax.random.fold_in(jax.random.key(seed), 1), (8, 512, 128), dtype=_x0.dtype)
    del _x0
    return _d

def reference(L0_attn_u, L0_attn_W_in, L0_attn_conv_w, L0_attn_conv_b, L0_attn_dt_bias, L0_attn_A_log, L0_attn_Dskip, L0_attn_ln_w, L0_attn_ln_b, L0_attn_W_out, L0_ffn_router_w, L0_ffn_router_b, L0_ffn_routed_w1, L0_ffn_routed_w3, L0_ffn_routed_w2, L0_ffn_shared_w1, L0_ffn_shared_w3, L0_ffn_shared_w2):

    def _L0_attn_ref(u, W_in, conv_w, conv_b, dt_bias, A_log, Dskip, ln_w, ln_b, W_out):
        import jax, jax.numpy as jnp
        import numpy as np
        import math
        D_MODEL = 128
        EXPAND = 2
        D_INNER = EXPAND * D_MODEL
        HEADDIM = 16
        NHEADS = D_INNER // (HEADDIM * 2)
        D_STATE = 16
        NGROUPS = 1
        D_CONV = 4
        CHUNK = 32
        D_IN_PROJ = D_INNER + 2 * NGROUPS * D_STATE + NHEADS
        CONV_DIM = D_INNER // 2 + 2 * NGROUPS * D_STATE

        def _segsum(x):
            T = x.shape[-1]
            cs = jnp.cumsum(x, axis=-1)
            seg = cs[..., :, None] - cs[..., None, :]
            mask = jnp.tril(jnp.ones((T, T), dtype=bool))
            return jnp.where(mask, seg, -jnp.inf)

        def _ssd(X, Adt, B, C, chunk):
            b, l, h, p = X.shape
            c = l // chunk
            n = B.shape[-1]
            X = X.reshape(b, c, chunk, h, p)
            A = Adt.reshape(b, c, chunk, h).transpose(0, 3, 1, 2)
            B = B.reshape(b, c, chunk, n)
            C = C.reshape(b, c, chunk, n)
            A_cs = jnp.cumsum(A, axis=-1)
            Lmat = jnp.exp(_segsum(A))
            Y_diag = jnp.einsum('bcln,bcsn,bhcls,bcshp->bclhp', C, B, Lmat, X)
            decay_states = jnp.exp(A_cs[..., -1:] - A_cs)
            states = jnp.einsum('bcln,bhcl,bclhp->bchpn', B, decay_states, X)
            init = jnp.zeros_like(states[:, :1])
            states_cat = jnp.concatenate([init, states], axis=1)
            A_last = jnp.pad(A_cs[..., -1], ((0, 0), (0, 0), (1, 0)))
            decay_chunk = jnp.exp(_segsum(A_last))
            new_states = jnp.einsum('bhzc,bchpn->bzhpn', decay_chunk, states_cat)
            states_in = new_states[:, :-1]
            out_decay = jnp.exp(A_cs)
            Y_off = jnp.einsum('bcln,bchpn,bhcl->bclhp', C, states_in, out_decay)
            return (Y_diag + Y_off).reshape(b, l, h, p)

        def _forward(u, W_in, conv_w, conv_b, dt_bias, A_log, Dskip, ln_w, ln_b, W_out):
            b, l, _ = u.shape
            zxbcdt = jnp.einsum('bld,ed->ble', u, W_in)
            half = D_INNER // 2
            z = zxbcdt[..., :half]
            xBC = zxbcdt[..., half:half + CONV_DIM]
            dt = zxbcdt[..., half + CONV_DIM:]
            dt = jax.nn.softplus(dt + dt_bias)
            xBC_ncl = xBC.transpose(0, 2, 1)
            xBC_ncl = jax.lax.conv_general_dilated(xBC_ncl, conv_w, window_strides=(1,), padding=[(D_CONV - 1, 0)], feature_group_count=CONV_DIM, dimension_numbers=('NCH', 'OIH', 'NCH'))
            xBC = jax.nn.silu(xBC_ncl.transpose(0, 2, 1) + conv_b)
            x = xBC[..., :half]
            Bm = xBC[..., half:half + NGROUPS * D_STATE]
            Cm = xBC[..., half + NGROUPS * D_STATE:]
            A = -jnp.exp(A_log)
            xh = x.reshape(b, l, NHEADS, HEADDIM)
            y = _ssd(xh * dt[..., None], A * dt, Bm, Cm, CHUNK)
            y = y + xh * Dskip[None, None, :, None]
            y = y.reshape(b, l, half)
            y = jnp.concatenate([y, z], axis=-1)
            mu = jnp.mean(y, axis=-1, keepdims=True)
            var = jnp.mean((y - mu) ** 2, axis=-1, keepdims=True)
            y = (y - mu) / jnp.sqrt(var + 1e-05) * ln_w + ln_b
            return jnp.einsum('ble,de->bld', y, W_out)
        return _forward(u, W_in, conv_w, conv_b, dt_bias, A_log, Dskip, ln_w, ln_b, W_out)

    def _L0_ffn_ref(x, router_w, router_b, routed_w1, routed_w3, routed_w2, shared_w1, shared_w3, shared_w2):
        import jax, jax.numpy as jnp
        import numpy as np
        BEST_K = 2

        def _expert(xf, w1, w3, w2):
            return jax.nn.silu(xf @ w1) * (xf @ w3) @ w2
        B, S, D = x.shape
        T = B * S
        xf = x.reshape(T, D)
        logits = xf @ router_w + router_b
        topk_vals, topk_idx = jax.lax.top_k(logits, BEST_K)
        sparse = jnp.full_like(logits, -jnp.inf)
        sparse = sparse.at[jnp.arange(T)[:, None], topk_idx].set(topk_vals)
        gates = jax.nn.softmax(sparse, axis=-1)
        routed = jax.vmap(_expert, in_axes=(None, 0, 0, 0))(xf, routed_w1, routed_w3, routed_w2)
        routed_out = jnp.einsum('etd,te->td', routed, gates)
        shared_out = jax.vmap(_expert, in_axes=(None, 0, 0, 0))(xf, shared_w1, shared_w3, shared_w2).sum(axis=0)
        return (routed_out + shared_out).reshape(B, S, D)
    x = L0_attn_u
    x = x + 0.5 * _L0_ffn_ref(_layernorm(x, axis=-1), L0_ffn_router_w, L0_ffn_router_b, L0_ffn_routed_w1, L0_ffn_routed_w3, L0_ffn_routed_w2, L0_ffn_shared_w1, L0_ffn_shared_w3, L0_ffn_shared_w2)
    x = x + _L0_attn_ref(_layernorm(x, axis=-1), L0_attn_W_in, L0_attn_conv_w, L0_attn_conv_b, L0_attn_dt_bias, L0_attn_A_log, L0_attn_Dskip, L0_attn_ln_w, L0_attn_ln_b, L0_attn_W_out)
    x = x + 0.5 * _L0_ffn_ref(_layernorm(x, axis=-1), L0_ffn_router_w, L0_ffn_router_b, L0_ffn_routed_w1, L0_ffn_routed_w3, L0_ffn_routed_w2, L0_ffn_shared_w1, L0_ffn_shared_w3, L0_ffn_shared_w2)
    return x

_drawn_inputs = setup_inputs


def setup_inputs(seed=0):
    import zlib

    import numpy as np

    out = dict(_drawn_inputs(seed))
    spreads = {'L0_attn_conv_b': (0.0, 0.1),
     'L0_attn_Dskip': (1.0, 0.2),
     'L0_attn_ln_w': (1.0, 0.2),
     'L0_attn_ln_b': (0.0, 0.1),
     'L0_ffn_router_b': (0.0, 0.8)}
    factors = {'L0_ffn_router_w': 8.0,
     'L0_ffn_routed_w1': 8.0,
     'L0_ffn_routed_w3': 8.0,
     'L0_ffn_routed_w2': 8.0,
     'L0_ffn_shared_w1': 8.0,
     'L0_ffn_shared_w3': 8.0,
     'L0_ffn_shared_w2': 8.0}
    for name, (base, spread) in spreads.items():
        noise = np.random.default_rng([zlib.crc32(name.encode()), seed]).standard_normal(out[name].shape)
        drawn = base * np.exp(spread * noise) if base else spread * noise
        out[name] = jnp.asarray(drawn.astype(out[name].dtype))
    for name, factor in factors.items():
        out[name] = (out[name] * factor).astype(out[name].dtype)
    return out
```

```python
import concourse.bass as bass
from concourse import mybir
from contextlib import ExitStack

F32 = mybir.dt.float32
F32R = mybir.dt.float32r
BF16 = mybir.dt.bfloat16
ALU = mybir.AluOpType
ACT = mybir.ActivationFunctionType
AX = mybir.AxisListType

P = 128
B, L, D = 8, 512, 128
SEQ_TILES = L // P
TILES = B * SEQ_TILES
E, H, SHARED = 8, 64, 2
PAIRS = (E + SHARED) // 2
EPS = 1e-5

HEADS, HDIM, STATE, TAPS = 8, 16, 16, 4
CHUNK = 32
BLOCKS = P // CHUNK
CHUNKS = L // CHUNK
HALF = HEADS * HDIM
HGROUPS = HEADS // BLOCKS
ARTANH = [1.0 / (2 * k + 1) for k in range(8)]


class Own:

    def __init__(self, engine, sem, base, most):
        self.engine, self.sem, self.base, self.most, self.n = engine, sem, base, most, 0

    def link(self, instruction):
        self.n += 1
        assert self.n <= self.most
        instruction.then_inc(self.sem, 1)
        self.engine.wait_ge(self.sem, self.base + self.n)

    def close(self):
        assert self.n == self.most


def settle(engine, sem):
    engine.sem_inc(sem, 1)


def split_mm(pe, out, w_hi, w_lo, x_hi, x_lo, start, stop):
    pe.matmul(out, w_hi, x_hi, start=start, stop=False)
    pe.matmul(out, w_hi, x_lo, start=False, stop=False)
    return pe.matmul(out, w_lo, x_hi, start=False, stop=stop)


def run_steps(engine, step):
    step(0, 0, True, False)
    with engine.Fori(0, B // 2 - 1) as k:
        step(k * 2 + 1, 1, False, False)
        step(k * 2 + 2, 0, False, False)
    step(B - 1, 1, False, True)


def ffn_phase(nc, tag, R, load_x, store_x):
    X, ident, identb, eps_pow = R["X"], R["ident"], R["identb"], R["mhalf"]
    with ExitStack() as ctx:
        def sb(name, shape, dt=F32):
            return ctx.enter_context(nc.sbuf_tensor(f"{tag}_{name}", shape, dt))

        def sem(name):
            return ctx.enter_context(nc.semaphore(f"{tag}_{name}"))

        stats = sb("stats", [P, SEQ_TILES, 6])
        mv = [sb(f"mv{p}", [P, SEQ_TILES, 2]) for p in range(2)]
        ve = [sb(f"ve{p}", [P, SEQ_TILES]) for p in range(2)]
        rstd = [sb(f"rstd{p}", [P, SEQ_TILES]) for p in range(2)]
        xn = [sb(f"xn{p}", [P, SEQ_TILES, D]) for p in range(2)]
        xh = [sb(f"xh{p}", [P, L], F32R) for p in range(2)]
        xl = [sb(f"xl{p}", [P, L], F32R) for p in range(2)]
        lg = sb("lg", [P, SEQ_TILES, E])
        lg2 = sb("lg2", [P, SEQ_TILES, E])
        eq = sb("eq", [P, SEQ_TILES, E])
        one1 = sb("one1", [P, SEQ_TILES, E])
        one2 = sb("one2", [P, SEQ_TILES, E])
        m1 = sb("m1", [P, SEQ_TILES])
        m2 = sb("m2", [P, SEQ_TILES])
        km = sb("km", [P, SEQ_TILES])
        dm = sb("dm", [P, SEQ_TILES])
        ed = sb("ed", [P, SEQ_TILES])
        g1 = sb("g1", [P, SEQ_TILES])
        g2 = sb("g2", [P, SEQ_TILES])
        gate = sb("gate", [P, SEQ_TILES, E])
        rest = sb("rest", [P, SEQ_TILES, E])
        parts = [sb(f"parts{p}", [P, SEQ_TILES, 3, E], BF16) for p in range(2)]
        gT = [sb(f"gT{p}", [3 * E, L], BF16) for p in range(2)]
        sil = [sb(f"sil{p}", [P, L]) for p in range(2)]
        pr = [sb(f"pr{p}", [P, L]) for p in range(2)]
        h = [sb(f"h{p}", [P, L]) for p in range(2)]
        hh = [sb(f"hh{p}", [P, L], F32R) for p in range(2)]
        hl = [sb(f"hl{p}", [P, L], F32R) for p in range(2)]
        oT = sb("oT", [P, L])

        PT, PS, PB, PD = R["bank"][0], R["bank"][1], R["bank"][2], R["bank"][3]
        PG = [R["bank"][4], R["bank"][6]]
        PU = [R["bank"][5], R["bank"][7]]
        gTp = PS[0:3 * E, 256:512].bitcast(BF16)

        ve_ready, rstd_ready = sem("ve_ready"), sem("rstd_ready")
        xn_ready, xT_ready = sem("xn_ready"), sem("xT_ready")
        xh_ready, xl_ready = sem("xh_ready"), sem("xl_ready")
        logits_ready, dm_ready, ed_ready = sem("logits_ready"), sem("dm_ready"), sem("ed_ready")
        parts_ready, gTp_ready, gT_ready = sem("parts_ready"), sem("gTp_ready"), sem("gT_ready")
        up_ready, sil_ready = sem("up_ready"), sem("sil_ready")
        prod_ready, bc_ready = sem("prod_ready"), sem("bc_ready")
        h_ready, hh_ready, hl_ready = sem("h_ready"), sem("hh_ready"), sem("hl_ready")
        oT_ready, back_ready = sem("oT_ready"), sem("back_ready")
        down_used = sem("down_used")
        x_done = sem("x_done")
        dve_own = sem("dve_own")
        stored = sem("stored")
        A_OPS, MAX_OPS = 2, 21
        DVE_OPS = A_OPS + MAX_OPS

        def chunk(s, c):
            return s * PAIRS + c

        def parity(p, c):
            return (p * PAIRS + c) % 2

        block = ctx.enter_context(nc.Block())

        @block.sync
        def _(sp):
            if load_x:
                for s in range(2, B):
                    sp.dma_start(X[:, s * SEQ_TILES:(s + 1) * SEQ_TILES, :], R["x_dram"][s])\
                        .then_inc(R["x_loaded"][s], 16)
            if store_x:
                for s in range(B):
                    sp.wait_ge(x_done, s + 1)
                    sp.dma_start(R["out_dram"][s], X[:, s * SEQ_TILES:(s + 1) * SEQ_TILES, :])\
                        .then_inc(stored, 16)
                sp.wait_ge(stored, 16 * B)

        @block.gpsimd
        def _(pool):
            def norm_power(s, p):
                pool.wait_ge(ve_ready, s + 1)
                pool.tensor_tensor(rstd[p][:, :], ve[p][:, :], eps_pow, ALU.pow).then_inc(rstd_ready, 1)

            def softmax_power(s):
                pool.wait_ge(dm_ready, s + 1)
                pool.tensor_tensor(ed[:, :], R["euler"], dm[:, :], ALU.pow).then_inc(ed_ready, 1)

            def low_part(s, p, c):
                n = chunk(s, c)
                b = parity(p, c)
                pool.wait_ge(hh_ready, n + 1)
                pool.tensor_tensor(hl[b][:, :], h[parity(p, c)][:, :], hh[b][:, :], ALU.subtract)\
                    .then_inc(hl_ready, 1)

            norm_power(0, 0)
            softmax_power(0)

            def step(s, p, first, last):
                if not last:
                    norm_power(s + 1, 1 - p)
                low_part(s, p, 0)
                low_part(s, p, 1)
                low_part(s, p, 2)
                if not last:
                    softmax_power(s + 1)
                low_part(s, p, 3)
                low_part(s, p, 4)
            run_steps(pool, step)

        @block.scalar
        def _(act):
            def x_high(s, p):
                act.wait_ge(xT_ready, s + 1)
                act.activation(xh[p][:, :], PT[:, :], ACT.Copy).then_inc(xh_ready, 1)

            def gates_out(s, p):
                act.wait_ge(gTp_ready, s + 1)
                act.activation(gT[p][:, :], gTp, ACT.Copy).then_inc(gT_ready, 1)

            def silu(s, p, c):
                n, b = chunk(s, c), parity(p, c)
                act.wait_ge(up_ready, n + 1)
                act.wait_ge(h_ready, n + 1)
                act.activation(sil[b][:, :], PG[b][:, :], ACT.Silu).then_inc(sil_ready, 1)

            def high_part(s, p, c):
                n = chunk(s, c)
                act.wait_ge(h_ready, n + 1 + 2)
                act.wait_ge(down_used, n + 1)
                act.activation(hh[parity(p, c)][:, :], h[parity(p, c)][:, :], ACT.Copy).then_inc(hh_ready, 1)

            def out_copy(s):
                act.wait_ge(down_used, chunk(s, PAIRS) + 2)
                act.activation(oT[:, :], PD[:, :], ACT.Copy).then_inc(oT_ready, 1)

            act.sem_inc(down_used, 2)
            x_high(0, 0)
            gates_out(0, 0)

            def step(s, p, first, last):
                silu(s, p, 0)
                if not first:
                    out_copy(s - 1)
                silu(s, p, 1)
                high_part(s, p, 0)
                if not last:
                    x_high(s + 1, 1 - p)
                silu(s, p, 2)
                high_part(s, p, 1)
                silu(s, p, 3)
                high_part(s, p, 2)
                if not last:
                    gates_out(s + 1, 1 - p)
                silu(s, p, 4)
                high_part(s, p, 3)
                high_part(s, p, 4)
            run_steps(act, step)
            out_copy(B - 1)

        @block.vector
        def _(dve):
            def normalise(s, p, first=False):
                own = Own(dve, dve_own, s * DVE_OPS, A_OPS)
                if load_x and first:
                    dve.wait_ge(R["x_loaded"][0], 16)
                seq = X[:, bass.ds(s * SEQ_TILES, SEQ_TILES), :]
                for t in range(SEQ_TILES):
                    i = dve.bn_stats(stats[:, t, :], X[:, bass.ds(s * SEQ_TILES + t, 1), :])
                own.link(i)
                settle(dve, R["settled"])
                for t in range(SEQ_TILES):
                    i = dve.bn_aggr(mv[p][:, t, :], stats[:, t, :])
                own.link(i)
                dve.tensor_scalar(ve[p][:, :], mv[p][:, :, 1], EPS, None, ALU.add).then_inc(ve_ready, 1)
                dve.wait_ge(rstd_ready, s + 1)
                for t in range(SEQ_TILES):
                    i = dve.tensor_scalar(xn[p][:, t:t + 1, :], X[:, bass.ds(s * SEQ_TILES + t, 1), :],
                                          mv[p][:, t, 0:1], rstd[p][:, t:t + 1], ALU.subtract, ALU.mult)
                i.then_inc(xn_ready, 1)
                own.close()

            def x_low(s, p):
                dve.wait_ge(xh_ready, s + 1)
                dve.tensor_tensor(xl[p][:, :], PT[:, :], xh[p][:, :], ALU.subtract).then_inc(xl_ready, 1)

            def over_experts(a):
                return a[:, :].rearrange("p (t o) -> p t o", o=1).to_broadcast([P, SEQ_TILES, E])

            def over_tiles(a):
                return a.rearrange("p (o e) -> p o e", o=1).to_broadcast([P, SEQ_TILES, E])

            def gates(s, p):
                own = Own(dve, dve_own, s * DVE_OPS + A_OPS, MAX_OPS)
                link = own.link
                dve.wait_ge(logits_ready, s + 1)
                logits = PS[:, 0:SEQ_TILES * E].rearrange("p (t e) -> p t e", e=E)
                link(dve.tensor_tensor(lg[:, :, :], logits, over_tiles(R["router_b"][:, :]), ALU.add))
                for src, top, one in ((lg, m1, one1), (lg2, m2, one2)):
                    link(dve.tensor_reduce(top[:, :], src[:, :, :], AX.X, ALU.max))
                    link(dve.tensor_tensor(eq[:, :, :], src[:, :, :], over_experts(top), ALU.is_equal))
                    link(dve.tensor_tensor(eq[:, :, :], eq[:, :, :], over_tiles(R["order"]), ALU.mult))
                    link(dve.tensor_reduce(km[:, :], eq[:, :, :], AX.X, ALU.max))
                    link(dve.tensor_tensor(one[:, :, :], eq[:, :, :], over_experts(km), ALU.is_equal))
                    if src is lg:
                        link(dve.scalar_tensor_tensor(lg2[:, :, :], one1[:, :, :], -3.0e38, lg[:, :, :],
                                                      ALU.mult, ALU.add))
                dve.tensor_tensor(dm[:, :], m2[:, :], m1[:, :], ALU.subtract).then_inc(dm_ready, 1)
                dve.wait_ge(ed_ready, s + 1)
                link(dve.tensor_scalar(g2[:, :], ed[:, :], 1.0, None, ALU.add))
                link(dve.reciprocal(g1[:, :], g2[:, :]))
                link(dve.tensor_tensor(g2[:, :], ed[:, :], g1[:, :], ALU.mult))
                link(dve.tensor_tensor(one1[:, :, :], one1[:, :, :], over_experts(g1), ALU.mult))
                link(dve.tensor_tensor(one2[:, :, :], one2[:, :, :], over_experts(g2), ALU.mult))
                link(dve.tensor_tensor(gate[:, :, :], one1[:, :, :], one2[:, :, :], ALU.add))
                link(dve.tensor_copy(parts[p][:, :, 0, :], gate[:, :, :]))
                link(dve.tensor_tensor(rest[:, :, :], gate[:, :, :], parts[p][:, :, 0, :], ALU.subtract))
                link(dve.tensor_copy(parts[p][:, :, 1, :], rest[:, :, :]))
                dve.tensor_tensor(parts[p][:, :, 2, :], rest[:, :, :], parts[p][:, :, 1, :], ALU.subtract)\
                    .then_inc(parts_ready, 1)
                own.close()

            def hidden(s, p, c):
                n, b = chunk(s, c), parity(p, c)
                dve.wait_ge(sil_ready, n + 1)
                dve.wait_ge(hl_ready, n + 1)
                if c == 0:
                    dve.tensor_tensor(h[b][:, :], sil[b][:, :], PU[b][:, :], ALU.mult).then_inc(h_ready, 1)
                else:
                    dve.tensor_tensor(pr[b][:, :], sil[b][:, :], PU[b][:, :], ALU.mult).then_inc(prod_ready, 1)
                    dve.wait_ge(prod_ready, s * (PAIRS - 1) + c)
                    dve.wait_ge(bc_ready, s * (PAIRS - 1) + c)
                    dve.tensor_tensor(h[b][:, :], pr[b][:, :], PB[:, :], ALU.mult).then_inc(h_ready, 1)

            def residual(s):
                dve.wait_ge(back_ready, s + 1)
                dve.tensor_tensor(X[:, bass.ds(s * SEQ_TILES, SEQ_TILES), :],
                                  X[:, bass.ds(s * SEQ_TILES, SEQ_TILES), :],
                                  PT[:, :].rearrange("p (t d) -> p t d", d=D), ALU.add).then_inc(x_done, 1)

            dve.sem_inc(h_ready, 2)
            normalise(0, 0, True)
            x_low(0, 0)
            gates(0, 0)

            def step(s, p, first, last):
                hidden(s, p, 0)
                if not first:
                    residual(s - 1)
                if not last:
                    normalise(s + 1, 1 - p)
                hidden(s, p, 1)
                if not last:
                    x_low(s + 1, 1 - p)
                hidden(s, p, 2)
                if not last:
                    gates(s + 1, 1 - p)
                hidden(s, p, 3)
                hidden(s, p, 4)
            if load_x:
                for s in range(1, B):
                    dve.wait_ge(R["x_loaded"][s], 16)
            run_steps(dve, step)
            residual(B - 1)

        @block.tensor
        def _(pe):
            def x_turn(s, p):
                pe.wait_ge(xn_ready, s + 1)
                for t in range(SEQ_TILES):
                    i = pe.transpose(PT[:, t * P:(t + 1) * P], xn[p][:, t, :], ident)
                i.then_inc(xT_ready, 1)

            def router(s, p):
                pe.wait_ge(xl_ready, s + 1)
                for t in range(SEQ_TILES):
                    tile = slice(t * P, (t + 1) * P)
                    out = PS[:, t * E:(t + 1) * E]
                    pe.matmul(out, xh[p][:, tile], R["rw_hi"][:, :], start=(t == 0), stop=False, skip_group_check=True)
                    pe.matmul(out, xh[p][:, tile], R["rw_lo"][:, :], start=False, stop=False, skip_group_check=True)
                    pe.matmul(out, xl[p][:, tile], R["rw_hi"][:, :], start=False, stop=False, skip_group_check=True)
                    i = pe.matmul(out, xl[p][:, tile], R["rw_lo"][:, :], start=False, stop=True, skip_group_check=True)
                i.then_inc(logits_ready, 1)

            def gates_turn(s, p):
                pe.wait_ge(parts_ready, s + 1)
                for t in range(SEQ_TILES):
                    i = pe.transpose(gTp[:, t * P:(t + 1) * P], parts[p][:, t, :, :].rearrange("p k e -> p (k e)"),
                                     identb[:, :])
                i.then_inc(gTp_ready, 1)

            def up(s, p, c):
                n, b = chunk(s, c), parity(p, c)
                pe.wait_ge(h_ready, n + 1)
                cols = slice(c * P, (c + 1) * P)
                split_mm(pe, PG[b][:, :], R["wg_hi"][:, cols], R["wg_lo"][:, cols], xh[p][:, :], xl[p][:, :], True, True)
                split_mm(pe, PU[b][:, :], R["wu_hi"][:, cols], R["wu_lo"][:, cols], xh[p][:, :], xl[p][:, :], True, True)\
                    .then_inc(up_ready, 1)
                if c:
                    if c == 1:
                        pe.wait_ge(gT_ready, s + 1)
                    pe.wait_ge(h_ready, n + 2)
                    pe.matmul(PB[:, :], R["selb"][:, (c - 1) * P:c * P], gT[p][:, :], start=True, stop=True)\
                        .then_inc(bc_ready, 1)

            def down(s, p, c):
                n, b = chunk(s, c), parity(p, c)
                pe.wait_ge(hl_ready, n + 1 + 2)
                if c == 0:
                    pe.wait_ge(oT_ready, s + 1)
                cols = slice(c * P, (c + 1) * P)
                split_mm(pe, PD[:, :], R["wd_hi"][:, cols], R["wd_lo"][:, cols], hh[b][:, :], hl[b][:, :],
                         c == 0, c == PAIRS - 1).then_inc(down_used, 1)

            def back(s):
                pe.wait_ge(oT_ready, s + 1 + 1)
                for t in range(SEQ_TILES):
                    i = pe.transpose(PT[:, t * P:(t + 1) * P], oT[:, t * P:(t + 1) * P], ident)
                i.then_inc(back_ready, 1)

            pe.sem_inc(oT_ready, 1)
            pe.sem_inc(hl_ready, 2)
            x_turn(0, 0)
            router(0, 0)
            gates_turn(0, 0)

            def step(s, p, first, last):
                up(s, p, 0)
                up(s, p, 1)
                if not first:
                    back(s - 1)
                if not last:
                    x_turn(s + 1, 1 - p)
                up(s, p, 2)
                down(s, p, 0)
                if not last:
                    router(s + 1, 1 - p)
                up(s, p, 3)
                down(s, p, 1)
                down(s, p, 2)
                up(s, p, 4)
                if not last:
                    gates_turn(s + 1, 1 - p)
                down(s, p, 3)
                down(s, p, 4)
            run_steps(pe, step)
            back(B - 1)


CONSTANTS = {}


def constants():
    import numpy as np
    row = np.arange(P)
    made = {"ident": np.eye(P),
            "mhalf": np.full((P, SEQ_TILES), -0.5),
            "euler": np.full((P, SEQ_TILES), np.exp(1.0)),
            "order": np.tile(E - np.arange(E), (P, 1)),
            "sel": np.kron((row[:, None] % E == np.arange(E)) & (row[:, None] < 3 * E), np.ones((1, H)))}
    block, inner = row // CHUNK, row % CHUNK
    same = block[:, None] == block
    made |= {
        "upto": same & (inner[:, None] <= inner),
        "after": same & (inner[:, None] > inner),
        "spread": inner[:, None] == inner,
        "spread_one": np.concatenate([(inner[:, None] == inner) & (block[:, None] == c) for c in range(BLOCKS)], axis=1),
        "own_block": block[:, None] == np.arange(BLOCKS),
        "causal": inner[:, None] <= np.arange(CHUNK),
        "causal_block": same & (inner[:, None] <= inner),
        "own_tile": np.kron(row[:, None] // HEADS == np.arange(SEQ_TILES), np.ones((1, BLOCKS))),
        "own_head": row[:, None] % HEADS == row // HDIM,
        "own_chunk": row[:, None] // STATE == block,
        "head_of": row[:, None] // HDIM == np.arange(HEADS)}
    at = 0
    for name, a in made.items():
        CONSTANTS[name] = (at, a.shape[1])
        at += a.shape[1]
    return np.ascontiguousarray(np.concatenate([a.astype(np.float32) for a in made.values()], axis=1))


def setup(nc, R, ins, ctx):
    def sb(name, shape, dt=F32):
        return ctx.enter_context(nc.sbuf_tensor(name, shape, dt))

    def sem(name):
        return ctx.enter_context(nc.semaphore(name))

    NU = PAIRS * P
    R["settled"] = sem("settled")
    R["X"] = sb("X", [P, TILES, D])
    R["x_loaded"] = [sem(f"x_loaded{s}") for s in range(B)]
    R["const"] = sb("const", [P, ins["constants"].shape[1]])
    for name, (at, n) in CONSTANTS.items():
        R[name] = R["const"][:, at:at + n]
    for name, shape, dt in (("identb", [P, P], BF16), ("router_b", [P, E], F32),
                            ("selb", [3 * E, E * H], BF16), ("rw", [P, E], F32), ("rw_hi", [P, E], F32R), ("rw_lo", [P, E], F32R),
                            ("wg_hi", [P, NU], F32R), ("wg_lo", [P, NU], F32R), ("wu_hi", [P, NU], F32R),
                            ("wu_lo", [P, NU], F32R), ("wd_hi", [P, NU], F32R), ("wd_lo", [P, NU], F32R)):
        R[name] = sb(name, shape, dt)
    R["bank"] = [ctx.enter_context(nc.psum_tensor(f"bank{k}", [P, 512], F32)) for k in range(8)]
    x_dram = ins["L0_attn_u"].rearrange("b (t p) d -> b p t d", p=P)
    R["x_dram"] = [x_dram[s] for s in range(B)]

    with ExitStack() as own_ctx:
        wg, wu, wd = (own_ctx.enter_context(nc.sbuf_tensor(f"{n}_in", [P, NU], F32)) for n in ("wg", "wu", "wd"))
        small_in, up_in, down_in, const_in, hi_ready = (own_ctx.enter_context(nc.semaphore(n)) for n in (
            "small_in", "up_in", "down_in", "const_in", "hi_ready"))
        block = own_ctx.enter_context(nc.Block())

        @block.sync
        def _(sp):
            sp.dma_start(R["const"][:, :], ins["constants"]).then_inc(const_in, 16)
            for s in range(2):
                sp.dma_start(R["X"][:, s * SEQ_TILES:(s + 1) * SEQ_TILES, :], R["x_dram"][s]).then_inc(R["x_loaded"][s], 16)
            for w, which in ((wg, "w1"), (wu, "w3")):
                v = w[:, :].rearrange("p (e h) -> p e h", h=H)
                sp.dma_start(v[:, 0:SHARED, :], ins[f"L0_ffn_shared_{which}"].rearrange("e d h -> d e h")).then_inc(up_in, 16)
                sp.dma_start(v[:, SHARED:, :], ins[f"L0_ffn_routed_{which}"].rearrange("e d h -> d e h")).then_inc(up_in, 16)

        @block.scalar
        def _(act):
            act.dma_start(R["rw"][:, :], ins["L0_ffn_router_w"]).then_inc(small_in, 16)
            act.dma_start(R["router_b"][:, :], ins["L0_ffn_router_b"].rearrange("(o e) -> o e", o=1).to_broadcast([P, E])).then_inc(small_in, 16)
            v = wd[:, :].rearrange("p (j d) -> p j d", d=D)
            act.dma_start(v[:, 0:1, :], ins["L0_ffn_shared_w2"].rearrange("(j e) h d -> (e h) j d", e=2)).then_inc(down_in, 16)
            act.dma_start(v[:, 1:, :], ins["L0_ffn_routed_w2"].rearrange("(j e) h d -> (e h) j d", e=2)).then_inc(down_in, 16)
            act.wait_ge(small_in, 32)
            act.activation(R["rw_hi"][:, :], R["rw"][:, :], ACT.Copy).then_inc(hi_ready, 1)
            act.wait_ge(up_in, 64)
            act.activation(R["wg_hi"][:, :], wg[:, :], ACT.Copy).then_inc(hi_ready, 1)
            act.activation(R["wu_hi"][:, :], wu[:, :], ACT.Copy).then_inc(hi_ready, 1)
            act.wait_ge(down_in, 32)
            act.activation(R["wd_hi"][:, :], wd[:, :], ACT.Copy, scale=0.5).then_inc(hi_ready, 1)

        @block.vector
        def _(dve):
            dve.wait_ge(const_in, 16)
            dve.tensor_copy(R["identb"][:, :], R["ident"])
            dve.tensor_copy(R["selb"][:, :], R["sel"][0:3 * E, :])
            for n, (name, src) in enumerate((("rw", R["rw"]), ("wg", wg), ("wu", wu))):
                dve.wait_ge(hi_ready, n + 1)
                dve.tensor_tensor(R[f"{name}_lo"][:, :], src[:, :], R[f"{name}_hi"][:, :], ALU.subtract)
            dve.wait_ge(hi_ready, 4)
            dve.scalar_tensor_tensor(R["wd_lo"][:, :], wd[:, :], 0.5, R["wd_hi"][:, :], ALU.mult, ALU.subtract)


def mamba_setup(nc, R, ins, ctx):
    def sb(name, shape, dt=F32):
        R[name] = ctx.enter_context(nc.sbuf_tensor(name, shape, dt))
        return R[name]

    W = TAPS * P
    for name, n in (("wz", P + HEADS), ("wx", W), ("wbc", W)):
        sb(f"{name}_hi", [P, n], F32R)
        sb(f"{name}_lo", [P, n], F32R)
    sb("wo", [P, 2 * D])
    sb("out_bias", [P, 1])
    sb("decay_rate", [P, HEADS])
    sb("dt_bias", [P, HEADS])
    sb("skip", [P, HALF])
    sb("cb_x", [P, 1])
    sb("cb_bc", [P, 1])
    W_in, conv_w, conv_b = ins["L0_attn_W_in"], ins["L0_attn_conv_w"], ins["L0_attn_conv_b"]

    with ExitStack() as own_ctx:
        def tmp(name, shape, dt=F32):
            return own_ctx.enter_context(nc.sbuf_tensor(name, shape, dt))

        def sem(name):
            return own_ctx.enter_context(nc.semaphore(name))

        rz, rx, rbc, rdt = tmp("rz", [P, D]), tmp("rx", [P, D]), tmp("rbc", [P, D]), tmp("rdt", [HEADS, D])
        cw_x, cw_bc = tmp("cw_x", [P, TAPS]), tmp("cw_bc", [P, TAPS])
        tx, tbc = tmp("tx", [P, TAPS, D]), tmp("tbc", [P, TAPS, D])
        wo_rows, wo_raw = tmp("wo_rows", [P, 2 * D]), tmp("wo_raw", [P, 2 * D])
        lnw, lnb = tmp("lnw", [P, 2]), tmp("lnb", [P, 2])
        alog, dskip, dcol, dcol8 = tmp("alog", [P, HEADS]), tmp("dskip", [P, HEADS]), tmp("dcol", [P, 1]), tmp("dcol8", [P, HEADS])
        cleared, rows_in, taps_ready, turned = sem("cleared"), sem("rows_in"), sem("taps_ready"), sem("turned")
        high, raw_ready, bias_ready, own, small = sem("high"), sem("raw_ready"), sem("bias_ready"), sem("own_s"), sem("small_m")
        expd = sem("expd")
        bk = R["bank"]
        block = own_ctx.enter_context(nc.Block())
        B0, C0, DT0 = 2 * HALF, 2 * HALF + STATE, 2 * HALF + 2 * STATE

        def col(v):
            return v.rearrange("(p o) -> p o", o=1)

        @block.sync
        def _(sp):
            sp.dma_start(rz[:, :], W_in[0:HALF, :]).then_inc(rows_in, 16)
            sp.dma_start(rx[:, :], W_in[HALF:2 * HALF, :]).then_inc(rows_in, 16)
            sp.dma_start(rdt[:, :], W_in[DT0:DT0 + HEADS, :]).then_inc(rows_in, 16)
            sp.dma_start(cw_x[:, :], conv_w[0:HALF, 0, :]).then_inc(rows_in, 16)
            sp.dma_start(R["cb_x"][:, :], col(conv_b[0:HALF])).then_inc(rows_in, 16)
            sp.dma_start(wo_rows[:, :], ins["L0_attn_W_out"]).then_inc(rows_in, 16)
            sp.wait_ge(cleared, 3)
            for r in range(BLOCKS + 1):
                src = C0 if r < BLOCKS else B0
                rows = slice(r * STATE, (r + 1) * STATE)
                sp.dma_start(rbc[rows, :], W_in[src:src + STATE, :]).then_inc(rows_in, 16)
                sp.dma_start(cw_bc[rows, :], conv_w[src - HALF:src - HALF + STATE, 0, :]).then_inc(rows_in, 16)
                sp.dma_start(R["cb_bc"][rows, :], col(conv_b[src - HALF:src - HALF + STATE])).then_inc(rows_in, 16)

        @block.scalar
        def _(act):
            def row(v):
                return v.rearrange("(o e) -> o e", o=1).to_broadcast([P, HEADS])
            act.dma_start(alog[:, :], row(ins["L0_attn_A_log"])).then_inc(small, 16)
            act.dma_start(dskip[:, :], row(ins["L0_attn_Dskip"])).then_inc(small, 16)
            act.dma_start(R["dt_bias"][:, :], row(ins["L0_attn_dt_bias"])).then_inc(small, 16)
            for j in range(2):
                act.dma_start(lnw[:, j:j + 1], col(ins["L0_attn_ln_w"][j * P:(j + 1) * P])).then_inc(small, 16)
                act.dma_start(lnb[:, j:j + 1], col(ins["L0_attn_ln_b"][j * P:(j + 1) * P])).then_inc(small, 16)
            act.wait_ge(small, 16 * 7)
            act.activation(alog[:, :], alog[:, :], ACT.Exp).then_inc(expd, 1)
            for n, (name, k) in enumerate((("wz", P + HEADS), ("wx", W), ("wbc", W))):
                act.wait_ge(turned, n + 1)
                act.activation(R[f"{name}_hi"][:, :], bk[n][:, 0:k], ACT.Copy).then_inc(high, 1)

        @block.vector
        def _(dve):
            dve.memset(rbc[:, :], 0.0).then_inc(cleared, 1)
            dve.memset(cw_bc[:, :], 0.0).then_inc(cleared, 1)
            dve.memset(R["cb_bc"][:, :], 0.0).then_inc(cleared, 1)
            dve.wait_ge(rows_in, 16 * (6 + 3 * (BLOCKS + 1)))
            for t in range(TAPS):
                dve.tensor_scalar(tx[:, t, :], rx[:, :], cw_x[:, t:t + 1], None, ALU.mult)
                i = dve.tensor_scalar(tbc[:, t, :], rbc[:, :], cw_bc[:, t:t + 1], None, ALU.mult)
            i.then_inc(taps_ready, 1)
            dve.wait_ge(expd, 1)
            dve.tensor_scalar(R["decay_rate"][:, :], alog[:, :], -1.0, None, ALU.mult)
            dve.tensor_tensor(dcol8[:, :], dskip[:, :], R["head_of"], ALU.mult).then_inc(own, 1)
            dve.wait_ge(own, 1)
            dve.tensor_reduce(dcol[:, :], dcol8[:, :], AX.X, ALU.add).then_inc(own, 1)
            dve.wait_ge(own, 2)
            dve.tensor_scalar(R["skip"][:, :], R["ident"], dcol[:, 0:1], None, ALU.mult)
            for n, (name, k) in enumerate((("wz", P + HEADS), ("wx", W), ("wbc", W))):
                dve.wait_ge(high, n + 1)
                dve.tensor_tensor(R[f"{name}_lo"][:, :], bk[n][:, 0:k], R[f"{name}_hi"][:, :], ALU.subtract)
            dve.wait_ge(turned, 4)
            dve.tensor_copy(wo_raw[:, :], bk[3][:, 0:2 * D]).then_inc(raw_ready, 1)
            dve.wait_ge(raw_ready, 1)
            for j in range(2):
                dve.tensor_scalar(R["wo"][:, j * D:(j + 1) * D], wo_raw[:, j * D:(j + 1) * D], lnw[:, j:j + 1], None, ALU.mult)
            dve.wait_ge(bias_ready, 1)
            dve.tensor_copy(R["out_bias"][:, :], bk[4][:, 0:1])

        @block.tensor
        def _(pe):
            pe.wait_ge(taps_ready, 1)
            pe.transpose(bk[0][:, 0:P], rz[:, :], R["ident"])
            pe.transpose(bk[0][:, P:P + HEADS], rdt[:, :], R["ident"][0:HEADS, 0:HEADS]).then_inc(turned, 1)
            for t in range(TAPS):
                i = pe.transpose(bk[1][:, t * P:(t + 1) * P], tx[:, t, :], R["ident"])
            i.then_inc(turned, 1)
            for t in range(TAPS):
                i = pe.transpose(bk[2][:, t * P:(t + 1) * P], tbc[:, t, :], R["ident"])
            i.then_inc(turned, 1)
            for j in range(2):
                i = pe.transpose(bk[3][:, j * D:(j + 1) * D], wo_rows[:, j * D:(j + 1) * D], R["ident"])
            i.then_inc(turned, 1)
            pe.wait_ge(raw_ready, 1)
            pe.wait_ge(small, 16 * 7)
            pe.matmul(bk[4][:, 0:1], wo_raw[:, 0:D], lnb[:, 0:1], start=True, stop=False)
            pe.matmul(bk[4][:, 0:1], wo_raw[:, D:2 * D], lnb[:, 1:2], start=False, stop=True).then_inc(bias_ready, 1)


def mamba_phase(nc, R):
    X, bk = R["X"], R["bank"]
    with ExitStack() as ctx:
        def sb(name, shape, dt=F32):
            return ctx.enter_context(nc.sbuf_tensor(f"m_{name}", shape, dt))

        produced = {}

        def sems(engine, names):
            produced[engine] = names.split()
            return [ctx.enter_context(nc.semaphore(f"m_{n}")) for n in names.split()]

        TH = SEQ_TILES * HEADS
        stats, mv = sb("stats", [P, SEQ_TILES, 6]), sb("mv", [P, SEQ_TILES, 2])
        ve, rstd = sb("ve", [P, SEQ_TILES]), sb("rstd", [P, SEQ_TILES])
        xn = sb("xn", [P, SEQ_TILES, D])
        PAD = TAPS - 1
        xh = [sb(f"xh{p}", [P, PAD + L], F32R) for p in range(2)]
        xl = [sb(f"xl{p}", [P, PAD + L], F32R) for p in range(2)]
        raw, neg, u, v, w, q, pos = (sb(n, [P, TH]) for n in ("raw", "neg", "u", "v", "w", "q", "pos"))
        dt = [sb(f"dt{p}", [P, TH]) for p in range(2)]
        at = sb("at", [P, TH])
        ecd = [sb(f"ecd{p}", [P, 2 * TH]) for p in range(2)]
        amask, aB = sb("amask", [P, P]), [sb(f"aB{p}", [P, CHUNKS * HGROUPS]) for p in range(2)]
        totX = sb("totX", [TH, CHUNKS])
        carry = [sb(f"carry{p}", [P, STATE, CHUNKS]) for p in range(2)]
        yz = sb("yz", [P, SEQ_TILES, 2 * HALF])
        xc, Cc, Bc = sb("xc", [P, L]), sb("Cc", [BLOCKS * STATE, L]), sb("Bc", [STATE, L])
        xdt, xdec = sb("xdt", [P, L]), sb("xdec", [P, L])
        XB = sb("XB", [P, SEQ_TILES, BLOCKS, HGROUPS, BLOCKS * HDIM])
        Bm, Gm = sb("Bm", [P, SEQ_TILES, BLOCKS, STATE]), sb("Gm", [P, SEQ_TILES, P])
        Rg = [sb(f"Rg{g}", [P, CHUNKS, CHUNK]) for g in range(HGROUPS)]
        Eg = [sb(f"Eg{g}", [P, L]) for g in range(HGROUPS)]
        Mg = [sb(f"Mg{g}", [P, BLOCKS, SEQ_TILES, CHUNK]) for g in range(HGROUPS)]
        after_chunk, into_chunk = sb("after_chunk", [P, STATE, CHUNKS]), sb("into_chunk", [P, CHUNKS, STATE])
        STs, Cm, yo = sb("STs", [BLOCKS * STATE, L]), sb("Cm", [BLOCKS * STATE, L]), sb("yo", [P, L])
        stats2, mv2 = sb("stats2", [P, SEQ_TILES, 6]), sb("mv2", [P, SEQ_TILES, 2])
        ve2, rstd2 = sb("ve2", [P, SEQ_TILES]), sb("rstd2", [P, SEQ_TILES])
        yzn = sb("yzn", [P, SEQ_TILES, 2 * HALF])
        yT = [sb(f"yT{j}", [P, L]) for j in range(2)]
        oT = sb("oT", [P, L])

        PT, PS = bk[0], bk[1]
        PZ, PX, PBC, PXT = bk[2], bk[3], bk[4], bk[5]
        PSEG = [bk[6], bk[7]]
        PBT, PG, PGR, PY = bk[2], bk[3], bk[4], bk[5]
        PST, PSTT, PYO = bk[2], bk[3], bk[6]
        PYT, PO = [bk[2], bk[3]], bk[7]

        (s_xT, s_dt, s_cum, s_dtp, s_z, s_x, s_bc, s_xt, s_bt, s_g, s_gr, s_seg0, s_seg1, s_y, s_st, s_stt, s_yoff,
         s_yt, s_o, s_back) = sems("pe", "xT_ready dt_ready cum_ready total_ready z_ready x_ready bc_ready "
                                   "xt_ready bt_ready g_ready g_spread seg0_ready seg1_ready y_ready st_ready "
                                   "stt_ready yoff_ready yt_ready o_ready back_ready")
        pe_sems = (s_xT, s_dt, s_cum, s_dtp, s_z, s_x, s_bc, s_xt, s_bt, s_g, s_gr, s_seg0, s_seg1, s_y, s_st, s_stt, s_yoff,
                   s_yt, s_o, s_back)
        act_sems = (s_xh, s_u, s_ecd, s_carry, s_zc, s_xc, s_bcs, s_E0, s_E1, s_STs, s_yT, s_oT) = sems(
            "act", "xh_copied exp_ready decay_ready carry_ready z_copied xc_ready cb_ready e0_ready e1_ready "
            "states_copied yT_ready oT_ready")
        dve_sems = (s_ve, s_xn, s_xl, s_neg, s_at, s_aB, s_totX, s_xdt, s_xdec, s_XB, s_Bm, s_Gm, s_M0, s_M1, s_scan,
                    s_yo, s_yzy, s_ve2, s_yzn, s_xdone) = sems(
            "dve", "ve_ready xn_ready xl_ready neg_ready at_ready ab_ready totx_ready xdt_ready xdec_ready xb_ready "
            "bm_ready gm_ready m0_ready m1_ready scan_done yo_ready yzy_ready ve2_ready yzn_ready x_done")
        pool_sems = (s_rstd, s_R0, s_R1, s_Cm, s_Sin, s_rstd2) = sems(
            "pool", "rstd_ready r0_ready r1_ready cm_ready sin_ready rstd2_ready")
        s_own, s_own2 = sems("own", "own own2")
        OWN_OPS = (2, 14, 1)
        OWN = sum(OWN_OPS)

        def starts(engine, made):
            for one in made:
                engine.sem_inc(one, 1)

        def now(engine, *which):
            s, which = which[-1], which[:-1]
            for one in which:
                engine.wait_ge(one, s + 2)

        def before(engine, *which):
            s, which = which[-1], which[:-1]
            for one in which:
                engine.wait_ge(one, s + 1)

        def tiles(a, n=D):
            return a[:, :].rearrange("p (t d) -> p t d", d=n)

        block = ctx.enter_context(nc.Block())

        @block.gpsimd
        def _(pool):
            starts(pool, pool_sems)

            def norm(s):
                now(pool, s_ve, s)
                pool.tensor_tensor(rstd[:, :], ve[:, :], R["mhalf"], ALU.pow).then_inc(s_rstd, 1)

            def step(s, p, first, last):
                now(pool, s_aB, s)
                for g, (seg, done) in enumerate(((s_seg0, s_R0), (s_seg1, s_R1))):
                    before(pool, seg, s)
                    a = aB[p][:, :].rearrange("p (c g o) -> p c g o", g=HGROUPS, o=1)[:, :, g, :]
                    pool.tensor_tensor(Rg[g][:, :, :], a.to_broadcast([P, CHUNKS, CHUNK]),
                                       R["causal"].rearrange("p (o l) -> p o l", o=1).to_broadcast([P, CHUNKS, CHUNK]),
                                       ALU.mult).then_inc(done, 1)
                now(pool, s_bcs, s)
                before(pool, s_yoff, s)
                pool.tensor_tensor(tiles(Cm, P), tiles(Cc, P),
                                   R["own_chunk"][0:BLOCKS * STATE, :].rearrange("p (o l) -> p o l", o=1)
                                   .to_broadcast([BLOCKS * STATE, SEQ_TILES, P]), ALU.mult).then_inc(s_Cm, 1)
                if not last:
                    norm(s + 1)
                now(pool, s_scan, s)
                before(pool, s_stt, s)
                settle(pool, R["settled"])
                pool.tensor_copy(into_chunk[:, 1:, :],
                                 after_chunk[:, :, 0:CHUNKS - 1].rearrange("p n c -> p c n")).then_inc(s_Sin, 1)
                now(pool, s_ve2, s)
                pool.tensor_tensor(rstd2[:, :], ve2[:, :], R["mhalf"], ALU.pow).then_inc(s_rstd2, 1)

            norm(0)
            run_steps(pool, step)

        @block.scalar
        def _(act):
            starts(act, act_sems)

            def x_high(s, p):
                now(act, s_xT, s)
                act.activation(xh[p][:, PAD:], PT[:, :], ACT.Copy).then_inc(s_xh, 1)

            def dt_exp(s):
                now(act, s_neg, s)
                act.activation(u[:, :], neg[:, :], ACT.Exp).then_inc(s_u, 1)

            def decays(s, p):
                now(act, s_cum, s)
                act.activation(ecd[p][:, :], PS[:, TH:3 * TH], ACT.Exp).then_inc(s_ecd, 1)

            def carries(s, p):
                now(act, s_dtp, s)
                act.activation(carry[p][:, :, 1:], PS[:, 257:256 + CHUNKS].rearrange("p (o c) -> p o c", o=1)
                               .to_broadcast([P, STATE, CHUNKS - 1]), ACT.Exp).then_inc(s_carry, 1)

            x_high(0, 0)
            dt_exp(0)
            decays(0, 0)
            carries(0, 0)

            def step(s, p, first, last):
                now(act, s_z, s)
                before(act, s_yzn, s)
                act.activation(yz[:, :, HALF:], tiles(PZ), ACT.Copy).then_inc(s_zc, 1)
                now(act, s_x, s)
                before(act, s_y, s)
                act.activation(xc[:, :], PX[:, :], ACT.Silu, bias=R["cb_x"][:, 0:1]).then_inc(s_xc, 1)
                now(act, s_bc, s)
                before(act, s_Cm, s)
                NC = BLOCKS * STATE
                act.activation(Cc[:, :], PBC[0:NC, :], ACT.Silu, bias=R["cb_bc"][0:NC, 0:1])
                act.activation(Bc[:, :], PBC[NC:NC + STATE, :], ACT.Silu, bias=R["cb_bc"][NC:NC + STATE, 0:1])\
                    .then_inc(s_bcs, 1)
                for g, (seg, m, done) in enumerate(((s_seg0, s_M0, s_E0), (s_seg1, s_M1, s_E1))):
                    now(act, seg, s)
                    before(act, m, s)
                    act.activation(Eg[g][:, :], PSEG[g][:, :], ACT.Exp).then_inc(done, 1)
                if not last:
                    x_high(s + 1, 1 - p)
                    dt_exp(s + 1)
                now(act, s_stt, s)
                before(act, s_yoff, s)
                act.activation(STs[:, :], PSTT[0:NC, :], ACT.Copy).then_inc(s_STs, 1)
                if not last:
                    decays(s + 1, 1 - p)
                    carries(s + 1, 1 - p)
                now(act, s_yt, s)
                before(act, s_o, s)
                act.activation(yT[0][:, :], PYT[0][:, :], ACT.Copy)
                act.activation(yT[1][:, :], PYT[1][:, :], ACT.Copy).then_inc(s_yT, 1)
                now(act, s_o, s)
                before(act, s_back, s)
                act.activation(oT[:, :], PO[:, :], ACT.Identity, bias=R["out_bias"][:, 0:1]).then_inc(s_oT, 1)
            run_steps(act, step)

        @block.vector
        def _(dve):
            starts(dve, dve_sems)
            dve.memset(XB[:, :, :, :, :], 0.0)
            dve.memset(into_chunk[:, 0:1, :], 0.0)
            for p in range(2):
                dve.memset(carry[p][:, :, 0:1], 0.0)
                dve.memset(xh[p][:, 0:PAD].bitcast(F32), 0.0)
                dve.memset(xl[p][:, 0:PAD].bitcast(F32), 0.0)

            def moments(own, src, stats, mv, ve, ready):
                for t in range(SEQ_TILES):
                    i = dve.bn_stats(stats[:, t, :], src(t))
                own.link(i)
                settle(dve, R["settled"])
                for t in range(SEQ_TILES):
                    i = dve.bn_aggr(mv[:, t, :], stats[:, t, :])
                own.link(i)
                dve.tensor_scalar(ve[:, :], mv[:, :, 1], EPS, None, ALU.add).then_inc(ready, 1)

            def norm(s, p):
                own = Own(dve, s_own, s * OWN, OWN_OPS[0])
                moments(own, lambda t: X[:, bass.ds(s * SEQ_TILES + t, 1), :], stats, mv, ve, s_ve)
                now(dve, s_rstd, s)
                for t in range(SEQ_TILES):
                    i = dve.tensor_scalar(xn[:, t:t + 1, :], X[:, bass.ds(s * SEQ_TILES + t, 1), :],
                                          mv[:, t, 0:1], rstd[:, t:t + 1], ALU.subtract, ALU.mult)
                i.then_inc(s_xn, 1)
                own.close()

            def x_low(s, p):
                now(dve, s_xh, s)
                dve.tensor_tensor(xl[p][:, PAD:], PT[:, :], xh[p][:, PAD:], ALU.subtract).then_inc(s_xl, 1)

            def time_steps(s, p):
                own = Own(dve, s_own, s * OWN + OWN_OPS[0], OWN_OPS[1])
                link = own.link
                th = lambda a: a[:, 0:TH].rearrange("p (t h) -> p t h", h=HEADS)
                row = lambda a: a[:, :].rearrange("p (o h) -> p o h", o=1).to_broadcast([P, SEQ_TILES, HEADS])
                now(dve, s_dt, s)
                link(dve.tensor_tensor(th(raw), th(PS), row(R["dt_bias"]), ALU.add))
                dve.scalar_tensor_tensor(neg[:, :], raw[:, :], -1.0, raw[:, :], ALU.mult, ALU.min).then_inc(s_neg, 1)
                dve.tensor_scalar(pos[:, :], raw[:, :], 0.0, None, ALU.max)
                now(dve, s_u, s)
                link(dve.tensor_scalar(v[:, :], u[:, :], 2.0, None, ALU.add))
                link(dve.reciprocal(w[:, :], v[:, :]))
                link(dve.tensor_tensor(v[:, :], u[:, :], w[:, :], ALU.mult))
                link(dve.tensor_tensor(w[:, :], v[:, :], v[:, :], ALU.mult))
                link(dve.tensor_scalar(q[:, :], w[:, :], ARTANH[-1], None, ALU.mult))
                for c in ARTANH[-2:0:-1]:
                    link(dve.scalar_tensor_tensor(q[:, :], q[:, :], c, w[:, :], ALU.add, ALU.mult))
                link(dve.scalar_tensor_tensor(q[:, :], q[:, :], 1.0, v[:, :], ALU.add, ALU.mult))
                link(dve.scalar_tensor_tensor(dt[p][:, :], q[:, :], 2.0, pos[:, :], ALU.mult, ALU.add))
                dve.tensor_tensor(th(at), th(dt[p]), row(R["decay_rate"]), ALU.mult).then_inc(s_at, 1)
                own.close()

            def block_decays(s, p):
                own = Own(dve, s_own, s * OWN + sum(OWN_OPS[:2]), OWN_OPS[2])
                now(dve, s_ecd, s)
                own.link(dve.tensor_tensor(amask[:, :].rearrange("p (c b) -> p c b", b=BLOCKS),
                                           PS[:, 128:256].rearrange("p (c b) -> p c b", b=BLOCKS),
                                           R["own_block"].rearrange("p (o b) -> p o b", o=1)
                                           .to_broadcast([P, CHUNKS * HGROUPS, BLOCKS]), ALU.mult))
                dve.tensor_reduce(aB[p][:, :], amask[:, :].rearrange("p (c b) -> p c b", b=BLOCKS), AX.X, ALU.add)\
                    .then_inc(s_aB, 1)
                dve.tensor_tensor(totX[:, :].rearrange("p (t c) -> p t c", c=BLOCKS),
                                  PS[0:TH, 96:96 + BLOCKS].rearrange("p (o c) -> p o c", o=1)
                                  .to_broadcast([TH, SEQ_TILES, BLOCKS]),
                                  R["own_tile"][0:TH, :].rearrange("p (t c) -> p t c", c=BLOCKS), ALU.mult)\
                    .then_inc(s_totX, 1)
                own.close()

            norm(0, 0)
            x_low(0, 0)
            time_steps(0, 0)
            block_decays(0, 0)

            def heads(a, at):
                return a[:, at:at + TH].rearrange("p (h o) -> p h o", o=1).to_broadcast([P, TH, HDIM])

            def per_head(a):
                return a[:, :].rearrange("p (h o) -> p h o", o=HDIM)

            def step(s, p, first, last):
                now(dve, s_xt, s)
                dve.tensor_tensor(per_head(xdt), per_head(PXT), heads(dt[p], 0), ALU.mult).then_inc(s_xdt, 1)
                now(dve, s_xdt, s)
                before(dve, s_st, s)
                dve.tensor_tensor(per_head(xdec), per_head(xdt), heads(ecd[p], TH), ALU.mult).then_inc(s_xdec, 1)
                before(dve, s_y, s)
                for c in range(BLOCKS):
                    for b in range(BLOCKS):
                        src = xdt[c * CHUNK:(c + 1) * CHUNK, :].rearrange("p (t g b k) -> p t g b k", t=SEQ_TILES,
                                                                          g=HGROUPS, b=BLOCKS)[:, :, :, b, :]
                        i = dve.tensor_copy(XB[b * CHUNK:(b + 1) * CHUNK, :, c, :, b * HDIM:(b + 1) * HDIM], src)
                i.then_inc(s_XB, 1)
                now(dve, s_bt, s)
                dve.tensor_tensor(Bm[:, :, :, :],
                                  PBT[:, 0:SEQ_TILES * STATE].rearrange("p (t o n) -> p t o n", t=SEQ_TILES, o=1)
                                  .to_broadcast([P, SEQ_TILES, BLOCKS, STATE]),
                                  R["own_block"].rearrange("p (a c o) -> p a c o", a=1, o=1)
                                  .to_broadcast([P, SEQ_TILES, BLOCKS, STATE]), ALU.mult).then_inc(s_Bm, 1)
                now(dve, s_g, s)
                before(dve, s_gr, s)
                dve.tensor_tensor(Gm[:, :, :], tiles(PG, P),
                                  R["causal_block"].rearrange("p (o l) -> p o l", o=1).to_broadcast([P, SEQ_TILES, P]),
                                  ALU.mult).then_inc(s_Gm, 1)
                now(dve, s_gr, s)
                for g, (e, done) in enumerate(((s_E0, s_M0), (s_E1, s_M1))):
                    now(dve, e, s)
                    dve.tensor_tensor(Mg[g][:, :, :, :].rearrange("p c t l -> p (c t l)"), Eg[g][:, :], PGR[:, :],
                                      ALU.mult).then_inc(done, 1)
                if not last:
                    norm(s + 1, 1 - p)
                    x_low(s + 1, 1 - p)
                    time_steps(s + 1, 1 - p)
                now(dve, s_st, s)
                now(dve, s_carry, s)
                before(dve, s_Sin, s)
                dve.tensor_tensor_scan(after_chunk[:, :, :].rearrange("p n c -> p (n c)"),
                                       carry[p][:, :, :].rearrange("p n c -> p (n c)"), PST[:, 0:STATE * CHUNKS],
                                       0.0, ALU.mult, ALU.add).then_inc(s_scan, 1)
                now(dve, s_yoff, s)
                dve.tensor_tensor(per_head(yo), per_head(PYO), heads(ecd[p], 0), ALU.mult).then_inc(s_yo, 1)
                now(dve, s_yo, s)
                now(dve, s_y, s)
                dve.tensor_tensor(yz[:, :, 0:HALF], tiles(yo), tiles(PY), ALU.add).then_inc(s_yzy, 1)
                if not last:
                    block_decays(s + 1, 1 - p)
                own = Own(dve, s_own2, s * 2, 2)
                now(dve, s_yzy, s)
                now(dve, s_zc, s)
                moments(own, lambda t: yz[:, t, :], stats2, mv2, ve2, s_ve2)
                now(dve, s_rstd2, s)
                for t in range(SEQ_TILES):
                    i = dve.tensor_scalar(yzn[:, t, :], yz[:, t, :], mv2[:, t, 0:1], rstd2[:, t:t + 1],
                                          ALU.subtract, ALU.mult)
                i.then_inc(s_yzn, 1)
                own.close()
                now(dve, s_back, s)
                seq = X[:, bass.ds(s * SEQ_TILES, SEQ_TILES), :]
                dve.tensor_tensor(seq, seq, tiles(PT), ALU.add).then_inc(s_xdone, 1)
            run_steps(dve, step)

        @block.tensor
        def _(pe):
            starts(pe, pe_sems)

            def four(out, src, ident, done):
                for t in range(SEQ_TILES):
                    i = pe.transpose(out(t), src(t), ident)
                i.then_inc(done, 1)

            def tile(t):
                return slice(t * P, (t + 1) * P)

            def x_turn(s, p):
                now(pe, s_xn, s)
                four(lambda t: PT[:, tile(t)], lambda t: xn[:, t, :], R["ident"], s_xT)

            def times(s, p):
                now(pe, s_xl, s)
                before(pe, s_carry, s)
                cols = slice(P, P + HEADS)
                for t in range(SEQ_TILES):
                    out, tt = PS[:, t * HEADS:(t + 1) * HEADS], slice(PAD + t * P, PAD + (t + 1) * P)
                    pe.matmul(out, xh[p][:, tt], R["wz_hi"][:, cols], start=(t == 0), stop=False, skip_group_check=True)
                    pe.matmul(out, xh[p][:, tt], R["wz_lo"][:, cols], start=False, stop=False, skip_group_check=True)
                    i = pe.matmul(out, xl[p][:, tt], R["wz_hi"][:, cols], start=False, stop=True, skip_group_check=True)
                i.then_inc(s_dt, 1)

            def sums(s, p):
                now(pe, s_at, s)
                pe.matmul(PS[:, TH:2 * TH], R["upto"], at[:, :], start=True, stop=True)
                pe.matmul(PS[:, 2 * TH:3 * TH], R["after"], at[:, :], start=True, stop=True)
                for c in range(BLOCKS):
                    pe.matmul(PS[:, 128 + c * TH:128 + (c + 1) * TH], R["spread_one"][:, tile(c)], at[:, :],
                              start=True, stop=True)
                pe.matmul(PS[0:TH, 96:96 + BLOCKS], at[:, :], R["own_block"], start=True, stop=True).then_inc(s_cum, 1)

            def totals(s, p):
                now(pe, s_totX, s)
                pe.matmul(PS[:, 256:256 + CHUNKS], R["own_head"][0:TH, :], totX[:, :], start=True, stop=True)\
                    .then_inc(s_dtp, 1)

            x_turn(0, 0)
            times(0, 0)
            sums(0, 0)
            totals(0, 0)

            def conv(out, w, p, done):
                for k in range(TAPS):
                    i = split_mm(pe, out, R[f"{w}_hi"][:, tile(k)], R[f"{w}_lo"][:, tile(k)], xh[p][:, k:k + L],
                                 xl[p][:, k:k + L], k == 0, k == TAPS - 1)
                i.then_inc(done, 1)

            def step(s, p, first, last):
                before(pe, s_yT, s)
                for t in range(SEQ_TILES):
                    tt = slice(PAD + t * P, PAD + (t + 1) * P)
                    out = PZ[:, tile(t)]
                    pe.matmul(out, xh[p][:, tt], R["wz_hi"][:, 0:P], start=(t == 0), stop=False, skip_group_check=True)
                    pe.matmul(out, xh[p][:, tt], R["wz_lo"][:, 0:P], start=False, stop=False, skip_group_check=True)
                    i = pe.matmul(out, xl[p][:, tt], R["wz_hi"][:, 0:P], start=False, stop=True, skip_group_check=True)
                i.then_inc(s_z, 1)
                conv(PX[:, :], "wx", p, s_x)
                before(pe, s_M1, s)
                conv(PBC[:, :], "wbc", p, s_bc)
                now(pe, s_xc, s)
                before(pe, s_yzy, s)
                four(lambda t: PXT[:, tile(t)], lambda t: xc[:, tile(t)], R["ident"], s_xt)
                now(pe, s_bcs, s)
                now(pe, s_zc, s)
                settle(pe, R["settled"])
                four(lambda t: PBT[:, t * STATE:(t + 1) * STATE], lambda t: Bc[:, tile(t)],
                     R["ident"][0:STATE, 0:STATE], s_bt)
                for t in range(SEQ_TILES):
                    i = pe.matmul(PG[:, tile(t)], Bc[:, tile(t)], Cc[0:STATE, tile(t)], start=True, stop=True)
                i.then_inc(s_g, 1)
                now(pe, s_R0, s)
                before(pe, s_yo, s)
                pe.matmul(PSEG[0][:, :], R["after"], Rg[0][:, :, :].rearrange("p c l -> p (c l)"), start=True, stop=True)\
                    .then_inc(s_seg0, 1)
                now(pe, s_R1, s)
                before(pe, s_oT, s)
                pe.matmul(PSEG[1][:, :], R["after"], Rg[1][:, :, :].rearrange("p c l -> p (c l)"), start=True, stop=True)\
                    .then_inc(s_seg1, 1)
                now(pe, s_Gm, s)
                for c in range(BLOCKS):
                    i = pe.matmul(PGR[:, tile(c)], R["spread"], Gm[:, :, c * CHUNK:(c + 1) * CHUNK], start=True, stop=True)
                i.then_inc(s_gr, 1)
                if not last:
                    x_turn(s + 1, 1 - p)
                now(pe, s_XB, s)
                for t in range(SEQ_TILES):
                    pe.matmul(PY[:, tile(t)], xc[:, tile(t)], R["skip"][:, :], start=(t == 0), stop=False,
                              skip_group_check=True)
                for g, m in ((0, s_M0), (1, s_M1)):
                    now(pe, m, s)
                    for t in range(SEQ_TILES):
                        for c in range(BLOCKS):
                            at_col = t * P + g * BLOCKS * HDIM
                            i = pe.matmul(PY[c * CHUNK:(c + 1) * CHUNK, at_col:at_col + BLOCKS * HDIM],
                                          Mg[g][:, c, t, :], XB[:, t, c, g, :], start=False, stop=True,
                                          skip_group_check=True)
                i.then_inc(s_y, 1)
                now(pe, s_xdec, s)
                now(pe, s_Bm, s)
                for t in range(SEQ_TILES):
                    out = PST[:, 0:STATE * CHUNKS].rearrange("p (n c) -> p c n", c=CHUNKS)[:, t * BLOCKS:(t + 1) * BLOCKS, :]
                    i = pe.matmul(out, xdec[:, tile(t)], Bm[:, t, :, :], start=True, stop=True)
                i.then_inc(s_st, 1)
                if not last:
                    times(s + 1, 1 - p)
                now(pe, s_Sin, s)
                NC = BLOCKS * STATE
                settle(pe, R["settled"])
                four(lambda t: PSTT[0:NC, tile(t)],
                     lambda t: into_chunk[:, t * BLOCKS:(t + 1) * BLOCKS, :].rearrange("p c n -> p (c n)"),
                     R["ident"], s_stt)
                now(pe, s_STs, s)
                now(pe, s_Cm, s)
                for t in range(SEQ_TILES):
                    i = pe.matmul(PYO[:, tile(t)], Cm[:, tile(t)], STs[:, tile(t)], start=True, stop=True)
                i.then_inc(s_yoff, 1)
                if not last:
                    sums(s + 1, 1 - p)
                    totals(s + 1, 1 - p)
                now(pe, s_yzn, s)
                for j in range(2):
                    for t in range(SEQ_TILES):
                        i = pe.transpose(PYT[j][:, tile(t)], yzn[:, t, j * HALF:(j + 1) * HALF], R["ident"])
                i.then_inc(s_yt, 1)
                now(pe, s_yT, s)
                pe.matmul(PO[:, :], R["wo"][:, 0:D], yT[0][:, :], start=True, stop=False)
                pe.matmul(PO[:, :], R["wo"][:, D:2 * D], yT[1][:, :], start=False, stop=True).then_inc(s_o, 1)
                now(pe, s_oT, s)
                four(lambda t: PT[:, tile(t)], lambda t: oT[:, tile(t)], R["ident"], s_back)
            run_steps(pe, step)


def program(nc, ins, out):
    with ExitStack() as ctx:
        R = {}
        out_dram = out.rearrange("b (t p) d -> b p t d", p=P)
        R["out_dram"] = [out_dram[s] for s in range(B)]
        setup(nc, R, ins, ctx)
        mamba_setup(nc, R, ins, ctx)
        ffn_phase(nc, "ffn1", R, True, False)
        mamba_phase(nc, R)
        ffn_phase(nc, "ffn2", R, False, True)


def kernel(**inputs):
    import numpy as np
    import concourse.bacc as bacc
    from concourse.bass_utils import run_bass_kernel_spmd

    nc = bacc.Bacc("TRN2", target_bir_lowering=False, num_devices=1)
    arrays = {name: np.ascontiguousarray(a) for name, a in inputs.items()}
    arrays["constants"] = constants()
    ins = {name: nc.dram_tensor(name, a.shape, mybir.dt.from_np(a.dtype), kind="ExternalInput").ap()
           for name, a in arrays.items()}
    out = nc.dram_tensor("out", (B, L, D), F32, kind="ExternalOutput").ap()
    program(nc, ins, out)
    return run_bass_kernel_spmd(nc, [arrays], core_ids=[0]).results[0]["out"]
```

```python
import concourse.bass as bass
from concourse import mybir
from contextlib import ExitStack

F32 = mybir.dt.float32
F32R = mybir.dt.float32r
BF16 = mybir.dt.bfloat16
ALU = mybir.AluOpType
ACT = mybir.ActivationFunctionType
AX = mybir.AxisListType

P = 128
B, L, D = 8, 512, 128
SEQ_TILES = L // P
TILES = B * SEQ_TILES
E, H, SHARED, TOP = 8, 64, 2, 2
PAIRS = (E + SHARED) // 2
EPS = 1e-5

HEADS, HDIM, STATE, TAPS = 8, 16, 16, 4
CHUNK = 32
BLOCKS = P // CHUNK
CHUNKS = L // CHUNK
HALF = HEADS * HDIM
HGROUPS = HEADS // BLOCKS
ARTANH = [1.0 / (2 * k + 1) for k in range(8)]


class Own:

    def __init__(self, engine, sem, base, most):
        self.engine, self.sem, self.base, self.most, self.n = engine, sem, base, most, 0

    def mark(self, instruction):
        self.n += 1
        instruction.then_inc(self.sem, 1)

    def ready(self):
        if self.n:
            self.engine.wait_ge(self.sem, self.base + self.n)

    def link(self, instruction):
        self.mark(instruction)
        self.ready()

    def close(self):
        assert self.n == self.most, self.n


def settle(engine, sem):
    engine.sem_inc(sem, 1)


def split_mm(pe, out, w_hi, w_lo, x_hi, x_lo, start, stop):
    pe.matmul(out, w_hi, x_hi, start=start, stop=False)
    pe.matmul(out, w_hi, x_lo, start=False, stop=False)
    return pe.matmul(out, w_lo, x_hi, start=False, stop=stop)


def run_steps(engine, step):
    step(0, 0, True, False)
    with engine.Fori(0, B // 2 - 1) as k:
        step(k * 2 + 1, 1, False, False)
        step(k * 2 + 2, 0, False, False)
    step(B - 1, 1, False, True)


def ffn_phase(nc, tag, R, load_x, store_x):
    X, ident = R["X"], R["ident"]
    with ExitStack() as ctx:
        def sb(name, shape, dt=F32):
            return ctx.enter_context(nc.sbuf_tensor(f"{tag}_{name}", shape, dt))

        def sem(name):
            return ctx.enter_context(nc.semaphore(f"{tag}_{name}"))

        stats = sb("stats", [P, SEQ_TILES, 6])
        mv = [sb(f"mv{p}", [P, SEQ_TILES, 2]) for p in range(2)]
        ve = [sb(f"ve{p}", [P, SEQ_TILES]) for p in range(2)]
        rstd = [sb(f"rstd{p}", [P, SEQ_TILES]) for p in range(2)]
        xn = [sb(f"xn{p}", [P, SEQ_TILES, D]) for p in range(2)]
        xh = [sb(f"xh{p}", [P, L], F32R) for p in range(2)]
        xl = [sb(f"xl{p}", [P, L], F32R) for p in range(2)]
        biased, eq = sb("biased", [P, SEQ_TILES, E]), sb("eq", [P, SEQ_TILES, E])
        key = sb("key", [P, SEQ_TILES, E])
        lg = [sb(f"lg{k}", [P, SEQ_TILES, E]) for k in range(TOP)]
        one = sb("one", [P, SEQ_TILES, TOP, E])
        top, km = sb("top", [P, TOP, SEQ_TILES]), sb("km", [P, SEQ_TILES])
        dm, ed, den = sb("dm", [P, SEQ_TILES]), sb("ed", [P, SEQ_TILES]), sb("den", [P, SEQ_TILES])
        gk = sb("gk", [P, SEQ_TILES, TOP])
        gparts = sb("gparts", [P, SEQ_TILES, TOP, 2], F32R)
        GROWS = TOP * 2 * E
        spots = [sb(f"spots{p}", [P, SEQ_TILES, GROWS]) for p in range(2)]
        gT = [sb(f"gT{p}", [GROWS, L], F32R) for p in range(2)]
        sil = [sb(f"sil{b}", [P, L]) for b in range(2)]
        pr = [sb(f"pr{b}", [P, L]) for b in range(2)]
        h = [sb(f"h{c}", [P, L]) for c in range(PAIRS)]
        hh = [sb(f"hh{c}", [P, L], F32R) for c in range(PAIRS)]
        hl = [sb(f"hl{c}", [P, L], F32R) for c in range(PAIRS)]
        oT = sb("oT", [P, L])

        PT, PS, PB, PD = R["bank"][0:4]
        PG = [R["bank"][4], R["bank"][6]]
        PU = [R["bank"][5], R["bank"][7]]

        ve_ready, rstd_ready, xn_ready = sem("ve_ready"), sem("rstd_ready"), sem("xn_ready")
        xT_ready, xh_ready, xl_ready = sem("xT_ready"), sem("xh_ready"), sem("xl_ready")
        logits_ready, dm_ready, ed_ready = sem("logits_ready"), sem("dm_ready"), sem("ed_ready")
        spots_ready, gTp_ready, gT_ready = sem("spots_ready"), sem("gTp_ready"), sem("gT_ready")
        up_ready, sil_ready, prod_ready = sem("up_ready"), sem("sil_ready"), sem("prod_ready")
        bc_ready, h_ready, hh_ready, hl_ready = sem("bc_ready"), sem("h_ready"), sem("hh_ready"), sem("hl_ready")
        down_done, oT_ready, back_ready, x_done = sem("down_done"), sem("oT_ready"), sem("back_ready"), sem("x_done")
        norm_own, gate_own, stored = sem("norm_own"), sem("gate_own"), sem("stored")
        NORM_OPS, GATE_OPS, ROUTED = 2, 18, PAIRS - 1
        CREDIT = {prod_ready: 2, hl_ready: PAIRS, down_done: PAIRS, oT_ready: 1, back_ready: 1, x_done: 1}

        def chunk(s, c):
            return s * PAIRS + c

        def buf(p, c):
            return (p * PAIRS + c) % 2

        def hidden_written(engine, s, c):
            if c == 0:
                engine.wait_ge(prod_ready, chunk(s, 0) + 1 + CREDIT[prod_ready])
            else:
                engine.wait_ge(h_ready, s * ROUTED + c)

        block = ctx.enter_context(nc.Block())

        @block.sync
        def _(sp):
            if load_x:
                for s in range(2, B):
                    sp.dma_start(X[:, s * SEQ_TILES:(s + 1) * SEQ_TILES, :], R["x_dram"][s])\
                        .then_inc(R["x_loaded"][s], 16)
            if store_x:
                for s in range(B):
                    sp.wait_ge(x_done, s + 1 + CREDIT[x_done])
                    sp.dma_start(R["out_dram"][s], X[:, s * SEQ_TILES:(s + 1) * SEQ_TILES, :])\
                        .then_inc(stored, 16)
                sp.wait_ge(stored, 16 * B)

        @block.gpsimd
        def _(pool):
            def norm_power(s, p):
                pool.wait_ge(ve_ready, s + 1)
                pool.tensor_tensor(rstd[p][:, :], ve[p][:, :], R["mhalf"], ALU.pow).then_inc(rstd_ready, 1)

            def softmax_power(s):
                pool.wait_ge(dm_ready, s + 1)
                pool.tensor_tensor(ed[:, :], R["euler"], dm[:, :], ALU.pow).then_inc(ed_ready, 1)

            def low_part(s, c):
                pool.wait_ge(hh_ready, chunk(s, c) + 1)
                pool.tensor_tensor(hl[c][:, :], h[c][:, :], hh[c][:, :], ALU.subtract).then_inc(hl_ready, 1)

            pool.sem_inc(hl_ready, CREDIT[hl_ready])
            norm_power(0, 0)
            norm_power(1, 1)
            softmax_power(0)

            def step(s, p, first, last):
                if not first:
                    low_part(s - 1, 4)
                low_part(s, 0)
                if not last:
                    norm_power(s + 2, p)
                low_part(s, 1)
                low_part(s, 2)
                if not last:
                    softmax_power(s + 1)
                low_part(s, 3)
            run_steps(pool, step)
            low_part(B - 1, 4)

        @block.scalar
        def _(act):
            def x_high(s, p):
                act.wait_ge(xT_ready, s + 1)
                act.activation(xh[p][:, :], PT[:, :], ACT.Copy).then_inc(xh_ready, 1)

            def gates_out(s, p):
                act.wait_ge(gTp_ready, s + 1)
                act.activation(gT[p][:, :], PB[0:GROWS, :], ACT.Copy).then_inc(gT_ready, 1)

            def silu(s, p, c):
                n, b = chunk(s, c), buf(p, c)
                act.wait_ge(up_ready, n + 1)
                act.wait_ge(prod_ready, n - 1 + CREDIT[prod_ready])
                act.activation(sil[b][:, :], PG[b][:, :], ACT.Silu).then_inc(sil_ready, 1)

            def high_part(s, c):
                hidden_written(act, s, c)
                act.wait_ge(down_done, chunk(s, c) + 1 - PAIRS + CREDIT[down_done])
                act.activation(hh[c][:, :], h[c][:, :], ACT.Copy).then_inc(hh_ready, 1)

            def out_copy(s):
                act.wait_ge(down_done, chunk(s, PAIRS) + CREDIT[down_done])
                act.wait_ge(back_ready, s + CREDIT[back_ready])
                act.activation(oT[:, :], PD[:, :], ACT.Copy).then_inc(oT_ready, 1)

            act.sem_inc(oT_ready, CREDIT[oT_ready])
            x_high(0, 0)

            def step(s, p, first, last):
                silu(s, p, 0)
                gates_out(s, p)
                if not last:
                    x_high(s + 1, 1 - p)
                if not first:
                    high_part(s - 1, 4)
                silu(s, p, 1)
                high_part(s, 0)
                silu(s, p, 2)
                high_part(s, 1)
                if not first:
                    out_copy(s - 1)
                silu(s, p, 3)
                high_part(s, 2)
                silu(s, p, 4)
                high_part(s, 3)
            run_steps(act, step)
            high_part(B - 1, 4)
            out_copy(B - 1)

        @block.vector
        def _(dve):
            def over_experts(a):
                return a.rearrange("p (t o) -> p t o", o=1).to_broadcast([P, SEQ_TILES, E])

            def over_tiles(a):
                return a.rearrange("p (o e) -> p o e", o=1).to_broadcast([P, SEQ_TILES, E])

            class Norm:

                def __init__(self, s, p):
                    self.s, self.p = s, p
                    self.x = lambda t: X[:, bass.ds(s * SEQ_TILES + t, 1), :]
                    self.own = Own(dve, norm_own, s * NORM_OPS, NORM_OPS)

                def stats(self):
                    for t in range(SEQ_TILES):
                        i = dve.bn_stats(stats[:, t, :], self.x(t))
                    self.own.mark(i)

                def moments(self):
                    self.own.ready()
                    settle(dve, R["settled"])
                    for t in range(SEQ_TILES):
                        i = dve.bn_aggr(mv[self.p][:, t, :], stats[:, t, :])
                    self.own.mark(i)

                def variance(self):
                    self.own.ready()
                    dve.tensor_scalar(ve[self.p][:, :], mv[self.p][:, :, 1], EPS, None, ALU.add).then_inc(ve_ready, 1)
                    self.own.close()

                def apply(self, t):
                    if t == 0:
                        dve.wait_ge(rstd_ready, self.s + 1)
                    i = dve.tensor_scalar(xn[self.p][:, t:t + 1, :], self.x(t), mv[self.p][:, t, 0:1],
                                          rstd[self.p][:, t:t + 1], ALU.subtract, ALU.mult)
                    if t == SEQ_TILES - 1:
                        i.then_inc(xn_ready, 1)

            class Gates:

                def __init__(self, s, p):
                    self.s, self.p = s, p
                    self.own = Own(dve, gate_own, s * GATE_OPS, GATE_OPS)

                def chain(self, instruction_of):
                    self.own.ready()
                    self.own.mark(instruction_of())

                def logits(self):
                    dve.wait_ge(logits_ready, self.s + 1)
                    v = PS[:, 0:SEQ_TILES * 2 * E].rearrange("p (t k e) -> p t k e", k=2, e=E)
                    self.chain(lambda: dve.tensor_tensor(biased[:, :, :], v[:, :, 0, :], over_tiles(R["router_b"][:, :]), ALU.add))
                    self.chain(lambda: dve.tensor_tensor(lg[0][:, :, :], v[:, :, 1, :], biased[:, :, :], ALU.add))

                def largest(self, k):
                    self.chain(lambda: dve.tensor_reduce(top[:, k, :], lg[k][:, :, :], AX.X, ALU.max))

                def equal(self, k):
                    self.chain(lambda: dve.tensor_tensor(eq[:, :, :], lg[k][:, :, :], over_experts(top[:, k, :]), ALU.is_equal))

                def order(self):
                    self.chain(lambda: dve.tensor_tensor(key[:, :, :], eq[:, :, :], over_tiles(R["order"]), ALU.mult))

                def first_of(self):
                    self.chain(lambda: dve.tensor_reduce(km[:, :], key[:, :, :], AX.X, ALU.max))

                def mark(self, k):
                    self.chain(lambda: dve.tensor_tensor(one[:, :, k, :], key[:, :, :], over_experts(km[:, :]), ALU.is_equal))

                def remove(self):
                    self.chain(lambda: dve.scalar_tensor_tensor(lg[1][:, :, :], one[:, :, 0, :], -3.0e38, lg[0][:, :, :],
                                                                ALU.mult, ALU.add))

                def distance(self):
                    self.own.ready()
                    dve.tensor_tensor(dm[:, :], top[:, 1, :], top[:, 0, :], ALU.subtract).then_inc(dm_ready, 1)

                def denominator(self):
                    dve.wait_ge(ed_ready, self.s + 1)
                    self.chain(lambda: dve.tensor_scalar(den[:, :], ed[:, :], 1.0, None, ALU.add))

                def weights(self):
                    self.chain(lambda: dve.reciprocal(gk[:, :, 0], den[:, :]))
                    self.chain(lambda: dve.tensor_tensor(gk[:, :, 1], ed[:, :], gk[:, :, 0], ALU.mult))

                def parts(self):
                    self.chain(lambda: dve.tensor_copy(gparts[:, :, :, 0], gk[:, :, :]))
                    self.chain(lambda: dve.tensor_tensor(gparts[:, :, :, 1], gk[:, :, :], gparts[:, :, :, 0], ALU.subtract))

                def place(self):
                    self.own.ready()
                    N = SEQ_TILES * TOP
                    dve.tensor_tensor(spots[self.p][:, :, :].rearrange("p t (k w e) -> p (t k) w e", w=2, e=E),
                                      one[:, :, :, :].rearrange("p t k (o e) -> p (t k) o e", o=1).to_broadcast([P, N, 2, E]),
                                      gparts[:, :, :, :].rearrange("p t k (w o) -> p (t k) w o", o=1).to_broadcast([P, N, 2, E]),
                                      ALU.mult).then_inc(spots_ready, 1)
                    self.own.close()

            def x_low(s, p):
                dve.wait_ge(xh_ready, s + 1)
                dve.tensor_tensor(xl[p][:, :], PT[:, :], xh[p][:, :], ALU.subtract).then_inc(xl_ready, 1)

            def product(s, p, c):
                n, b = chunk(s, c), buf(p, c)
                dve.wait_ge(sil_ready, n + 1)
                if c == 0:
                    dve.wait_ge(hl_ready, n + 1 - PAIRS + CREDIT[hl_ready])
                out = h[0] if c == 0 else pr[b]
                dve.tensor_tensor(out[:, :], sil[b][:, :], PU[b][:, :], ALU.mult).then_inc(prod_ready, 1)

            def gated(s, p, c):
                n, b = chunk(s, c), buf(p, c)
                dve.wait_ge(prod_ready, n + 1 + CREDIT[prod_ready])
                dve.wait_ge(bc_ready, s * ROUTED + c)
                dve.wait_ge(hl_ready, n + 1 - PAIRS + CREDIT[hl_ready])
                dve.tensor_tensor(h[c][:, :], pr[b][:, :], PB[:, :], ALU.mult).then_inc(h_ready, 1)

            def residual(s):
                dve.wait_ge(back_ready, s + 1 + CREDIT[back_ready])
                seq = X[:, bass.ds(s * SEQ_TILES, SEQ_TILES), :]
                dve.tensor_tensor(seq, seq, PT[:, :].rearrange("p (t d) -> p t d", d=D), ALU.add).then_inc(x_done, 1)

            for one_sem in (prod_ready, x_done):
                dve.sem_inc(one_sem, CREDIT[one_sem])
            for s in range(2):
                if load_x:
                    dve.wait_ge(R["x_loaded"][s], 16)
                n = Norm(s, s)
                n.stats()
                n.moments()
                n.variance()
                for t in range(SEQ_TILES):
                    n.apply(t)
            x_low(0, 0)
            g = Gates(0, 0)
            g.logits()
            for k in range(TOP):
                if k:
                    g.remove()
                g.largest(k)
                g.equal(k)
                g.order()
                g.first_of()
                g.mark(k)
            g.distance()
            g.denominator()
            g.weights()
            g.parts()
            g.place()
            if load_x:
                for s in range(2, B):
                    dve.wait_ge(R["x_loaded"][s], 16)

            def step(s, p, first, last):
                if last:
                    product(s, p, 0)
                    for c in range(1, PAIRS):
                        product(s, p, c)
                        gated(s, p, c)
                        if c == 3:
                            residual(s - 1)
                    return
                g = Gates(s + 1, 1 - p)
                n = Norm(s + 2, p)
                product(s, p, 0)
                n.stats()
                x_low(s + 1, 1 - p)
                n.moments()
                product(s, p, 1)
                n.variance()
                gated(s, p, 1)
                g.logits()
                product(s, p, 2)
                g.largest(0)
                n.apply(0)
                g.equal(0)
                n.apply(1)
                g.order()
                gated(s, p, 2)
                g.first_of()
                n.apply(2)
                g.mark(0)
                n.apply(3)
                g.remove()
                product(s, p, 3)
                g.largest(1)
                if not first:
                    residual(s - 1)
                g.equal(1)
                gated(s, p, 3)
                g.distance()
                g.order()
                g.first_of()
                g.mark(1)
                product(s, p, 4)
                g.denominator()
                g.weights()
                gated(s, p, 4)
                g.parts()
                g.place()
            run_steps(dve, step)
            residual(B - 1)

        @block.tensor
        def _(pe):
            def four(out, src, done):
                for t in range(SEQ_TILES):
                    i = pe.transpose(out(slice(t * P, (t + 1) * P)), src(t), ident)
                i.then_inc(done, 1)

            def x_turn(s, p):
                pe.wait_ge(xn_ready, s + 1)
                pe.wait_ge(x_done, s - 2 + CREDIT[x_done])
                four(lambda cols: PT[:, cols], lambda t: xn[p][:, t, :], xT_ready)

            def router(s, p):
                pe.wait_ge(xl_ready, s + 1)
                for t in range(SEQ_TILES):
                    tile = slice(t * P, (t + 1) * P)
                    out = PS[:, t * 2 * E:(t + 1) * 2 * E]
                    pe.matmul(out, xh[p][:, tile], R["rw_parts"][:, :], start=(t == 0), stop=False, skip_group_check=True)
                    i = pe.matmul(out, xl[p][:, tile], R["rw_parts"][:, :], start=False, stop=True, skip_group_check=True)
                i.then_inc(logits_ready, 1)

            def gates_turn(s, p):
                pe.wait_ge(spots_ready, s + 1)
                four(lambda cols: PB[0:GROWS, cols], lambda t: spots[p][:, t, :], gTp_ready)

            def up(s, p, c):
                n, b = chunk(s, c), buf(p, c)
                pe.wait_ge(prod_ready, n - 1 + CREDIT[prod_ready])
                cols = slice(c * P, (c + 1) * P)
                split_mm(pe, PG[b][:, :], R["wg_hi"][:, cols], R["wg_lo"][:, cols], xh[p][:, :], xl[p][:, :], True, True)
                split_mm(pe, PU[b][:, :], R["wu_hi"][:, cols], R["wu_lo"][:, cols], xh[p][:, :], xl[p][:, :], True, True)\
                    .then_inc(up_ready, 1)

            def gates_spread(s, p, c):
                if c == 1:
                    pe.wait_ge(gT_ready, s + 1)
                else:
                    pe.wait_ge(h_ready, s * ROUTED + c - 1)
                pe.matmul(PB[:, :], R["spread_gates"][:, (c - 1) * P:c * P], gT[p][:, :], start=True, stop=True)\
                    .then_inc(bc_ready, 1)

            def down(s, c):
                pe.wait_ge(hl_ready, chunk(s, c) + 1 + CREDIT[hl_ready])
                if c == 0:
                    pe.wait_ge(oT_ready, s + CREDIT[oT_ready])
                cols = slice(c * P, (c + 1) * P)
                split_mm(pe, PD[:, :], R["wd_hi"][:, cols], R["wd_lo"][:, cols], hh[c][:, :], hl[c][:, :],
                         c == 0, c == PAIRS - 1).then_inc(down_done, 1)

            def back(s):
                pe.wait_ge(oT_ready, s + 1 + CREDIT[oT_ready])
                four(lambda cols: PT[:, cols], lambda t: oT[:, t * P:(t + 1) * P], back_ready)

            for one_sem in (down_done, back_ready):
                pe.sem_inc(one_sem, CREDIT[one_sem])
            pe.wait_ge(xn_ready, 1)
            four(lambda cols: PT[:, cols], lambda t: xn[0][:, t, :], xT_ready)
            router(0, 0)

            def step(s, p, first, last):
                up(s, p, 0)
                gates_turn(s, p)
                if first:
                    pe.wait_ge(xn_ready, 2)
                    four(lambda cols: PT[:, cols], lambda t: xn[1][:, t, :], xT_ready)
                elif not last:
                    x_turn(s + 1, 1 - p)
                if not first:
                    down(s - 1, 2)
                up(s, p, 1)
                gates_spread(s, p, 1)
                if not first:
                    down(s - 1, 3)
                up(s, p, 2)
                if not last:
                    router(s + 1, 1 - p)
                if not first:
                    down(s - 1, 4)
                gates_spread(s, p, 2)
                up(s, p, 3)
                if not first:
                    back(s - 1)
                down(s, 0)
                gates_spread(s, p, 3)
                up(s, p, 4)
                down(s, 1)
                gates_spread(s, p, 4)
            run_steps(pe, step)
            for c in (2, 3, 4):
                down(B - 1, c)
            back(B - 1)


CONSTANTS = {}


def constants():
    import numpy as np
    row = np.arange(P)
    made = {"ident": np.eye(P),
            "mhalf": np.full((P, SEQ_TILES), -0.5),
            "euler": np.full((P, SEQ_TILES), np.exp(1.0)),
            "order": np.tile(E - np.arange(E), (P, 1)),
            "sel": np.kron((row[:, None] % E == np.arange(E)) & (row[:, None] < 4 * E), np.ones((1, H)))}
    block, inner = row // CHUNK, row % CHUNK
    same = block[:, None] == block
    made |= {
        "upto": same & (inner[:, None] <= inner),
        "after": same & (inner[:, None] > inner),
        "spread": inner[:, None] == inner,
        "spread_one": np.concatenate([(inner[:, None] == inner) & (block[:, None] == c) for c in range(BLOCKS)], axis=1),
        "own_block": block[:, None] == np.arange(BLOCKS),
        "causal": inner[:, None] <= np.arange(CHUNK),
        "causal_block": same & (inner[:, None] <= inner),
        "own_tile": np.kron(row[:, None] // HEADS == np.arange(SEQ_TILES), np.ones((1, BLOCKS))),
        "own_head": row[:, None] % HEADS == row // HDIM,
        "own_chunk": row[:, None] // STATE == block,
        "head_of": row[:, None] // HDIM == np.arange(HEADS)}
    at = 0
    for name, a in made.items():
        CONSTANTS[name] = (at, a.shape[1])
        at += a.shape[1]
    return np.ascontiguousarray(np.concatenate([a.astype(np.float32) for a in made.values()], axis=1))


def setup(nc, R, ins, ctx):
    def sb(name, shape, dt=F32):
        return ctx.enter_context(nc.sbuf_tensor(name, shape, dt))

    def sem(name):
        return ctx.enter_context(nc.semaphore(name))

    NU = PAIRS * P
    R["settled"] = sem("settled")
    R["X"] = sb("X", [P, TILES + SEQ_TILES, D])
    R["x_loaded"] = [sem(f"x_loaded{s}") for s in range(B)]
    R["const"] = sb("const", [P, ins["constants"].shape[1]])
    for name, (at, n) in CONSTANTS.items():
        R[name] = R["const"][:, at:at + n]
    for name, shape, dt in (("router_b", [P, E], F32), ("spread_gates", [4 * E, E * H], F32R),
                            ("rw", [P, E], F32), ("rw_parts", [P, 2 * E], F32R),
                            ("wg_hi", [P, NU], F32R), ("wg_lo", [P, NU], F32R), ("wu_hi", [P, NU], F32R),
                            ("wu_lo", [P, NU], F32R), ("wd_hi", [P, NU], F32R), ("wd_lo", [P, NU], F32R)):
        R[name] = sb(name, shape, dt)
    R["bank"] = [ctx.enter_context(nc.psum_tensor(f"bank{k}", [P, 512], F32)) for k in range(8)]
    x_dram = ins["L0_attn_u"].rearrange("b (t p) d -> b p t d", p=P)
    R["x_dram"] = [x_dram[s] for s in range(B)]

    with ExitStack() as own_ctx:
        wg, wu, wd = (own_ctx.enter_context(nc.sbuf_tensor(f"{n}_in", [P, NU], F32)) for n in ("wg", "wu", "wd"))
        small_in, up_in, down_in, const_in, hi_ready = (own_ctx.enter_context(nc.semaphore(n)) for n in (
            "small_in", "up_in", "down_in", "const_in", "hi_ready"))
        block = own_ctx.enter_context(nc.Block())

        @block.sync
        def _(sp):
            sp.dma_start(R["const"][:, :], ins["constants"]).then_inc(const_in, 16)
            for s in range(2):
                sp.dma_start(R["X"][:, s * SEQ_TILES:(s + 1) * SEQ_TILES, :], R["x_dram"][s]).then_inc(R["x_loaded"][s], 16)
            for w, which in ((wg, "w1"), (wu, "w3")):
                v = w[:, :].rearrange("p (e h) -> p e h", h=H)
                sp.dma_start(v[:, 0:SHARED, :], ins[f"L0_ffn_shared_{which}"].rearrange("e d h -> d e h")).then_inc(up_in, 16)
                sp.dma_start(v[:, SHARED:, :], ins[f"L0_ffn_routed_{which}"].rearrange("e d h -> d e h")).then_inc(up_in, 16)

        @block.scalar
        def _(act):
            act.dma_start(R["rw"][:, :], ins["L0_ffn_router_w"]).then_inc(small_in, 16)
            act.dma_start(R["router_b"][:, :], ins["L0_ffn_router_b"].rearrange("(o e) -> o e", o=1).to_broadcast([P, E])).then_inc(small_in, 16)
            v = wd[:, :].rearrange("p (j d) -> p j d", d=D)
            act.dma_start(v[:, 0:1, :], ins["L0_ffn_shared_w2"].rearrange("(j e) h d -> (e h) j d", e=2)).then_inc(down_in, 16)
            act.dma_start(v[:, 1:, :], ins["L0_ffn_routed_w2"].rearrange("(j e) h d -> (e h) j d", e=2)).then_inc(down_in, 16)
            act.wait_ge(small_in, 32)
            act.activation(R["rw_parts"][:, 0:E], R["rw"][:, :], ACT.Copy).then_inc(hi_ready, 1)
            act.wait_ge(up_in, 64)
            act.activation(R["wg_hi"][:, :], wg[:, :], ACT.Copy).then_inc(hi_ready, 1)
            act.activation(R["wu_hi"][:, :], wu[:, :], ACT.Copy).then_inc(hi_ready, 1)
            act.wait_ge(down_in, 32)
            act.activation(R["wd_hi"][:, :], wd[:, :], ACT.Copy, scale=0.5).then_inc(hi_ready, 1)

        @block.vector
        def _(dve):
            dve.memset(R["X"][:, TILES:, :], 0.0)
            dve.wait_ge(const_in, 16)
            dve.tensor_copy(R["spread_gates"][:, :], R["sel"][0:4 * E, :])
            dve.wait_ge(hi_ready, 1)
            dve.tensor_tensor(R["rw_parts"][:, E:2 * E], R["rw"][:, :], R["rw_parts"][:, 0:E], ALU.subtract)
            for n, (name, src) in enumerate((("wg", wg), ("wu", wu))):
                dve.wait_ge(hi_ready, n + 2)
                dve.tensor_tensor(R[f"{name}_lo"][:, :], src[:, :], R[f"{name}_hi"][:, :], ALU.subtract)
            dve.wait_ge(hi_ready, 4)
            dve.scalar_tensor_tensor(R["wd_lo"][:, :], wd[:, :], 0.5, R["wd_hi"][:, :], ALU.mult, ALU.subtract)


def mamba_setup(nc, R, ins, ctx):
    def sb(name, shape, dt=F32):
        R[name] = ctx.enter_context(nc.sbuf_tensor(name, shape, dt))
        return R[name]

    W = TAPS * P
    for name, n in (("wz", P + D), ("wx", W), ("wbc", W)):
        sb(f"{name}_hi", [P, n], F32R)
        sb(f"{name}_lo", [P, n], F32R)
    sb("wdt_parts", [P, 2 * HEADS], F32R)
    sb("wo_y", [P, D])
    sb("out_bias", [P, D])
    sb("decay_rate", [P, HEADS])
    sb("dt_bias", [P, HEADS])
    sb("skip", [P, HALF])
    sb("cb_x", [P, 1])
    sb("cb_bc", [P, 1])
    W_in, conv_w, conv_b = ins["L0_attn_W_in"], ins["L0_attn_conv_w"], ins["L0_attn_conv_b"]

    with ExitStack() as own_ctx:
        def tmp(name, shape, dt=F32):
            return own_ctx.enter_context(nc.sbuf_tensor(name, shape, dt))

        def sem(name):
            return own_ctx.enter_context(nc.semaphore(name))

        rz, rx, rbc, rdt = tmp("rz", [P, D]), tmp("rx", [P, D]), tmp("rbc", [P, D]), tmp("rdt", [HEADS, D])
        cw_x, cw_bc = tmp("cw_x", [P, TAPS]), tmp("cw_bc", [P, TAPS])
        tx, tbc = tmp("tx", [P, TAPS, D]), tmp("tbc", [P, TAPS, D])
        wo_rows, wo_raw, wo, wo_z = tmp("wo_rows", [P, 2 * D]), tmp("wo_raw", [P, 2 * D]), tmp("wo", [P, 2 * D]), tmp("wo_z", [P, D])
        share, lnb_cols = tmp("share", [P, P]), tmp("lnb_cols", [P, 2, P])
        lnw, lnb = tmp("lnw", [P, 2]), tmp("lnb", [P, 2])
        alog, dskip, dcol, dcol8 = tmp("alog", [P, HEADS]), tmp("dskip", [P, HEADS]), tmp("dcol", [P, 1]), tmp("dcol8", [P, HEADS])
        cleared, rows_in, taps_ready, turned = sem("cleared"), sem("rows_in"), sem("taps_ready"), sem("turned")
        high, raw_ready, wo_ready, own, small = sem("high"), sem("raw_ready"), sem("wo_ready"), sem("own_s"), sem("small_m")
        expd, mean_ready, wo_z_ready, z_turned = sem("expd"), sem("mean_ready"), sem("wo_z_ready"), sem("z_turned")
        bk = R["bank"]
        block = own_ctx.enter_context(nc.Block())
        B0, C0, DT0 = 2 * HALF, 2 * HALF + STATE, 2 * HALF + 2 * STATE

        def col(v):
            return v.rearrange("(p o) -> p o", o=1)

        @block.sync
        def _(sp):
            sp.dma_start(wo_rows[:, :], ins["L0_attn_W_out"]).then_inc(rows_in, 16)
            sp.dma_start(rz[:, :], W_in[0:HALF, :]).then_inc(rows_in, 16)
            sp.dma_start(rx[:, :], W_in[HALF:2 * HALF, :]).then_inc(rows_in, 16)
            sp.dma_start(rdt[:, :], W_in[DT0:DT0 + HEADS, :]).then_inc(rows_in, 16)
            sp.dma_start(cw_x[:, :], conv_w[0:HALF, 0, :]).then_inc(rows_in, 16)
            sp.dma_start(R["cb_x"][:, :], col(conv_b[0:HALF])).then_inc(rows_in, 16)
            sp.wait_ge(cleared, 3)
            for r in range(BLOCKS + 1):
                src = C0 if r < BLOCKS else B0
                rows = slice(r * STATE, (r + 1) * STATE)
                sp.dma_start(rbc[rows, :], W_in[src:src + STATE, :]).then_inc(rows_in, 16)
                sp.dma_start(cw_bc[rows, :], conv_w[src - HALF:src - HALF + STATE, 0, :]).then_inc(rows_in, 16)
                sp.dma_start(R["cb_bc"][rows, :], col(conv_b[src - HALF:src - HALF + STATE])).then_inc(rows_in, 16)

        @block.scalar
        def _(act):
            def row(v):
                return v.rearrange("(o e) -> o e", o=1).to_broadcast([P, HEADS])
            act.dma_start(alog[:, :], row(ins["L0_attn_A_log"])).then_inc(small, 16)
            act.dma_start(dskip[:, :], row(ins["L0_attn_Dskip"])).then_inc(small, 16)
            act.dma_start(R["dt_bias"][:, :], row(ins["L0_attn_dt_bias"])).then_inc(small, 16)
            for j in range(2):
                act.dma_start(lnw[:, j:j + 1], col(ins["L0_attn_ln_w"][j * P:(j + 1) * P])).then_inc(small, 16)
                act.dma_start(lnb[:, j:j + 1], col(ins["L0_attn_ln_b"][j * P:(j + 1) * P])).then_inc(small, 16)
            act.wait_ge(small, 16 * 7)
            act.activation(alog[:, :], alog[:, :], ACT.Exp).then_inc(expd, 1)
            for n, name in enumerate(("wx", "wbc")):
                act.wait_ge(turned, n + 1)
                act.activation(R[f"{name}_hi"][:, :], bk[n][:, 0:W], ACT.Copy).then_inc(high, 1)
            act.wait_ge(z_turned, 1)
            act.activation(R["wz_hi"][:, :], bk[3][:, 0:P + D], ACT.Copy)
            act.activation(R["wdt_parts"][:, 0:HEADS], bk[3][:, P + D:P + D + HEADS], ACT.Copy).then_inc(high, 1)

        @block.vector
        def _(dve):
            dve.memset(rbc[:, :], 0.0).then_inc(cleared, 1)
            dve.memset(cw_bc[:, :], 0.0).then_inc(cleared, 1)
            dve.memset(R["cb_bc"][:, :], 0.0).then_inc(cleared, 1)
            dve.memset(share[:, :], 1.0 / (2 * HALF))
            dve.wait_ge(rows_in, 16 * (6 + 3 * (BLOCKS + 1)))
            for t in range(TAPS):
                dve.tensor_scalar(tx[:, t, :], rx[:, :], cw_x[:, t:t + 1], None, ALU.mult)
                i = dve.tensor_scalar(tbc[:, t, :], rbc[:, :], cw_bc[:, t:t + 1], None, ALU.mult)
            i.then_inc(taps_ready, 1)
            dve.wait_ge(expd, 1)
            dve.tensor_scalar(R["decay_rate"][:, :], alog[:, :], -1.0, None, ALU.mult)
            dve.tensor_tensor(dcol8[:, :], dskip[:, :], R["head_of"], ALU.mult).then_inc(own, 1)
            dve.tensor_copy(lnb_cols[:, :, :], lnb[:, :].rearrange("p (j o) -> p j o", o=1).to_broadcast([P, 2, P]))
            dve.wait_ge(own, 1)
            dve.tensor_reduce(dcol[:, :], dcol8[:, :], AX.X, ALU.add).then_inc(own, 1)
            dve.wait_ge(turned, 3)
            dve.tensor_copy(wo_raw[:, :], bk[2][:, 0:2 * D]).then_inc(raw_ready, 1)
            dve.wait_ge(own, 2)
            dve.tensor_scalar(R["skip"][:, :], R["ident"], dcol[:, 0:1], None, ALU.mult)
            dve.wait_ge(raw_ready, 1)
            for j in range(2):
                i = dve.tensor_scalar(wo[:, j * D:(j + 1) * D], wo_raw[:, j * D:(j + 1) * D], lnw[:, j:j + 1], None, ALU.mult)
            i.then_inc(wo_ready, 1)
            dve.wait_ge(wo_ready, 1)
            dve.wait_ge(mean_ready, 1)
            dve.tensor_tensor(wo_z[:, :], wo[:, D:2 * D], bk[4][:, 0:D], ALU.subtract).then_inc(wo_z_ready, 1)
            dve.tensor_tensor(R["wo_y"][:, :], wo[:, 0:D], bk[4][:, 0:D], ALU.subtract)
            dve.tensor_copy(R["out_bias"][:, :], bk[4][:, D:2 * D])
            for n, name in enumerate(("wx", "wbc")):
                dve.wait_ge(high, n + 1)
                dve.tensor_tensor(R[f"{name}_lo"][:, :], bk[n][:, 0:W], R[f"{name}_hi"][:, :], ALU.subtract)
            dve.wait_ge(high, 3)
            dve.tensor_tensor(R["wz_lo"][:, :], bk[3][:, 0:P + D], R["wz_hi"][:, :], ALU.subtract)
            dve.tensor_tensor(R["wdt_parts"][:, HEADS:2 * HEADS], bk[3][:, P + D:P + D + HEADS],
                              R["wdt_parts"][:, 0:HEADS], ALU.subtract)

        @block.tensor
        def _(pe):
            pe.wait_ge(taps_ready, 1)
            for t in range(TAPS):
                i = pe.transpose(bk[0][:, t * P:(t + 1) * P], tx[:, t, :], R["ident"])
            i.then_inc(turned, 1)
            for t in range(TAPS):
                i = pe.transpose(bk[1][:, t * P:(t + 1) * P], tbc[:, t, :], R["ident"])
            i.then_inc(turned, 1)
            for j in range(2):
                i = pe.transpose(bk[2][:, j * D:(j + 1) * D], wo_rows[:, j * D:(j + 1) * D], R["ident"])
            i.then_inc(turned, 1)
            pe.transpose(bk[3][:, 0:P], rz[:, :], R["ident"])
            pe.transpose(bk[3][:, P + D:P + D + HEADS], rdt[:, :], R["ident"][0:HEADS, 0:HEADS])
            pe.wait_ge(wo_ready, 1)
            for j in range(2):
                pe.matmul(bk[4][:, 0:D], share[:, :], wo[:, j * D:(j + 1) * D], start=(j == 0), stop=(j == 1))
            for j in range(2):
                i = pe.matmul(bk[4][:, D:2 * D], lnb_cols[:, j, :], wo_raw[:, j * D:(j + 1) * D], start=(j == 0),
                              stop=(j == 1))
            i.then_inc(mean_ready, 1)
            pe.wait_ge(wo_z_ready, 1)
            pe.matmul(bk[3][:, P:P + D], rz[:, :], wo_z[:, :], start=True, stop=True).then_inc(z_turned, 1)


def mamba_phase(nc, R):
    X, bk = R["X"], R["bank"]
    with ExitStack() as ctx:
        def sb(name, shape, dt=F32):
            return ctx.enter_context(nc.sbuf_tensor(f"m_{name}", shape, dt))

        def sems(names):
            return [ctx.enter_context(nc.semaphore(f"m_{n}")) for n in names.split()]

        TH = SEQ_TILES * HEADS
        NC = BLOCKS * STATE
        PAD = TAPS - 1
        stats, mv = sb("stats", [P, SEQ_TILES, 6]), sb("mv", [P, SEQ_TILES, 2])
        ve, rstd = sb("ve", [P, SEQ_TILES]), sb("rstd", [P, SEQ_TILES])
        xn = [sb(f"xn{p}", [P, SEQ_TILES, D]) for p in range(2)]
        xh = [sb(f"xh{p}", [P, PAD + L], F32R) for p in range(2)]
        xl = [sb(f"xl{p}", [P, PAD + L], F32R) for p in range(2)]
        raw, neg, u, v, w, q, pos = (sb(n, [P, TH]) for n in ("raw", "neg", "u", "v", "w", "q", "pos"))
        dt = [sb(f"dt{p}", [P, TH]) for p in range(2)]
        at = sb("at", [P, TH])
        ecd = [sb(f"ecd{p}", [P, 2 * TH]) for p in range(2)]
        amask, aB = sb("amask", [P, P]), sb("aB", [P, CHUNKS * HGROUPS])
        totX = sb("totX", [TH, CHUNKS])
        carry = sb("carry", [P, STATE, CHUNKS])
        xc, Cc, Bc = sb("xc", [P, L]), sb("Cc", [NC, L]), sb("Bc", [STATE, L])
        xdt, xdec = sb("xdt", [P, L]), sb("xdec", [P, L])
        XB = sb("XB", [P, SEQ_TILES, BLOCKS, HGROUPS, BLOCKS * HDIM])
        Bm, Gm = sb("Bm", [P, SEQ_TILES, BLOCKS, STATE]), sb("Gm", [P, SEQ_TILES, P])
        Rg = [sb(f"Rg{g}", [P, CHUNKS, CHUNK]) for g in range(HGROUPS)]
        Eg = [sb(f"Eg{g}", [P, L]) for g in range(HGROUPS)]
        Mg = [sb(f"Mg{g}", [P, BLOCKS, SEQ_TILES, CHUNK]) for g in range(HGROUPS)]
        after_chunk, state = sb("after_chunk", [P, STATE, CHUNKS]), sb("state", [P, CHUNKS, STATE])
        STs, Cm = sb("STs", [NC, L]), sb("Cm", [NC, L])
        yo, y = sb("yo", [P, L]), sb("y", [P, L])
        stats2, mv2 = sb("stats2", [P, SEQ_TILES, 2, 6]), sb("mv2", [P, SEQ_TILES, 2])
        ve2, rstd2 = sb("ve2", [P, SEQ_TILES]), sb("rstd2", [P, SEQ_TILES])
        yT = sb("yT", [P, L])

        PZ = [bk[0], bk[2]]
        PS = bk[1]
        PXT, PX, PBT, PST = bk[3], bk[3], bk[3], bk[3]
        PSTT, PYO, PBC, PGR = bk[4], bk[4], bk[4], bk[4]
        PY = bk[5]
        PSEG = [bk[6], bk[7]]
        PYT = bk[7]
        PXCT, PG = bk[6], bk[6]
        SUM0, BT0 = 2 * TH, STATE * CHUNKS

        (xT_ready, dt_ready, cum_ready, total_ready, z_ready, x_ready, bc_ready, xt_ready, bt_ready, g_ready, g_spread,
         seg0_ready, seg1_ready, y_ready, st_ready, stt_ready, yoff_ready, yt_ready, o_ready) = pe_sems = sems(
            "xT_ready dt_ready cum_ready total_ready z_ready x_ready bc_ready xt_ready bt_ready g_ready g_spread "
            "seg0_ready seg1_ready y_ready st_ready stt_ready yoff_ready yt_ready o_ready")
        (xh_ready, exp_ready, decay_ready, carry_ready, xc_ready, cb_ready, e0_ready, e1_ready, states_copied,
         xb_act, yT_ready) = act_sems = sems(
            "xh_ready exp_ready decay_ready carry_ready xc_ready cb_ready e0_ready e1_ready states_copied xb_act yT_ready")
        (ve_ready, xn_ready, xl_ready, neg_ready, at_ready, ab_ready, totx_ready, xdt_ready, xdec_ready, xb_dve,
         bm_ready, gm_ready, m0_ready, m1_ready, scan_done, yo_ready, yz_ready, ve2_ready, zstats_done,
         x_done) = dve_sems = sems(
            "ve_ready xn_ready xl_ready neg_ready at_ready ab_ready totx_ready xdt_ready xdec_ready xb_dve "
            "bm_ready gm_ready m0_ready m1_ready scan_done yo_ready yz_ready ve2_ready zstats_done x_done")
        (rstd_ready, r0_ready, r1_ready, cm_ready, rstd2_ready, bias_added, state_ready) = pool_sems = sems(
            "rstd_ready r0_ready r1_ready cm_ready rstd2_ready bias_added state_ready")
        own_time, own_norm, own_out, own_decay = sems("own_time own_norm own_out own_decay")
        TIME_OPS, NORM_OPS, OUT_OPS = 15, 2, 2

        def starts(engine, made):
            for one in made:
                engine.sem_inc(one, 1)

        def now(engine, *which):
            s, which = which[-1], which[:-1]
            for one in which:
                engine.wait_ge(one, s + 2)

        def before(engine, *which):
            s, which = which[-1], which[:-1]
            for one in which:
                engine.wait_ge(one, s + 1)

        def tiles(a, n=D):
            return a[:, :].rearrange("p (t d) -> p t d", d=n)

        def tile(t):
            return slice(t * P, (t + 1) * P)

        def spread_block(engine, c, b):
            src = xdt[c * CHUNK:(c + 1) * CHUNK, :].rearrange("p (t g b k) -> p t g b k", t=SEQ_TILES, g=HGROUPS,
                                                              b=BLOCKS)[:, :, :, b, :]
            return XB[b * CHUNK:(b + 1) * CHUNK, :, c, :, b * HDIM:(b + 1) * HDIM], src

        block = ctx.enter_context(nc.Block())

        @block.gpsimd
        def _(pool):
            starts(pool, pool_sems)

            def norm_power(s):
                now(pool, ve_ready, s)
                pool.tensor_tensor(rstd[:, :], ve[:, :], R["mhalf"], ALU.pow).then_inc(rstd_ready, 1)

            def out_power(s):
                now(pool, ve2_ready, s)
                pool.tensor_tensor(rstd2[:, :], ve2[:, :], R["mhalf"], ALU.pow).then_inc(rstd2_ready, 1)

            def spread_decays(s):
                now(pool, ab_ready, s)
                for g, (seg, done) in enumerate(((seg0_ready, r0_ready), (seg1_ready, r1_ready))):
                    before(pool, seg, s)
                    a = aB[:, :].rearrange("p (c g o) -> p c g o", g=HGROUPS, o=1)[:, :, g, :]
                    pool.tensor_tensor(Rg[g][:, :, :], a.to_broadcast([P, CHUNKS, CHUNK]),
                                       R["causal"].rearrange("p (o l) -> p o l", o=1).to_broadcast([P, CHUNKS, CHUNK]),
                                       ALU.mult).then_inc(done, 1)

            def add_bias(s):
                now(pool, xn_ready, s)
                seq = X[:, bass.ds(s * SEQ_TILES, SEQ_TILES), :]
                pool.tensor_tensor(seq, seq, R["out_bias"][:, :].rearrange("p (o d) -> p o d", o=1)
                                   .to_broadcast([P, SEQ_TILES, D]), ALU.add).then_inc(bias_added, 1)

            def step(s, p, first, last):
                add_bias(s)
                if not last:
                    norm_power(s + 2)
                if not first:
                    out_power(s - 1)
                now(pool, cb_ready, s)
                before(pool, yoff_ready, s)
                pool.tensor_tensor(tiles(Cm, P), tiles(Cc, P),
                                   R["own_chunk"][0:NC, :].rearrange("p (o l) -> p o l", o=1)
                                   .to_broadcast([NC, SEQ_TILES, P]), ALU.mult).then_inc(cm_ready, 1)
                if not last:
                    spread_decays(s + 1)
                states(s)

            def states(s):
                now(pool, scan_done, s)
                before(pool, stt_ready, s)
                settle(pool, R["settled"])
                pool.tensor_copy(state[:, 1:, :],
                                 after_chunk[:, :, 0:CHUNKS - 1].rearrange("p n c -> p c n")).then_inc(state_ready, 1)

            norm_power(0)
            norm_power(1)
            spread_decays(0)
            run_steps(pool, step)
            out_power(B - 1)

        @block.scalar
        def _(act):
            starts(act, act_sems)

            def x_high(s, p):
                now(act, xT_ready, s)
                act.activation(xh[p][:, PAD:], PXT[:, :], ACT.Copy).then_inc(xh_ready, 1)

            def dt_exp(s):
                now(act, neg_ready, s)
                act.activation(u[:, :], neg[:, :], ACT.Exp).then_inc(exp_ready, 1)

            def decays(s, p):
                now(act, total_ready, s)
                act.activation(ecd[p][:, :], PS[:, SUM0:SUM0 + 2 * TH], ACT.Exp).then_inc(decay_ready, 1)

            def carries(s):
                before(act, scan_done, s)
                act.activation(carry[:, :, 1:], PS[:, 257:256 + CHUNKS].rearrange("p (o c) -> p o c", o=1)
                               .to_broadcast([P, STATE, CHUNKS - 1]), ACT.Exp).then_inc(carry_ready, 1)

            def states_copy(s):
                now(act, stt_ready, s)
                before(act, yoff_ready, s)
                act.activation(STs[:, :], PSTT[0:NC, :], ACT.Copy).then_inc(states_copied, 1)

            def y_copy(s):
                now(act, yt_ready, s)
                before(act, o_ready, s)
                act.activation(yT[:, :], PYT[:, :], ACT.Copy).then_inc(yT_ready, 1)

            x_high(0, 0)
            dt_exp(0)

            def step(s, p, first, last):
                if not first:
                    states_copy(s - 1)
                decays(s, p)
                carries(s)
                if not last:
                    x_high(s + 1, 1 - p)
                for g, (seg, m, done) in enumerate(((seg0_ready, m0_ready, e0_ready), (seg1_ready, m1_ready, e1_ready))):
                    now(act, seg, s)
                    before(act, m, s)
                    act.activation(Eg[g][:, :], PSEG[g][:, :], ACT.Exp).then_inc(done, 1)
                if not last:
                    dt_exp(s + 1)
                now(act, x_ready, s)
                before(act, y_ready, s)
                act.activation(xc[:, :], PX[:, :], ACT.Silu, bias=R["cb_x"][:, 0:1]).then_inc(xc_ready, 1)
                if not first:
                    y_copy(s - 1)
                now(act, bc_ready, s)
                before(act, cm_ready, s)
                act.activation(Cc[:, :], PBC[0:NC, :], ACT.Silu, bias=R["cb_bc"][0:NC, 0:1])
                act.activation(Bc[:, :], PBC[NC:NC + STATE, :], ACT.Silu, bias=R["cb_bc"][NC:NC + STATE, 0:1])\
                    .then_inc(cb_ready, 1)
                now(act, xdt_ready, s)
                for c in range(BLOCKS // 2, BLOCKS):
                    for b in range(BLOCKS):
                        dst, src = spread_block(act, c, b)
                        i = act.activation(dst, src, ACT.Copy)
                i.then_inc(xb_act, 1)
            run_steps(act, step)
            states_copy(B - 1)
            y_copy(B - 1)

        @block.vector
        def _(dve):
            starts(dve, dve_sems)
            dve.memset(XB[:, :, :, :, :], 0.0)
            dve.memset(state[:, 0:1, :], 0.0)
            dve.memset(carry[:, :, 0:1], 0.0)
            for p in range(2):
                dve.memset(xh[p][:, 0:PAD].bitcast(F32), 0.0)
                dve.memset(xl[p][:, 0:PAD].bitcast(F32), 0.0)

            def heads(a, at):
                return a[:, at:at + TH].rearrange("p (h o) -> p h o", o=1).to_broadcast([P, TH, HDIM])

            def per_head(a):
                return a[:, :].rearrange("p (h o) -> p h o", o=HDIM)

            def norm_stats(s):
                for t in range(SEQ_TILES):
                    i = dve.bn_stats(stats[:, t, :], X[:, bass.ds(s * SEQ_TILES + t, 1), :])
                i.then_inc(own_norm, 1)

            def norm_moments(s):
                dve.wait_ge(own_norm, s * NORM_OPS + 1)
                settle(dve, R["settled"])
                for t in range(SEQ_TILES):
                    i = dve.bn_aggr(mv[:, t, :], stats[:, t, :])
                i.then_inc(own_norm, 1)

            def norm_variance(s):
                dve.wait_ge(own_norm, s * NORM_OPS + 2)
                dve.tensor_scalar(ve[:, :], mv[:, :, 1], EPS, None, ALU.add).then_inc(ve_ready, 1)

            def norm_apply(s, p, t):
                if t == 0:
                    now(dve, rstd_ready, s)
                i = dve.tensor_scalar(xn[p][:, t:t + 1, :], X[:, bass.ds(s * SEQ_TILES + t, 1), :],
                                      mv[:, t, 0:1], rstd[:, t:t + 1], ALU.subtract, ALU.mult)
                if t == SEQ_TILES - 1:
                    i.then_inc(xn_ready, 1)

            def x_low(s, p):
                now(dve, xh_ready, s)
                dve.tensor_tensor(xl[p][:, PAD:], PXT[:, :], xh[p][:, PAD:], ALU.subtract).then_inc(xl_ready, 1)

            class TimeSteps:
                def __init__(self, s, p):
                    self.s, self.p = s, p
                    self.own = Own(dve, own_time, s * TIME_OPS, TIME_OPS)

                def th(self, a):
                    return a[:, 0:TH].rearrange("p (t h) -> p t h", h=HEADS)

                def part(self, k):
                    return PS[:, 0:2 * TH].rearrange("p (t k h) -> p t k h", k=2, h=HEADS)[:, :, k, :]

                def row(self, a):
                    return a[:, :].rearrange("p (o h) -> p o h", o=1).to_broadcast([P, SEQ_TILES, HEADS])

                def biased(self):
                    now(dve, dt_ready, self.s)
                    return dve.tensor_tensor(self.th(v), self.part(1), self.row(R["dt_bias"]), ALU.add)

                def raw(self):
                    return dve.tensor_tensor(self.th(raw), self.part(0), self.th(v), ALU.add)

                def negative(self):
                    return dve.scalar_tensor_tensor(neg[:, :], raw[:, :], -1.0, raw[:, :], ALU.mult, ALU.min)\
                        .then_inc(neg_ready, 1)

                def positive(self):
                    dve.tensor_scalar(pos[:, :], raw[:, :], 0.0, None, ALU.max)

                def plus_two(self):
                    now(dve, exp_ready, self.s)
                    return dve.tensor_scalar(v[:, :], u[:, :], 2.0, None, ALU.add)

                def inverse(self):
                    return dve.reciprocal(w[:, :], v[:, :])

                def ratio(self):
                    return dve.tensor_tensor(v[:, :], u[:, :], w[:, :], ALU.mult)

                def square(self):
                    return dve.tensor_tensor(w[:, :], v[:, :], v[:, :], ALU.mult)

                def term(self, k):
                    if k == len(ARTANH) - 1:
                        return dve.tensor_scalar(q[:, :], w[:, :], ARTANH[k], None, ALU.mult)
                    return dve.scalar_tensor_tensor(q[:, :], q[:, :], ARTANH[k], w[:, :] if k else v[:, :], ALU.add, ALU.mult)

                def softplus(self):
                    return dve.scalar_tensor_tensor(dt[self.p][:, :], q[:, :], 2.0, pos[:, :], ALU.mult, ALU.add)

                def decay(self):
                    dve.tensor_tensor(self.th(at), self.th(dt[self.p]), self.row(R["decay_rate"]), ALU.mult)\
                        .then_inc(at_ready, 1)

            def block_decays(s):
                now(dve, cum_ready, s)
                dve.tensor_tensor(amask[:, :].rearrange("p (c b) -> p c b", b=BLOCKS),
                                  PS[:, 128:256].rearrange("p (c b) -> p c b", b=BLOCKS),
                                  R["own_block"].rearrange("p (o b) -> p o b", o=1)
                                  .to_broadcast([P, CHUNKS * HGROUPS, BLOCKS]), ALU.mult).then_inc(own_decay, 1)
                dve.tensor_tensor(totX[:, :].rearrange("p (t c) -> p t c", c=BLOCKS),
                                  PS[0:TH, 272:272 + BLOCKS].rearrange("p (o c) -> p o c", o=1)
                                  .to_broadcast([TH, SEQ_TILES, BLOCKS]),
                                  R["own_tile"][0:TH, :].rearrange("p (t c) -> p t c", c=BLOCKS), ALU.mult)\
                    .then_inc(totx_ready, 1)
                dve.wait_ge(own_decay, s + 1)
                before(dve, r1_ready, s)
                dve.tensor_reduce(aB[:, :], amask[:, :].rearrange("p (c b) -> p c b", b=BLOCKS), AX.X, ALU.add)\
                    .then_inc(ab_ready, 1)

            def states_part(s, p):
                now(dve, yoff_ready, s)
                dve.tensor_tensor(per_head(yo), per_head(PYO), heads(ecd[p], 0), ALU.mult).then_inc(yo_ready, 1)

            def y_sum(s):
                now(dve, y_ready, yo_ready, s)
                before(dve, yt_ready, s)
                dve.tensor_tensor(y[:, :], yo[:, :], PY[:, :], ALU.add).then_inc(yz_ready, 1)

            def y_stats(s, t):
                if t == 0:
                    now(dve, yz_ready, s)
                    settle(dve, R["settled"])
                i = dve.bn_stats(stats2[:, t, 0, :], y[:, tile(t)])
                if t == SEQ_TILES - 1:
                    i.then_inc(own_out, 1)

            def y_moments(s, t):
                if t == 0:
                    now(dve, zstats_done, s)
                    dve.wait_ge(own_out, s * OUT_OPS + 1)
                    settle(dve, R["settled"])
                i = dve.bn_aggr(mv2[:, t, :], stats2[:, t, :, :].rearrange("p k n -> p (k n)"))
                if t == SEQ_TILES - 1:
                    i.then_inc(own_out, 1)

            def y_variance(s):
                dve.wait_ge(own_out, s * OUT_OPS + 2)
                dve.tensor_scalar(ve2[:, :], mv2[:, :, 1], EPS, None, ALU.add).then_inc(ve2_ready, 1)

            def z_stats(s):
                now(dve, z_ready, s)
                for t in range(SEQ_TILES):
                    i = dve.bn_stats(stats2[:, t, 1, :], PZ[t // 2][:, (t % 2) * 2 * D:(t % 2) * 2 * D + HALF])
                i.then_inc(zstats_done, 1)

            def residual(s):
                now(dve, o_ready, s)
                now(dve, rstd2_ready, s)
                now(dve, bias_added, s)
                for t in range(SEQ_TILES):
                    seq = X[:, bass.ds(s * SEQ_TILES + t, 1), :].rearrange("p o d -> p (o d)")
                    at_col = (t % 2) * 2 * D + HALF
                    i = dve.scalar_tensor_tensor(seq, PZ[t // 2][:, at_col:at_col + D], rstd2[:, t:t + 1], seq,
                                                 ALU.mult, ALU.add)
                i.then_inc(x_done, 1)

            def first_norm(s):
                norm_stats(s)
                norm_moments(s)
                norm_variance(s)
                for t in range(SEQ_TILES):
                    norm_apply(s, s, t)

            first_norm(0)
            x_low(0, 0)
            g = TimeSteps(0, 0)
            link = g.own.link
            link(g.biased())
            link(g.raw())
            g.negative()
            g.positive()
            for line in (g.plus_two, g.inverse, g.ratio, g.square):
                link(line())
            for k in range(len(ARTANH) - 1, -1, -1):
                link(g.term(k))
            link(g.softplus())
            g.decay()
            g.own.close()
            first_norm(1)
            block_decays(0)

            def step(s, p, first, last):
                back = not first
                ahead = not last

                def apart(i, work, *args):
                    g.own.mark(i)
                    if work in (y_stats, y_moments, y_variance):
                        if back:
                            work(s - 1, *args)
                    elif work is norm_apply:
                        norm_apply(s + 2, p, *args)
                    g.own.ready()

                if ahead:
                    x_low(s + 1, 1 - p)
                    norm_stats(s + 2)
                if back:
                    states_part(s - 1, 1 - p)
                if ahead:
                    norm_moments(s + 2)
                if back:
                    y_sum(s - 1)
                if ahead:
                    norm_variance(s + 2)
                    g = TimeSteps(s + 1, 1 - p)
                    apart(g.biased(), y_stats, 0)
                    apart(g.raw(), y_stats, 1)
                    g.negative()
                    g.positive()
                    if back:
                        y_stats(s - 1, 2)
                        y_stats(s - 1, 3)
                    apart(g.plus_two(), y_moments, 0)
                    apart(g.inverse(), y_moments, 1)
                    apart(g.ratio(), y_moments, 2)
                    apart(g.square(), y_moments, 3)
                    apart(g.term(7), norm_apply, 0)
                    apart(g.term(6), y_variance)
                    apart(g.term(5), norm_apply, 1)
                    apart(g.term(4), norm_apply, 2)
                    apart(g.term(3), norm_apply, 3)
                    apart(g.term(2), None)
                    apart(g.term(1), None)
                    apart(g.term(0), None)
                    apart(g.softplus(), None)
                    g.decay()
                    g.own.close()
                else:
                    for t in range(SEQ_TILES):
                        y_stats(s - 1, t)
                    for t in range(SEQ_TILES):
                        y_moments(s - 1, t)
                    y_variance(s - 1)
                if back:
                    residual(s - 1)
                now(dve, xt_ready, s)
                before(dve, xb_act, s)
                dve.tensor_tensor(per_head(xdt), per_head(PXCT), heads(dt[p], 0), ALU.mult).then_inc(xdt_ready, 1)
                if ahead:
                    block_decays(s + 1)
                now(dve, xdt_ready, s)
                now(dve, decay_ready, s)
                before(dve, st_ready, s)
                dve.tensor_tensor(per_head(xdec), per_head(xdt), heads(ecd[p], TH), ALU.mult).then_inc(xdec_ready, 1)
                now(dve, bt_ready, s)
                dve.tensor_tensor(Bm[:, :, :, :],
                                  PBT[:, BT0:BT0 + SEQ_TILES * STATE].rearrange("p (t o n) -> p t o n", t=SEQ_TILES, o=1)
                                  .to_broadcast([P, SEQ_TILES, BLOCKS, STATE]),
                                  R["own_block"].rearrange("p (a c o) -> p a c o", a=1, o=1)
                                  .to_broadcast([P, SEQ_TILES, BLOCKS, STATE]), ALU.mult).then_inc(bm_ready, 1)
                now(dve, g_ready, s)
                before(dve, g_spread, s)
                dve.tensor_tensor(Gm[:, :, :], tiles(PG, P),
                                  R["causal_block"].rearrange("p (o l) -> p o l", o=1).to_broadcast([P, SEQ_TILES, P]),
                                  ALU.mult).then_inc(gm_ready, 1)
                before(dve, y_ready, s)
                for c in range(BLOCKS // 2):
                    for b in range(BLOCKS):
                        dst, src = spread_block(dve, c, b)
                        i = dve.tensor_copy(dst, src)
                i.then_inc(xb_dve, 1)
                z_stats(s)
                now(dve, g_spread, s)
                for g_, (e, done) in enumerate(((e0_ready, m0_ready), (e1_ready, m1_ready))):
                    now(dve, e, s)
                    dve.tensor_tensor(Mg[g_][:, :, :, :].rearrange("p c t l -> p (c t l)"), Eg[g_][:, :], PGR[:, :],
                                      ALU.mult).then_inc(done, 1)
                now(dve, st_ready, s)
                now(dve, carry_ready, s)
                before(dve, state_ready, s)
                dve.tensor_tensor_scan(after_chunk[:, :, :].rearrange("p n c -> p (n c)"),
                                       carry[:, :, :].rearrange("p n c -> p (n c)"), PST[:, 0:STATE * CHUNKS],
                                       0.0, ALU.mult, ALU.add).then_inc(scan_done, 1)
            run_steps(dve, step)
            states_part(B - 1, 1)
            y_sum(B - 1)
            for t in range(SEQ_TILES):
                y_stats(B - 1, t)
            for t in range(SEQ_TILES):
                y_moments(B - 1, t)
            y_variance(B - 1)
            residual(B - 1)

        @block.tensor
        def _(pe):
            starts(pe, pe_sems)

            def four(out, src, ident, done):
                for t in range(SEQ_TILES):
                    i = pe.transpose(out(t), src(t), ident)
                i.then_inc(done, 1)

            def x_turn(s, p):
                now(pe, xn_ready, s)
                if not isinstance(s, int) or s > 0:
                    before(pe, scan_done, s - 1)
                four(lambda t: PXT[:, tile(t)], lambda t: xn[p][:, t, :], R["ident"], xT_ready)

            def times(s, p):
                now(pe, xl_ready, s)
                before(pe, carry_ready, s)
                before(pe, ab_ready, s)
                for t in range(SEQ_TILES):
                    out, tt = PS[:, t * 2 * HEADS:(t + 1) * 2 * HEADS], slice(PAD + t * P, PAD + (t + 1) * P)
                    pe.matmul(out, xh[p][:, tt], R["wdt_parts"][:, :], start=(t == 0), stop=False, skip_group_check=True)
                    i = pe.matmul(out, xl[p][:, tt], R["wdt_parts"][:, :], start=False, stop=True, skip_group_check=True)
                i.then_inc(dt_ready, 1)

            def sums(s):
                now(pe, at_ready, s)
                pe.matmul(PS[:, SUM0:SUM0 + TH], R["upto"], at[:, :], start=True, stop=True)
                pe.matmul(PS[:, SUM0 + TH:SUM0 + 2 * TH], R["after"], at[:, :], start=True, stop=True)
                for c in range(BLOCKS):
                    pe.matmul(PS[:, 128 + c * TH:128 + (c + 1) * TH], R["spread_one"][:, tile(c)], at[:, :],
                              start=True, stop=True)
                pe.matmul(PS[0:TH, 272:272 + BLOCKS], at[:, :], R["own_block"], start=True, stop=True).then_inc(cum_ready, 1)

            def totals(s):
                now(pe, totx_ready, s)
                pe.matmul(PS[:, 256:256 + CHUNKS], R["own_head"][0:TH, :], totX[:, :], start=True, stop=True)\
                    .then_inc(total_ready, 1)

            def conv(out, w, p, done):
                for k in range(TAPS):
                    i = split_mm(pe, out, R[f"{w}_hi"][:, tile(k)], R[f"{w}_lo"][:, tile(k)], xh[p][:, k:k + L],
                                 xl[p][:, k:k + L], k == 0, k == TAPS - 1)
                i.then_inc(done, 1)

            def segments(s):
                now(pe, r0_ready, s)
                before(pe, gm_ready, s)
                pe.matmul(PSEG[0][:, :], R["after"], Rg[0][:, :, :].rearrange("p c l -> p (c l)"), start=True, stop=True)\
                    .then_inc(seg0_ready, 1)
                now(pe, r1_ready, s)
                if not isinstance(s, int) or s > 0:
                    before(pe, yT_ready, s - 1)
                pe.matmul(PSEG[1][:, :], R["after"], Rg[1][:, :, :].rearrange("p c l -> p (c l)"), start=True, stop=True)\
                    .then_inc(seg1_ready, 1)

            def states_turn(s):
                now(pe, state_ready, s)
                now(pe, m1_ready, s)
                settle(pe, R["settled"])
                four(lambda t: PSTT[0:NC, tile(t)],
                     lambda t: state[:, t * BLOCKS:(t + 1) * BLOCKS, :].rearrange("p c n -> p (c n)"),
                     R["ident"], stt_ready)

            def states_out(s):
                now(pe, states_copied, s)
                now(pe, cm_ready, s)
                for t in range(SEQ_TILES):
                    i = pe.matmul(PYO[:, tile(t)], Cm[:, tile(t)], STs[:, tile(t)], start=True, stop=True)
                i.then_inc(yoff_ready, 1)

            def y_turn(s):
                now(pe, yz_ready, s)
                four(lambda t: PYT[:, tile(t)], lambda t: y[:, tile(t)], R["ident"], yt_ready)

            def output(s):
                now(pe, yT_ready, s)
                for t in range(SEQ_TILES):
                    at_col = (t % 2) * 2 * D + HALF
                    i = pe.matmul(PZ[t // 2][:, at_col:at_col + D], yT[:, tile(t)], R["wo_y"][:, :], start=False, stop=True,
                                  skip_group_check=True)
                i.then_inc(o_ready, 1)

            def z_and_output(s, p):
                before(pe, x_done, s)
                for t in range(SEQ_TILES):
                    tt = slice(PAD + t * P, PAD + (t + 1) * P)
                    out = PZ[t // 2][:, (t % 2) * 2 * D:(t % 2 + 1) * 2 * D]
                    pe.matmul(out, xh[p][:, tt], R["wz_hi"][:, :], start=(t % 2 == 0), stop=False, skip_group_check=True)
                    pe.matmul(out, xh[p][:, tt], R["wz_lo"][:, :], start=False, stop=False, skip_group_check=True)
                    i = pe.matmul(out, xl[p][:, tt], R["wz_hi"][:, :], start=False, stop=True, skip_group_check=True)
                i.then_inc(z_ready, 1)

            x_turn(0, 0)
            times(0, 0)
            sums(0)
            totals(0)

            def step(s, p, first, last):
                if not first:
                    states_turn(s - 1)
                if not last:
                    x_turn(s + 1, 1 - p)
                segments(s)
                if not first:
                    states_out(s - 1)
                if not last:
                    times(s + 1, 1 - p)
                conv(PX[:, :], "wx", p, x_ready)
                if not first:
                    now(pe, e1_ready, s)
                    y_turn(s - 1)
                before(pe, yo_ready, s)
                conv(PBC[:, :], "wbc", p, bc_ready)
                if not first:
                    output(s - 1)
                now(pe, xc_ready, s)
                now(pe, e0_ready, s)
                four(lambda t: PXCT[:, tile(t)], lambda t: xc[:, tile(t)], R["ident"], xt_ready)
                if not last:
                    sums(s + 1)
                now(pe, cb_ready, s)
                settle(pe, R["settled"])
                four(lambda t: PBT[:, BT0 + t * STATE:BT0 + (t + 1) * STATE], lambda t: Bc[:, tile(t)],
                     R["ident"][0:STATE, 0:STATE], bt_ready)
                now(pe, xdt_ready, s)
                for t in range(SEQ_TILES):
                    i = pe.matmul(PG[:, tile(t)], Bc[:, tile(t)], Cc[0:STATE, tile(t)], start=True, stop=True)
                i.then_inc(g_ready, 1)
                if not last:
                    totals(s + 1)
                z_and_output(s, p)
                before(pe, yz_ready, s)
                for t in range(SEQ_TILES):
                    pe.matmul(PY[:, tile(t)], xc[:, tile(t)], R["skip"][:, :], start=(t == 0), stop=False,
                              skip_group_check=True)
                now(pe, gm_ready, s)
                for c in range(BLOCKS):
                    i = pe.matmul(PGR[:, tile(c)], R["spread"], Gm[:, :, c * CHUNK:(c + 1) * CHUNK], start=True, stop=True)
                i.then_inc(g_spread, 1)
                now(pe, xdec_ready, s)
                now(pe, bm_ready, s)
                for t in range(SEQ_TILES):
                    out = PST[:, 0:STATE * CHUNKS].rearrange("p (n c) -> p c n", c=CHUNKS)[:, t * BLOCKS:(t + 1) * BLOCKS, :]
                    i = pe.matmul(out, xdec[:, tile(t)], Bm[:, t, :, :], start=True, stop=True)
                i.then_inc(st_ready, 1)
                now(pe, xb_dve, s)
                now(pe, xb_act, s)
                for g, m in ((0, m0_ready), (1, m1_ready)):
                    now(pe, m, s)
                    for t in range(SEQ_TILES):
                        for c in range(BLOCKS):
                            at_col = t * P + g * BLOCKS * HDIM
                            i = pe.matmul(PY[c * CHUNK:(c + 1) * CHUNK, at_col:at_col + BLOCKS * HDIM],
                                          Mg[g][:, c, t, :], XB[:, t, c, g, :], start=False, stop=True,
                                          skip_group_check=True)
                i.then_inc(y_ready, 1)
            run_steps(pe, step)
            states_turn(B - 1)
            states_out(B - 1)
            y_turn(B - 1)
            output(B - 1)


def program(nc, ins, out):
    with ExitStack() as ctx:
        R = {}
        out_dram = out.rearrange("b (t p) d -> b p t d", p=P)
        R["out_dram"] = [out_dram[s] for s in range(B)]
        setup(nc, R, ins, ctx)
        mamba_setup(nc, R, ins, ctx)
        ffn_phase(nc, "ffn1", R, True, False)
        mamba_phase(nc, R)
        ffn_phase(nc, "ffn2", R, False, True)


def kernel(**inputs):
    import numpy as np
    import concourse.bacc as bacc
    from concourse.bass_utils import run_bass_kernel_spmd

    nc = bacc.Bacc("TRN2", target_bir_lowering=False, num_devices=1)
    arrays = {name: np.ascontiguousarray(a) for name, a in inputs.items()}
    arrays["constants"] = constants()
    ins = {name: nc.dram_tensor(name, a.shape, mybir.dt.from_np(a.dtype), kind="ExternalInput").ap()
           for name, a in arrays.items()}
    out = nc.dram_tensor("out", (B, L, D), F32, kind="ExternalOutput").ap()
    program(nc, ins, out)
    return run_bass_kernel_spmd(nc, [arrays], core_ids=[0]).results[0]["out"]
```

```python
import concourse.bass as bass
from concourse import mybir
from contextlib import ExitStack

F32 = mybir.dt.float32
F32R = mybir.dt.float32r
BF16 = mybir.dt.bfloat16
ALU = mybir.AluOpType
ACT = mybir.ActivationFunctionType
AX = mybir.AxisListType

P = 128
B, L, D = 8, 512, 128
SEQ_TILES = L // P
TILES = B * SEQ_TILES
E, H, SHARED, TOP = 8, 64, 2, 2
PAIRS = (E + SHARED) // 2
EPS = 1e-5

HEADS, HDIM, STATE, TAPS = 8, 16, 16, 4
CHUNK = 32
BLOCKS = P // CHUNK
CHUNKS = L // CHUNK
HALF = HEADS * HDIM
HGROUPS = HEADS // BLOCKS
GATE_ROWS = TOP * 2 * E
ARTANH = [1.0 / (2 * k + 1) for k in range(8)]


class Own:

    def __init__(self, engine, sem, base, most):
        self.engine, self.sem, self.base, self.most, self.n = engine, sem, base, most, 0

    def mark(self, instruction):
        self.n += 1
        instruction.then_inc(self.sem, 1)

    def ready(self):
        if self.n:
            self.engine.wait_ge(self.sem, self.base + self.n)

    def link(self, instruction):
        self.mark(instruction)
        self.ready()

    def close(self):
        assert self.n == self.most, self.n


def settle(engine, sem):
    engine.sem_inc(sem, 1)


def split_mm(pe, out, w_hi, w_lo, x_hi, x_lo, start, stop):
    pe.matmul(out, w_hi, x_hi, start=start, stop=False)
    pe.matmul(out, w_hi, x_lo, start=False, stop=False)
    return pe.matmul(out, w_lo, x_hi, start=False, stop=stop)


def run_steps(engine, step):
    step(0, 0, True, False)
    with engine.Fori(0, B // 2 - 1) as k:
        step(k * 2 + 1, 1, False, False)
        step(k * 2 + 2, 0, False, False)
    step(B - 1, 1, False, True)


class Norm:

    def __init__(self, nc, R, ctx, tag):
        def sb(name, shape):
            return [ctx.enter_context(nc.sbuf_tensor(f"{tag}_{name}{p}", shape, F32)) for p in range(2)]

        self.X, self.mhalf, self.settled = R["X"], R["mhalf"], R["settled"]
        self.stats_of = ctx.enter_context(nc.sbuf_tensor(f"{tag}_stats", [P, SEQ_TILES, 6], F32))
        self.mv, self.ve, self.rstd, self.xn = (sb("mv", [P, SEQ_TILES, 2]), sb("ve", [P, SEQ_TILES]),
                                                sb("rstd", [P, SEQ_TILES]), sb("xn", [P, SEQ_TILES, D]))
        self.own, self.ve_ready, self.rstd_ready, self.xn_ready = (
            ctx.enter_context(nc.semaphore(f"{tag}_{n}")) for n in ("norm_own", "ve_ready", "rstd_ready", "xn_ready"))

    def x(self, s, t):
        return self.X[:, bass.ds(s * SEQ_TILES + t, 1), :]

    def stats(self, dve, s):
        for t in range(SEQ_TILES):
            i = dve.bn_stats(self.stats_of[:, t, :], self.x(s, t))
        i.then_inc(self.own, 1)

    def moments(self, dve, s, p, tiles=range(SEQ_TILES)):
        for t in tiles:
            if t == 0:
                dve.wait_ge(self.own, s * 2 + 1)
                settle(dve, self.settled)
            i = dve.bn_aggr(self.mv[p][:, t, :], self.stats_of[:, t, :])
            if t == SEQ_TILES - 1:
                i.then_inc(self.own, 1)

    def variance(self, dve, s, p):
        dve.wait_ge(self.own, s * 2 + 2)
        dve.tensor_scalar(self.ve[p][:, :], self.mv[p][:, :, 1], EPS, None, ALU.add).then_inc(self.ve_ready, 1)

    def power(self, pool, s, p):
        pool.wait_ge(self.ve_ready, s + 1)
        pool.tensor_tensor(self.rstd[p][:, :], self.ve[p][:, :], self.mhalf, ALU.pow).then_inc(self.rstd_ready, 1)

    def apply(self, dve, s, p, tiles=range(SEQ_TILES)):
        for t in tiles:
            if t == 0:
                dve.wait_ge(self.rstd_ready, s + 1)
            i = dve.tensor_scalar(self.xn[p][:, t:t + 1, :], self.x(s, t), self.mv[p][:, t, 0:1],
                                  self.rstd[p][:, t:t + 1], ALU.subtract, ALU.mult)
            if t == SEQ_TILES - 1:
                i.then_inc(self.xn_ready, 1)

    def first_moments(self, dve):
        for s in range(2):
            self.stats(dve, s)
            self.moments(dve, s, s)
            self.variance(dve, s, s)

    def first_apply(self, dve):
        for s in range(2):
            self.apply(dve, s, s)


def over_experts(a):
    return a.rearrange("p (t o) -> p t o", o=1).to_broadcast([P, SEQ_TILES, E])

def over_tiles(a):
    return a.rearrange("p (o e) -> p o e", o=1).to_broadcast([P, SEQ_TILES, E])


class Gates:

    OPS = 18

    def __init__(self, routing, dve, s, p, bank):
        self.r, self.dve, self.s, self.p, self.bank = routing, dve, s, p, bank
        self.own = Own(dve, routing.gate_own, s * self.OPS, self.OPS)

    def chain(self, instruction_of):
        self.own.ready()
        self.own.mark(instruction_of())

    def logits(self):
        self.dve.wait_ge(self.r.logits_ready, self.s + 1)
        v = self.bank[:, 0:SEQ_TILES * 2 * E].rearrange("p (t k e) -> p t k e", k=2, e=E)
        self.chain(lambda: self.dve.tensor_tensor(self.r.biased[:, :, :], v[:, :, 0, :], over_tiles(self.r.R["router_b"][:, :]), ALU.add))
        self.chain(lambda: self.dve.tensor_tensor(self.r.lg[0][:, :, :], v[:, :, 1, :], self.r.biased[:, :, :], ALU.add))

    def largest(self, k):
        self.chain(lambda: self.dve.tensor_reduce(self.r.top[:, k, :], self.r.lg[k][:, :, :], AX.X, ALU.max))

    def equal(self, k):
        self.chain(lambda: self.dve.tensor_tensor(self.r.eq[:, :, :], self.r.lg[k][:, :, :], over_experts(self.r.top[:, k, :]), ALU.is_equal))

    def order(self):
        self.chain(lambda: self.dve.tensor_tensor(self.r.key[:, :, :], self.r.eq[:, :, :], over_tiles(self.r.R["order"]), ALU.mult))

    def first_of(self):
        self.chain(lambda: self.dve.tensor_reduce(self.r.km[:, :], self.r.key[:, :, :], AX.X, ALU.max))

    def mark(self, k):
        self.chain(lambda: self.dve.tensor_tensor(self.r.one[:, :, k, :], self.r.key[:, :, :], over_experts(self.r.km[:, :]), ALU.is_equal))

    def remove(self):
        self.chain(lambda: self.dve.scalar_tensor_tensor(self.r.lg[1][:, :, :], self.r.one[:, :, 0, :], -3.0e38, self.r.lg[0][:, :, :],
                                                    ALU.mult, ALU.add))

    def distance(self):
        self.own.ready()
        self.dve.tensor_tensor(self.r.dm[:, :], self.r.top[:, 1, :], self.r.top[:, 0, :], ALU.subtract).then_inc(self.r.dm_ready, 1)

    def denominator(self):
        self.dve.wait_ge(self.r.ed_ready, self.s + 1)
        self.chain(lambda: self.dve.tensor_scalar(self.r.den[:, :], self.r.ed[:, :], 1.0, None, ALU.add))

    def weights(self):
        self.chain(lambda: self.dve.reciprocal(self.r.gk[:, :, 0], self.r.den[:, :]))
        self.chain(lambda: self.dve.tensor_tensor(self.r.gk[:, :, 1], self.r.ed[:, :], self.r.gk[:, :, 0], ALU.mult))

    def parts(self):
        self.chain(lambda: self.dve.tensor_copy(self.r.gparts[:, :, :, 0], self.r.gk[:, :, :]))
        self.chain(lambda: self.dve.tensor_tensor(self.r.gparts[:, :, :, 1], self.r.gk[:, :, :], self.r.gparts[:, :, :, 0], ALU.subtract))

    def place(self):
        self.own.ready()
        N = SEQ_TILES * TOP
        self.dve.tensor_tensor(self.r.spots[self.p][:, :, :].rearrange("p t (k w e) -> p (t k) w e", w=2, e=E),
                          self.r.one[:, :, :, :].rearrange("p t k (o e) -> p (t k) o e", o=1).to_broadcast([P, N, 2, E]),
                          self.r.gparts[:, :, :, :].rearrange("p t k (w o) -> p (t k) w o", o=1).to_broadcast([P, N, 2, E]),
                          ALU.mult).then_inc(self.r.spots_ready, 1)
        self.own.close()


class Routing:

    def __init__(self, nc, R, ctx, tag, norm):
        def sb(name, shape, dt=F32):
            return ctx.enter_context(nc.sbuf_tensor(f"{tag}_{name}", shape, dt))

        self.R, self.norm = R, norm
        self.xh = [sb(f"xh{p}", [P, L], F32R) for p in range(2)]
        self.xl = [sb(f"xl{p}", [P, L], F32R) for p in range(2)]
        self.biased, self.eq = sb("biased", [P, SEQ_TILES, E]), sb("eq", [P, SEQ_TILES, E])
        self.key = sb("key", [P, SEQ_TILES, E])
        self.lg = [sb(f"lg{k}", [P, SEQ_TILES, E]) for k in range(TOP)]
        self.one = sb("one", [P, SEQ_TILES, TOP, E])
        self.top, self.km = sb("top", [P, TOP, SEQ_TILES]), sb("km", [P, SEQ_TILES])
        self.dm, self.ed, self.den = sb("dm", [P, SEQ_TILES]), sb("ed", [P, SEQ_TILES]), sb("den", [P, SEQ_TILES])
        self.gk = sb("gk", [P, SEQ_TILES, TOP])
        self.gparts = sb("gparts", [P, SEQ_TILES, TOP, 2], F32R)
        self.spots = [sb(f"spots{p}", [P, SEQ_TILES, GATE_ROWS]) for p in range(2)]
        (self.xT_ready, self.xh_ready, self.xl_ready, self.logits_ready, self.dm_ready, self.ed_ready, self.spots_ready,
         self.gate_own) = (ctx.enter_context(nc.semaphore(f"{tag}_{n}")) for n in (
             "xT_ready", "xh_ready", "xl_ready", "logits_ready", "dm_ready", "ed_ready", "spots_ready", "gate_own"))

    def x_turn(self, pe, s, p, bank):
        pe.wait_ge(self.norm.xn_ready, s + 1)
        for t in range(SEQ_TILES):
            i = pe.transpose(bank[:, t * P:(t + 1) * P], self.norm.xn[p][:, t, :], self.R["ident"])
        i.then_inc(self.xT_ready, 1)

    def x_high(self, act, s, p, bank):
        act.wait_ge(self.xT_ready, s + 1)
        act.activation(self.xh[p][:, :], bank[:, :], ACT.Copy).then_inc(self.xh_ready, 1)

    def x_low(self, dve, s, p, bank):
        dve.wait_ge(self.xh_ready, s + 1)
        dve.tensor_tensor(self.xl[p][:, :], bank[:, :], self.xh[p][:, :], ALU.subtract).then_inc(self.xl_ready, 1)

    def router(self, pe, s, p, bank):
        pe.wait_ge(self.xl_ready, s + 1)
        for t in range(SEQ_TILES):
            tile = slice(t * P, (t + 1) * P)
            out = bank[:, t * 2 * E:(t + 1) * 2 * E]
            pe.matmul(out, self.xh[p][:, tile], self.R["rw_parts"][:, :], start=(t == 0), stop=False, skip_group_check=True)
            i = pe.matmul(out, self.xl[p][:, tile], self.R["rw_parts"][:, :], start=False, stop=True, skip_group_check=True)
        i.then_inc(self.logits_ready, 1)

    def softmax_power(self, pool, s):
        pool.wait_ge(self.dm_ready, s + 1)
        pool.tensor_tensor(self.ed[:, :], self.R["euler"], self.dm[:, :], ALU.pow).then_inc(self.ed_ready, 1)


def ffn_phase(nc, tag, R, norm, routing, next_norm, loading, weights, signals, out_dram):
    X, ident = R["X"], R["ident"]
    with ExitStack() as ctx:
        def sb(name, shape, dt=F32):
            return ctx.enter_context(nc.sbuf_tensor(f"{tag}_{name}", shape, dt))

        def sem(name):
            return R["all_phases"].enter_context(nc.semaphore(f"{tag}_{name}"))

        gT = [sb(f"gT{p}", [GATE_ROWS, L], F32R) for p in range(2)]
        sil = [sb(f"sil{b}", [P, L]) for b in range(2)]
        pr = [sb(f"pr{b}", [P, L]) for b in range(2)]
        h = [sb(f"h{c}", [P, L]) for c in range(PAIRS)]
        hh = [sb(f"hh{c}", [P, L], F32R) for c in range(PAIRS)]
        hl = [sb(f"hl{c}", [P, L], F32R) for c in range(PAIRS)]
        oT = sb("oT", [P, L])

        PT, PS, PB, PD = R["bank"][0:4]
        PG = [R["bank"][4], R["bank"][6]]
        PU = [R["bank"][5], R["bank"][7]]

        spots_ready = routing.spots_ready
        xh, xl, spots = routing.xh, routing.xl, routing.spots
        gTp_ready, gT_ready = sem("gTp_ready"), sem("gT_ready")
        up_ready, sil_ready, prod_ready = sem("up_ready"), sem("sil_ready"), sem("prod_ready")
        bc_ready, h_ready, hh_ready, hl_ready = sem("bc_ready"), sem("h_ready"), sem("hh_ready"), sem("hl_ready")
        down_done, oT_ready, back_ready, x_done = sem("down_done"), sem("oT_ready"), sem("back_ready"), sem("x_done")
        stored = sem("stored")
        ROUTED = PAIRS - 1
        CREDIT = {prod_ready: 2, hl_ready: PAIRS, down_done: PAIRS, oT_ready: 1, back_ready: 1, x_done: 1}

        def chunk(s, c):
            return s * PAIRS + c

        def buf(p, c):
            return (p * PAIRS + c) % 2

        def hidden_written(engine, s, c):
            if c == 0:
                engine.wait_ge(prod_ready, chunk(s, 0) + 1 + CREDIT[prod_ready])
            else:
                engine.wait_ge(h_ready, s * ROUTED + c)

        block = ctx.enter_context(nc.Block())

        @block.sync
        def _(sp):
            if loading:
                loading.sync(sp)
                weights.sync(sp)
            if out_dram is not None:
                for s in range(B):
                    sp.wait_ge(x_done, s + 1 + CREDIT[x_done])
                    sp.dma_start(out_dram[s], X[:, s * SEQ_TILES:(s + 1) * SEQ_TILES, :])\
                        .then_inc(stored, 16)
                sp.wait_ge(stored, 16 * B)

        @block.gpsimd
        def _(pool):
            def low_part(s, c):
                pool.wait_ge(hh_ready, chunk(s, c) + 1)
                pool.tensor_tensor(hl[c][:, :], h[c][:, :], hh[c][:, :], ALU.subtract).then_inc(hl_ready, 1)

            pool.sem_inc(hl_ready, CREDIT[hl_ready])
            if signals:
                signals.start(pool, signals.gpsimd)
            if loading:
                pool.wait_ge(loading.core_in, 16)
                norm.power(pool, 0, 0)
                loading.pool_router(pool)
                norm.power(pool, 1, 1)
                routing.softmax_power(pool, 0)
                loading.pool_down(pool)

            def step(s, p, first, last):
                if not first:
                    low_part(s - 1, 4)
                low_part(s, 0)
                if not last:
                    norm.power(pool, s + 2, p)
                low_part(s, 1)
                if last and next_norm:
                    next_norm.power(pool, 0, 0)
                low_part(s, 2)
                if not last:
                    routing.softmax_power(pool, s + 1)
                if last and next_norm:
                    next_norm.power(pool, 1, 1)
                low_part(s, 3)
            run_steps(pool, step)

        @block.scalar
        def _(act):
            def gates_out(s, p):
                act.wait_ge(gTp_ready, s + 1)
                act.activation(gT[p][:, :], PB[0:GATE_ROWS, :], ACT.Copy).then_inc(gT_ready, 1)

            def silu(s, p, c):
                n, b = chunk(s, c), buf(p, c)
                act.wait_ge(up_ready, n + 1)
                act.wait_ge(prod_ready, n - 1 + CREDIT[prod_ready])
                act.activation(sil[b][:, :], PG[b][:, :], ACT.Silu).then_inc(sil_ready, 1)

            def high_part(s, c):
                hidden_written(act, s, c)
                act.wait_ge(down_done, chunk(s, c) + 1 - PAIRS + CREDIT[down_done])
                act.activation(hh[c][:, :], h[c][:, :], ACT.Copy).then_inc(hh_ready, 1)

            def out_copy(s):
                act.wait_ge(down_done, chunk(s, PAIRS) + CREDIT[down_done])
                act.wait_ge(back_ready, s + CREDIT[back_ready])
                act.activation(oT[:, :], PD[:, :], ACT.Copy).then_inc(oT_ready, 1)

            act.sem_inc(oT_ready, CREDIT[oT_ready])
            if loading:
                loading.scalar_loads(act)
                signals.start(act, signals.scalar)
                loading.scalar_router(act)
                loading.scalar_gate(act)
                routing.x_high(act, 0, 0, PT)
                loading.scalar_weights(act)

            def step(s, p, first, last):
                gates_late = first and loading
                silu(s, p, 0)
                if not last:
                    routing.x_high(act, s + 1, 1 - p, PT)
                if not first:
                    high_part(s - 1, 4)
                if not gates_late:
                    gates_out(s, p)
                silu(s, p, 1)
                if gates_late:
                    gates_out(s, p)
                high_part(s, 0)
                silu(s, p, 2)
                high_part(s, 1)
                if not first:
                    out_copy(s - 1)
                silu(s, p, 3)
                high_part(s, 2)
                silu(s, p, 4)
                high_part(s, 3)
            run_steps(act, step)
            high_part(B - 1, 4)
            out_copy(B - 1)

        @block.vector
        def _(dve):
            def product(s, p, c):
                n, b = chunk(s, c), buf(p, c)
                dve.wait_ge(sil_ready, n + 1)
                if c == 0:
                    dve.wait_ge(hl_ready, n + 1 - PAIRS + CREDIT[hl_ready])
                out = h[0] if c == 0 else pr[b]
                dve.tensor_tensor(out[:, :], sil[b][:, :], PU[b][:, :], ALU.mult).then_inc(prod_ready, 1)

            def gated(s, p, c):
                n, b = chunk(s, c), buf(p, c)
                dve.wait_ge(prod_ready, n + 1 + CREDIT[prod_ready])
                dve.wait_ge(bc_ready, s * ROUTED + c)
                dve.wait_ge(hl_ready, n + 1 - PAIRS + CREDIT[hl_ready])
                dve.tensor_tensor(h[c][:, :], pr[b][:, :], PB[:, :], ALU.mult).then_inc(h_ready, 1)

            def residual(s):
                dve.wait_ge(back_ready, s + 1 + CREDIT[back_ready])
                seq = X[:, bass.ds(s * SEQ_TILES, SEQ_TILES), :]
                dve.tensor_tensor(seq, seq, PT[:, :].rearrange("p (t d) -> p t d", d=D), ALU.add).then_inc(x_done, 1)

            for one_sem in (prod_ready, x_done):
                dve.sem_inc(one_sem, CREDIT[one_sem])
            if loading:
                dve.memset(X[:, TILES:, :], 0.0)
                weights.clear(dve)
                signals.start(dve, signals.vector)
                for s in range(2):
                    dve.wait_ge(loading.x_loaded[s], 16)
                    norm.stats(dve, s)
                    norm.moments(dve, s, s)
                    norm.variance(dve, s, s)
                    if s == 0:
                        norm.apply(dve, 0, 0)
                routing.x_low(dve, 0, 0, PT)
                loading.vector_up(dve, 0)
                loading.vector_up(dve, 1)
                dve.wait_ge(loading.core_in, 16)
                dve.wait_ge(loading.router_in, 32)
                g = Gates(routing, dve, 0, 0, PS)
                g.logits()
                g.largest(0)
                norm.apply(dve, 1, 1, [0])
                g.equal(0)
                norm.apply(dve, 1, 1, [1])
                g.order()
                norm.apply(dve, 1, 1, [2])
                g.first_of()
                norm.apply(dve, 1, 1, [3])
                g.mark(0)
                g.remove()
                g.largest(1)
                g.distance()
                g.equal(1)
                g.order()
                g.first_of()
                g.mark(1)
                g.denominator()
                g.weights()
                g.parts()
                g.place()
                dve.wait_ge(loading.x_loaded[2], 16 * (B - 2))
            else:
                g = routing.begun
                g.denominator()
                g.weights()
                g.parts()
                g.place()

            def step(s, p, first, last):
                if last:
                    ahead = next_norm is not None
                    product(s, p, 0)
                    if ahead:
                        next_norm.stats(dve, 0)
                    product(s, p, 1)
                    if ahead:
                        next_norm.moments(dve, 0, 0)
                    gated(s, p, 1)
                    if ahead:
                        next_norm.variance(dve, 0, 0)
                        next_norm.stats(dve, 1)
                    product(s, p, 2)
                    if ahead:
                        next_norm.moments(dve, 1, 1)
                    gated(s, p, 2)
                    if ahead:
                        next_norm.variance(dve, 1, 1)
                    product(s, p, 3)
                    residual(s - 1)
                    gated(s, p, 3)
                    product(s, p, 4)
                    gated(s, p, 4)
                    if ahead:
                        next_norm.first_apply(dve)
                    return
                g = Gates(routing, dve, s + 1, 1 - p, PS)
                product(s, p, 0)
                norm.stats(dve, s + 2)
                routing.x_low(dve, s + 1, 1 - p, PT)
                norm.moments(dve, s + 2, p)
                product(s, p, 1)
                norm.variance(dve, s + 2, p)
                gated(s, p, 1)
                g.logits()
                product(s, p, 2)
                g.largest(0)
                norm.apply(dve, s + 2, p, [0])
                g.equal(0)
                norm.apply(dve, s + 2, p, [1])
                g.order()
                gated(s, p, 2)
                g.first_of()
                norm.apply(dve, s + 2, p, [2])
                g.mark(0)
                norm.apply(dve, s + 2, p, [3])
                g.remove()
                product(s, p, 3)
                g.largest(1)
                if not first:
                    residual(s - 1)
                g.equal(1)
                gated(s, p, 3)
                g.distance()
                g.order()
                g.first_of()
                g.mark(1)
                product(s, p, 4)
                g.denominator()
                g.weights()
                gated(s, p, 4)
                g.parts()
                g.place()
                if first and weights:
                    weights.taps(dve)
            run_steps(dve, step)
            dve.wait_ge(hh_ready, chunk(B - 1, 4) + 1)
            dve.wait_ge(hl_ready, chunk(B - 1, 4) + CREDIT[hl_ready])
            dve.tensor_tensor(hl[4][:, :], h[4][:, :], hh[4][:, :], ALU.subtract).then_inc(hl_ready, 1)
            residual(B - 1)

        @block.tensor
        def _(pe):
            def four(out, src, done):
                for t in range(SEQ_TILES):
                    i = pe.transpose(out(slice(t * P, (t + 1) * P)), src(t), ident)
                i.then_inc(done, 1)

            def gates_turn(s, p):
                pe.wait_ge(spots_ready, s + 1)
                four(lambda cols: PB[0:GATE_ROWS, cols], lambda t: spots[p][:, t, :], gTp_ready)

            def up(s, p, c):
                n, b = chunk(s, c), buf(p, c)
                pe.wait_ge(prod_ready, n - 1 + CREDIT[prod_ready])
                cols = slice(c * P, (c + 1) * P)
                split_mm(pe, PG[b][:, :], R["wg_hi"][:, cols], R["wg_lo"][:, cols], xh[p][:, :], xl[p][:, :], True, True)
                split_mm(pe, PU[b][:, :], R["wu_hi"][:, cols], R["wu_lo"][:, cols], xh[p][:, :], xl[p][:, :], True, True)\
                    .then_inc(up_ready, 1)

            def gates_spread(s, p, c):
                if c == 1:
                    pe.wait_ge(gT_ready, s + 1)
                else:
                    pe.wait_ge(h_ready, s * ROUTED + c - 1)
                pe.matmul(PB[:, :], R["spread_gates"][:, (c - 1) * P:c * P], gT[p][:, :], start=True, stop=True)\
                    .then_inc(bc_ready, 1)

            def down(s, c):
                pe.wait_ge(hl_ready, chunk(s, c) + 1 + CREDIT[hl_ready])
                if c == 0:
                    pe.wait_ge(oT_ready, s + CREDIT[oT_ready])
                cols = slice(c * P, (c + 1) * P)
                split_mm(pe, PD[:, :], R["wd_hi"][:, cols], R["wd_lo"][:, cols], hh[c][:, :], hl[c][:, :],
                         c == 0, c == PAIRS - 1).then_inc(down_done, 1)

            def back(s):
                pe.wait_ge(oT_ready, s + 1 + CREDIT[oT_ready])
                four(lambda cols: PT[:, cols], lambda t: oT[:, t * P:(t + 1) * P], back_ready)

            for one_sem in (down_done, back_ready):
                pe.sem_inc(one_sem, CREDIT[one_sem])
            if loading:
                signals.start(pe, signals.tensor)
                pe.wait_ge(loading.core_in, 16)
                routing.x_turn(pe, 0, 0, PT)
                pe.wait_ge(loading.router_split, 1)
                routing.router(pe, 0, 0, PS)
                pe.wait_ge(loading.up_split, 2)

            def step(s, p, first, last):
                gates_late = first and loading
                up(s, p, 0)
                if not last:
                    if not first:
                        pe.wait_ge(x_done, s - 1 + CREDIT[x_done])
                    routing.x_turn(pe, s + 1, 1 - p, PT)
                if not first:
                    down(s - 1, 2)
                if not gates_late:
                    gates_turn(s, p)
                up(s, p, 1)
                if gates_late:
                    gates_turn(s, p)
                if first and loading:
                    pe.wait_ge(loading.gates_spreader, 1)
                    pe.wait_ge(loading.down_split, 1)
                gates_spread(s, p, 1)
                if not first:
                    down(s - 1, 3)
                up(s, p, 2)
                if not last:
                    routing.router(pe, s + 1, 1 - p, PS)
                if not first:
                    down(s - 1, 4)
                gates_spread(s, p, 2)
                up(s, p, 3)
                if not first:
                    back(s - 1)
                down(s, 0)
                gates_spread(s, p, 3)
                up(s, p, 4)
                down(s, 1)
                gates_spread(s, p, 4)
            run_steps(pe, step)
            for c in (2, 3, 4):
                down(B - 1, c)
            back(B - 1)


CONSTANTS = {}
CORE = ("ident", "mhalf", "euler", "order", "sel")
CORE_COLUMNS = P + 2 * SEQ_TILES + E
SEL_COLUMNS = CORE_COLUMNS + E * H


def constants():
    import numpy as np
    row = np.arange(P)
    made = {"ident": np.eye(P),
            "mhalf": np.full((P, SEQ_TILES), -0.5),
            "euler": np.full((P, SEQ_TILES), np.exp(1.0)),
            "order": np.tile(E - np.arange(E), (P, 1)),
            "sel": np.kron((row[:, None] % E == np.arange(E)) & (row[:, None] < 4 * E), np.ones((1, H)))}
    block, inner = row // CHUNK, row % CHUNK
    same = block[:, None] == block
    made |= {
        "upto": same & (inner[:, None] <= inner),
        "after": same & (inner[:, None] > inner),
        "spread": inner[:, None] == inner,
        "spread_one": np.concatenate([(inner[:, None] == inner) & (block[:, None] == c) for c in range(BLOCKS)], axis=1),
        "own_block": block[:, None] == np.arange(BLOCKS),
        "causal": inner[:, None] <= np.arange(CHUNK),
        "causal_block": same & (inner[:, None] <= inner),
        "own_tile": np.kron(row[:, None] // HEADS == np.arange(SEQ_TILES), np.ones((1, BLOCKS))),
        "own_head": row[:, None] % HEADS == row // HDIM,
        "own_chunk": row[:, None] // STATE == block,
        "head_of": row[:, None] // HDIM == np.arange(HEADS)}
    at = 0
    assert tuple(made)[:len(CORE)] == CORE
    for name, a in made.items():
        CONSTANTS[name] = (at, a.shape[1])
        at += a.shape[1]
    return np.ascontiguousarray(np.concatenate([a.astype(np.float32) for a in made.values()], axis=1))


def allocate(nc, R, ins, ctx):
    def sb(name, shape, dt=F32):
        return ctx.enter_context(nc.sbuf_tensor(name, shape, dt))

    NU = PAIRS * P
    R["settled"] = ctx.enter_context(nc.semaphore("settled"))
    R["X"] = sb("X", [P, TILES + SEQ_TILES, D])
    R["const"] = sb("const", [P, ins["constants"].shape[1]])
    for name, (at, n) in CONSTANTS.items():
        R[name] = R["const"][:, at:at + n]
    for name, shape, dt in (("router_b", [P, E], F32), ("spread_gates", [4 * E, E * H], F32R),
                            ("rw", [P, E], F32), ("rw_parts", [P, 2 * E], F32R),
                            ("wg_hi", [P, NU], F32R), ("wg_lo", [P, NU], F32R), ("wu_hi", [P, NU], F32R),
                            ("wu_lo", [P, NU], F32R), ("wd_hi", [P, NU], F32R), ("wd_lo", [P, NU], F32R)):
        R[name] = sb(name, shape, dt)
    R["bank"] = [ctx.enter_context(nc.psum_tensor(f"bank{k}", [P, 512], F32)) for k in range(8)]


class Loading:

    def __init__(self, nc, R, ins, ctx):
        NU = PAIRS * P
        self.R, self.ins = R, ins
        self.wg, self.wu, self.wd, self.wd_half = (
            ctx.enter_context(nc.sbuf_tensor(f"{n}_in", [P, NU], F32)) for n in ("wg", "wu", "wd", "wd_half"))
        (self.core_in, self.const_in, self.router_in, self.wg_in, self.wu_in, self.wd_in, self.hi_ready, self.halved,
         self.router_split, self.up_split, self.down_split, self.gates_spreader, self.router_high) = (
            ctx.enter_context(nc.semaphore(n)) for n in (
                "core_in", "const_in", "router_in", "wg_in", "wu_in", "wd_in", "hi_ready", "halved", "router_split",
                "up_split", "down_split", "gates_spreader", "router_high"))
        self.x_loaded = [ctx.enter_context(nc.semaphore(f"x_loaded{s}")) for s in range(3)]
        self.x_dram = ins["L0_attn_u"].rearrange("b (t p) d -> b p t d", p=P)

    def load_x(self, sp, s):
        sp.dma_start(self.R["X"][:, s * SEQ_TILES:(s + 1) * SEQ_TILES, :], self.x_dram[s]).then_inc(self.x_loaded[min(s, 2)], 16)

    def sync(self, sp):
        self.load_x(sp, 0)
        for w, which, loaded in ((self.wg, "w1", self.wg_in), (self.wu, "w3", self.wu_in)):
            if w is self.wu:
                self.load_x(sp, 1)
            v = w[:, :].rearrange("p (e h) -> p e h", h=H)
            sp.dma_start(v[:, 0:SHARED, :], self.ins[f"L0_ffn_shared_{which}"].rearrange("e d h -> d e h")).then_inc(loaded, 16)
            sp.dma_start(v[:, SHARED:, :], self.ins[f"L0_ffn_routed_{which}"].rearrange("e d h -> d e h")).then_inc(loaded, 16)
        for s in range(2, B):
            self.load_x(sp, s)

    def scalar_loads(self, act):
        R, ins = self.R, self.ins
        act.dma_start(R["rw"][:, :], ins["L0_ffn_router_w"]).then_inc(self.router_in, 16)
        act.dma_start(R["const"][:, 0:CORE_COLUMNS], ins["constants"][:, 0:CORE_COLUMNS]).then_inc(self.core_in, 16)
        act.dma_start(R["router_b"][:, :], ins["L0_ffn_router_b"].rearrange("(o e) -> o e", o=1).to_broadcast([P, E])).then_inc(self.router_in, 16)
        rows, cols = slice(0, 4 * E), slice(CORE_COLUMNS, SEL_COLUMNS)
        act.dma_start(R["const"][rows, cols], ins["constants"][rows, cols]).then_inc(self.const_in, 16)
        v = self.wd[:, :].rearrange("p (j d) -> p j d", d=D)
        act.dma_start(v[:, 0:1, :], ins["L0_ffn_shared_w2"].rearrange("(j e) h d -> (e h) j d", e=2)).then_inc(self.wd_in, 16)
        act.dma_start(v[:, 1:, :], ins["L0_ffn_routed_w2"].rearrange("(j e) h d -> (e h) j d", e=2)).then_inc(self.wd_in, 16)

    def scalar_router(self, act):
        act.wait_ge(self.router_in, 32)
        act.activation(self.R["rw_parts"][:, 0:E], self.R["rw"][:, :], ACT.Copy).then_inc(self.router_high, 1)

    def scalar_gate(self, act):
        act.wait_ge(self.wg_in, 32)
        act.activation(self.R["wg_hi"][:, :], self.wg[:, :], ACT.Copy).then_inc(self.hi_ready, 1)

    def scalar_weights(self, act):
        R = self.R
        act.wait_ge(self.wu_in, 32)
        act.activation(R["wu_hi"][:, :], self.wu[:, :], ACT.Copy).then_inc(self.hi_ready, 1)
        act.wait_ge(self.wd_in, 32)
        act.activation(self.wd_half[:, :], self.wd[:, :], ACT.Copy, scale=0.5).then_inc(self.halved, 1)
        act.wait_ge(self.const_in, 16)
        act.activation(R["spread_gates"][:, :], R["sel"][0:4 * E, :], ACT.Copy).then_inc(self.gates_spreader, 1)
        act.wait_ge(self.halved, 1)
        act.activation(R["wd_hi"][:, :], self.wd_half[:, :], ACT.Copy).then_inc(self.hi_ready, 1)

    def pool_router(self, pool):
        pool.wait_ge(self.router_high, 1)
        pool.tensor_tensor(self.R["rw_parts"][:, E:2 * E], self.R["rw"][:, :], self.R["rw_parts"][:, 0:E], ALU.subtract)\
            .then_inc(self.router_split, 1)

    def vector_up(self, dve, n):
        name, src = (("wg", self.wg), ("wu", self.wu))[n]
        dve.wait_ge(self.hi_ready, n + 1)
        dve.tensor_tensor(self.R[f"{name}_lo"][:, :], src[:, :], self.R[f"{name}_hi"][:, :], ALU.subtract)\
            .then_inc(self.up_split, 1)

    def pool_down(self, pool):
        pool.wait_ge(self.hi_ready, 3)
        pool.tensor_tensor(self.R["wd_lo"][:, :], self.wd_half[:, :], self.R["wd_hi"][:, :], ALU.subtract)\
            .then_inc(self.down_split, 1)


class MambaWeights:

    def __init__(self, nc, R, ins, ctx):
        def sb(name, shape, dt=F32):
            R[name] = ctx.enter_context(nc.sbuf_tensor(name, shape, dt))
            return R[name]

        def tmp(name, shape, dt=F32):
            return ctx.enter_context(nc.sbuf_tensor(name, shape, dt))

        def sems(names):
            return [ctx.enter_context(nc.semaphore(n)) for n in names.split()]

        self.R, self.ins = R, ins
        W = TAPS * P
        for name, n in (("wz", P + D), ("wx", W), ("wbc", W)):
            sb(f"{name}_hi", [P, n], F32R)
            sb(f"{name}_lo", [P, n], F32R)
        sb("wdt_parts", [P, 2 * HEADS], F32R)
        sb("wo_y", [P, D])
        sb("out_bias", [P, D])
        sb("decay_rate", [P, HEADS])
        sb("dt_bias", [P, HEADS])
        sb("skip", [P, HALF])
        sb("after_r", [P, P], F32R)
        sb("cb_x", [P, 1])
        sb("cb_bc", [P, 1])
        self.rz, self.rx, self.rbc, self.rdt = tmp("rz", [P, D]), tmp("rx", [P, D]), tmp("rbc", [P, D]), tmp("rdt", [HEADS, D])
        self.cw_x, self.cw_bc = tmp("cw_x", [P, TAPS]), tmp("cw_bc", [P, TAPS])
        self.tx, self.tbc = tmp("tx", [P, TAPS, D]), tmp("tbc", [P, TAPS, D])
        self.wo_rows, self.wo_raw, self.wo, self.wo_z = (
            tmp("wo_rows", [P, 2 * D]), tmp("wo_raw", [P, 2 * D]), tmp("wo", [P, 2 * D]), tmp("wo_z", [P, D]))
        self.share, self.lnb_cols = tmp("share", [P, P]), tmp("lnb_cols", [P, 2, P])
        self.lnw, self.lnb = tmp("lnw", [P, 2]), tmp("lnb", [P, 2])
        self.alog, self.dskip, self.dcol, self.dcol8 = (
            tmp("alog", [P, HEADS]), tmp("dskip", [P, HEADS]), tmp("dcol", [P, 1]), tmp("dcol8", [P, HEADS]))
        (self.cleared, self.rows_in, self.small, self.own_skip, self.dt_turned, self.dt_high, self.dt_split, self.x_turned,
         self.bc_turned, self.wo_turned, self.x_high, self.bc_high, self.z_high, self.raw_ready, self.wo_ready,
         self.mean_ready, self.wo_z_ready, self.z_turned, self.rate_exp, self.weights_ready, self.rate_ready,
         self.conv_split, self.taps_ready, self.centred) = sems(
            "cleared rows_in small own_skip dt_turned dt_high dt_split x_turned bc_turned wo_turned x_high bc_high z_high "
            "raw_ready wo_ready mean_ready wo_z_ready z_turned rate_exp weights_ready rate_ready conv_split taps_ready centred")
        bk = R["bank"]
        self.x_bank, self.bc_bank, self.wo_bank, self.z_bank, self.mean_bank, self.dt_bank = bk[0], bk[2], bk[5], bk[7], bk[6], bk[7]

    def clear(self, dve):
        dve.memset(self.rbc[:, :], 0.0).then_inc(self.cleared, 1)
        dve.memset(self.cw_bc[:, :], 0.0).then_inc(self.cleared, 1)
        dve.memset(self.R["cb_bc"][:, :], 0.0).then_inc(self.cleared, 1)
        dve.memset(self.share[:, :], 1.0 / (2 * HALF))

    def sync(self, sp):
        R, ins = self.R, self.ins
        W_in, conv_w, conv_b = ins["L0_attn_W_in"], ins["L0_attn_conv_w"], ins["L0_attn_conv_b"]
        B0, C0, DT0 = 2 * HALF, 2 * HALF + STATE, 2 * HALF + 2 * STATE

        def col(v):
            return v.rearrange("(p o) -> p o", o=1)

        def row(v):
            return v.rearrange("(o e) -> o e", o=1).to_broadcast([P, HEADS])

        loads = [(R["const"][:, SEL_COLUMNS:], ins["constants"][:, SEL_COLUMNS:]),
                 (self.wo_rows[:, :], ins["L0_attn_W_out"]), (self.rz[:, :], W_in[0:HALF, :]),
                 (self.rx[:, :], W_in[HALF:2 * HALF, :]), (self.rdt[:, :], W_in[DT0:DT0 + HEADS, :]),
                 (self.cw_x[:, :], conv_w[0:HALF, 0, :]), (R["cb_x"][:, :], col(conv_b[0:HALF]))]
        for r in range(BLOCKS + 1):
            src = C0 if r < BLOCKS else B0
            rows = slice(r * STATE, (r + 1) * STATE)
            loads += [(self.rbc[rows, :], W_in[src:src + STATE, :]),
                      (self.cw_bc[rows, :], conv_w[src - HALF:src - HALF + STATE, 0, :]),
                      (R["cb_bc"][rows, :], col(conv_b[src - HALF:src - HALF + STATE]))]
        small = [(self.alog[:, :], row(ins["L0_attn_A_log"])), (self.dskip[:, :], row(ins["L0_attn_Dskip"])),
                 (R["dt_bias"][:, :], row(ins["L0_attn_dt_bias"]))]
        for j in range(2):
            small += [(self.lnw[:, j:j + 1], col(ins["L0_attn_ln_w"][j * P:(j + 1) * P])),
                      (self.lnb[:, j:j + 1], col(ins["L0_attn_ln_b"][j * P:(j + 1) * P]))]
        self.loads = 16 * len(loads), 16 * len(small)
        sp.wait_ge(self.cleared, 3)
        for dst, src in loads:
            sp.dma_start(dst, src).then_inc(self.rows_in, 16)
        for dst, src in small:
            sp.dma_start(dst, src).then_inc(self.small, 16)

    def taps(self, engine):
        engine.wait_ge(self.rows_in, self.loads[0])
        for t in range(TAPS):
            engine.tensor_scalar(self.tx[:, t, :], self.rx[:, :], self.cw_x[:, t:t + 1], None, ALU.mult)
            i = engine.tensor_scalar(self.tbc[:, t, :], self.rbc[:, :], self.cw_bc[:, t:t + 1], None, ALU.mult)
        i.then_inc(self.taps_ready, 1)

    def vector_skip(self, dve):
        R = self.R
        dve.wait_ge(self.small, self.loads[1])
        dve.tensor_tensor(self.dcol8[:, :], self.dskip[:, :], R["head_of"], ALU.mult).then_inc(self.own_skip, 1)
        dve.tensor_copy(self.lnb_cols[:, :, :], self.lnb[:, :].rearrange("p (j o) -> p j o", o=1).to_broadcast([P, 2, P]))
        dve.wait_ge(self.own_skip, 1)
        dve.tensor_reduce(self.dcol[:, :], self.dcol8[:, :], AX.X, ALU.add).then_inc(self.own_skip, 1)
        dve.wait_ge(self.own_skip, 2)
        dve.tensor_scalar(R["skip"][:, :], R["ident"], self.dcol[:, 0:1], None, ALU.mult)


    def scalar_rate(self, act):
        act.wait_ge(self.small, self.loads[1])
        act.activation(self.alog[:, :], self.alog[:, :], ACT.Exp).then_inc(self.rate_exp, 1)

    def scalar_dt(self, act):
        act.wait_ge(self.dt_turned, 1)
        act.activation(self.R["wdt_parts"][:, 0:HEADS], self.dt_bank[:, 0:HEADS], ACT.Copy).then_inc(self.dt_high, 1)

    def scalar_conv(self, act):
        act.wait_ge(self.x_turned, 1)
        act.activation(self.R["wx_hi"][:, :], self.x_bank[:, :], ACT.Copy).then_inc(self.x_high, 1)
        act.activation(self.R["after_r"][:, :], self.R["after"], ACT.Copy)
        act.wait_ge(self.bc_turned, 1)
        act.activation(self.R["wbc_hi"][:, :], self.bc_bank[:, :], ACT.Copy).then_inc(self.bc_high, 1)

    def scalar_z(self, act):
        act.wait_ge(self.z_turned, 1)
        act.activation(self.R["wz_hi"][:, :], self.z_bank[:, 2 * D:4 * D], ACT.Copy).then_inc(self.z_high, 1)

    def vector_rate(self, dve):
        dve.wait_ge(self.rate_exp, 1)
        dve.tensor_scalar(self.R["decay_rate"][:, :], self.alog[:, :], -1.0, None, ALU.mult).then_inc(self.rate_ready, 1)

    def vector_dt(self, dve):
        dve.wait_ge(self.dt_high, 1)
        dve.tensor_tensor(self.R["wdt_parts"][:, HEADS:2 * HEADS], self.dt_bank[:, 0:HEADS],
                          self.R["wdt_parts"][:, 0:HEADS], ALU.subtract).then_inc(self.dt_split, 1)

    def vector_out(self, dve):
        dve.wait_ge(self.wo_turned, 1)
        dve.tensor_copy(self.wo_raw[:, :], self.wo_bank[:, 0:2 * D]).then_inc(self.raw_ready, 1)
        dve.wait_ge(self.raw_ready, 1)
        for j in range(2):
            i = dve.tensor_scalar(self.wo[:, j * D:(j + 1) * D], self.wo_raw[:, j * D:(j + 1) * D], self.lnw[:, j:j + 1],
                                  None, ALU.mult)
        i.then_inc(self.wo_ready, 1)

    def vector_conv(self, dve):
        dve.wait_ge(self.x_high, 1)
        dve.tensor_tensor(self.R["wx_lo"][:, :], self.x_bank[:, :], self.R["wx_hi"][:, :], ALU.subtract)
        dve.wait_ge(self.bc_high, 1)
        dve.tensor_tensor(self.R["wbc_lo"][:, :], self.bc_bank[:, :], self.R["wbc_hi"][:, :], ALU.subtract)\
            .then_inc(self.conv_split, 1)

    def vector_centre(self, dve):
        dve.wait_ge(self.mean_ready, 1)
        dve.tensor_tensor(self.wo_z[:, :], self.wo[:, D:2 * D], self.mean_bank[:, 0:D], ALU.subtract).then_inc(self.wo_z_ready, 1)
        dve.tensor_tensor(self.R["wo_y"][:, :], self.wo[:, 0:D], self.mean_bank[:, 0:D], ALU.subtract)
        dve.tensor_copy(self.R["out_bias"][:, :], self.mean_bank[:, D:2 * D]).then_inc(self.centred, 1)

    def vector_z(self, dve):
        dve.wait_ge(self.z_high, 1)
        dve.tensor_tensor(self.R["wz_lo"][:, :], self.z_bank[:, 2 * D:4 * D], self.R["wz_hi"][:, :], ALU.subtract)\
            .then_inc(self.weights_ready, 1)

    def turn(self, pe):
        ident = self.R["ident"]
        pe.transpose(self.dt_bank[:, 0:HEADS], self.rdt[:, :], ident[0:HEADS, 0:HEADS]).then_inc(self.dt_turned, 1)
        for j in range(2):
            i = pe.transpose(self.wo_bank[:, j * D:(j + 1) * D], self.wo_rows[:, j * D:(j + 1) * D], ident)
        i.then_inc(self.wo_turned, 1)
        for t in range(TAPS):
            i = pe.transpose(self.x_bank[:, t * P:(t + 1) * P], self.tx[:, t, :], ident)
        i.then_inc(self.x_turned, 1)
        for t in range(TAPS):
            i = pe.transpose(self.bc_bank[:, t * P:(t + 1) * P], self.tbc[:, t, :], ident)
        i.then_inc(self.bc_turned, 1)

    def centre(self, pe):
        pe.wait_ge(self.dt_split, 1)
        pe.transpose(self.z_bank[:, 2 * D:3 * D], self.rz[:, :], self.R["ident"])
        pe.wait_ge(self.wo_ready, 1)
        for j in range(2):
            pe.matmul(self.mean_bank[:, 0:D], self.share[:, :], self.wo[:, j * D:(j + 1) * D], start=(j == 0), stop=(j == 1))
        for j in range(2):
            i = pe.matmul(self.mean_bank[:, D:2 * D], self.lnb_cols[:, j, :], self.wo_raw[:, j * D:(j + 1) * D],
                          start=(j == 0), stop=(j == 1))
        i.then_inc(self.mean_ready, 1)

    def z_to_output(self, pe):
        pe.wait_ge(self.wo_z_ready, 1)
        pe.matmul(self.z_bank[:, 3 * D:4 * D], self.rz[:, :], self.wo_z[:, :], start=True, stop=True).then_inc(self.z_turned, 1)


class MambaSignals:

    def __init__(self, nc, ctx):
        def sems(names):
            return [ctx.enter_context(nc.semaphore(f"m_{n}")) for n in names.split()]

        self.tensor = sems("xT_ready dt_ready cum_ready total_ready z_ready x_ready bc_ready xt_ready bt_ready g_ready "
                           "g_spread seg0_ready seg1_ready y_ready st_ready stt_ready yoff_ready yt_ready o_ready")
        self.scalar = sems("xh_ready exp_ready decay_ready carry_ready xc_ready cb_ready e0_ready e1_ready "
                           "states_copied xb_act yT_ready")
        self.vector = sems("xl_ready neg_ready at_ready ab_ready totx_ready xdt_ready xdec_ready xb_dve bm_ready "
                           "gm_ready m0_ready m1_ready scan_done yo_ready yz_ready ve2_ready zstats_done x_done")
        self.gpsimd = sems("r0_ready r1_ready cm_ready rstd2_ready bias_added state_ready")

    @staticmethod
    def start(engine, made):
        for one in made:
            engine.sem_inc(one, 1)


def mamba_phase(nc, R, signals, norm, next_norm, next_routing, weights):
    X, bk = R["X"], R["bank"]
    with ExitStack() as ctx:
        def sb(name, shape, dt=F32):
            return ctx.enter_context(nc.sbuf_tensor(f"m_{name}", shape, dt))

        def sems(names):
            return [R["all_phases"].enter_context(nc.semaphore(f"m_{n}")) for n in names.split()]

        TH = SEQ_TILES * HEADS
        NC = BLOCKS * STATE
        PAD = TAPS - 1
        xn, xn_ready = norm.xn, norm.xn_ready
        xh = [sb(f"xh{p}", [P, PAD + L], F32R) for p in range(2)]
        xl = [sb(f"xl{p}", [P, PAD + L], F32R) for p in range(2)]
        raw, neg, u, v, w, q, pos = (sb(n, [P, TH]) for n in ("raw", "neg", "u", "v", "w", "q", "pos"))
        dt = [sb(f"dt{p}", [P, TH]) for p in range(2)]
        at = sb("at", [P, TH])
        ecd = [sb(f"ecd{p}", [P, 2 * TH]) for p in range(2)]
        amask, aB = sb("amask", [P, P]), sb("aB", [P, CHUNKS * HGROUPS])
        totX = sb("totX", [TH, CHUNKS])
        carry = sb("carry", [P, STATE, CHUNKS])
        xc, Cc, Bc = sb("xc", [P, L]), sb("Cc", [NC, L]), sb("Bc", [STATE, L])
        xdt, xdec = sb("xdt", [P, L]), sb("xdec", [P, L])
        XB = sb("XB", [P, SEQ_TILES, BLOCKS, HGROUPS, BLOCKS * HDIM])
        Bm, Gm = sb("Bm", [P, SEQ_TILES, BLOCKS, STATE]), sb("Gm", [P, SEQ_TILES, P])
        a_parts = [sb(f"a_{k}", [P, CHUNKS * HGROUPS], F32R) for k in ("hi", "lo")]
        Rg = [[sb(f"Rg{g}{k}", [P, CHUNKS, CHUNK], F32R) for k in ("hi", "lo")] for g in range(HGROUPS)]
        Eg = [sb(f"Eg{g}", [P, L]) for g in range(HGROUPS)]
        Mg = [sb(f"Mg{g}", [P, BLOCKS, SEQ_TILES, CHUNK]) for g in range(HGROUPS)]
        after_chunk, state = sb("after_chunk", [P, STATE, CHUNKS]), sb("state", [P, CHUNKS, STATE])
        STs, Cm = sb("STs", [NC, L]), sb("Cm", [NC, L])
        yo, y = sb("yo", [P, L]), sb("y", [P, L])
        stats2, mv2 = sb("stats2", [P, SEQ_TILES, 2, 6]), sb("mv2", [P, SEQ_TILES, 2])
        ve2, rstd2 = sb("ve2", [P, SEQ_TILES]), sb("rstd2", [P, SEQ_TILES])
        yT = sb("yT", [P, L])

        PZ = [bk[0], bk[2]]
        PS = bk[1]
        PXT, PX, PBT, PST = bk[3], bk[3], bk[3], bk[3]
        PSTT, PYO, PBC, PGR = bk[4], bk[4], bk[4], bk[4]
        PY = bk[5]
        PSEG = [bk[6], bk[7]]
        PYT = bk[7]
        PXCT, PG = bk[6], bk[6]
        NEXT_XT, NEXT_LOGITS = bk[6], bk[1]
        SUM0, BT0 = 2 * TH, STATE * CHUNKS

        (xT_ready, dt_ready, cum_ready, total_ready, z_ready, x_ready, bc_ready, xt_ready, bt_ready, g_ready, g_spread,
         seg0_ready, seg1_ready, y_ready, st_ready, stt_ready, yoff_ready, yt_ready, o_ready) = signals.tensor
        (xh_ready, exp_ready, decay_ready, carry_ready, xc_ready, cb_ready, e0_ready, e1_ready, states_copied,
         xb_act, yT_ready) = signals.scalar
        (xl_ready, neg_ready, at_ready, ab_ready, totx_ready, xdt_ready, xdec_ready, xb_dve, bm_ready, gm_ready,
         m0_ready, m1_ready, scan_done, yo_ready, yz_ready, ve2_ready, zstats_done, x_done) = signals.vector
        r0_ready, r1_ready, cm_ready, rstd2_ready, bias_added, state_ready = signals.gpsimd
        own_time, own_out, own_decay, own_parts, pads_cleared, xb_cleared = sems(
            "own_time own_out own_decay own_parts pads_cleared xb_cleared")
        TIME_OPS, OUT_OPS = 15, 2

        def now(engine, *which):
            s, which = which[-1], which[:-1]
            for one in which:
                engine.wait_ge(one, s + 2)

        def before(engine, *which):
            s, which = which[-1], which[:-1]
            for one in which:
                engine.wait_ge(one, s + 1)

        def tiles(a, n=D):
            return a[:, :].rearrange("p (t d) -> p t d", d=n)

        def tile(t):
            return slice(t * P, (t + 1) * P)

        def spread_block(engine, c, b):
            src = xdt[c * CHUNK:(c + 1) * CHUNK, :].rearrange("p (t g b k) -> p t g b k", t=SEQ_TILES, g=HGROUPS,
                                                              b=BLOCKS)[:, :, :, b, :]
            return XB[b * CHUNK:(b + 1) * CHUNK, :, c, :, b * HDIM:(b + 1) * HDIM], src

        block = ctx.enter_context(nc.Block())

        @block.gpsimd
        def _(pool):
            for p in range(2):
                pool.memset(xh[p][:, 0:PAD].bitcast(F32), 0.0)
                pool.memset(xl[p][:, 0:PAD].bitcast(F32), 0.0)
            pool.memset(carry[:, :, 0:1], 0.0)
            pool.memset(state[:, 0:1, :], 0.0).then_inc(pads_cleared, 1)
            pool.memset(XB[:, :, :, :, :], 0.0).then_inc(xb_cleared, 1)

            def out_power(s):
                now(pool, ve2_ready, s)
                pool.tensor_tensor(rstd2[:, :], ve2[:, :], R["mhalf"], ALU.pow).then_inc(rstd2_ready, 1)

            def spread_decays(s):
                now(pool, ab_ready, s)
                settle(pool, R["settled"])
                pool.tensor_copy(a_parts[0][:, :], aB[:, :]).then_inc(own_parts, 1)
                pool.wait_ge(own_parts, s * 2 + 1)
                pool.tensor_tensor(a_parts[1][:, :], aB[:, :], a_parts[0][:, :], ALU.subtract).then_inc(own_parts, 1)
                for g, (seg, done) in enumerate(((seg0_ready, r0_ready), (seg1_ready, r1_ready))):
                    before(pool, seg, s)
                    for k in range(2):
                        if k and not g:
                            pool.wait_ge(own_parts, s * 2 + 2)
                        a = a_parts[k][:, :].rearrange("p (c g o) -> p c g o", g=HGROUPS, o=1)[:, :, g, :]
                        i = pool.tensor_tensor(Rg[g][k][:, :, :], a.to_broadcast([P, CHUNKS, CHUNK]),
                                               R["causal"].rearrange("p (o l) -> p o l", o=1)
                                               .to_broadcast([P, CHUNKS, CHUNK]), ALU.mult)
                    i.then_inc(done, 1)

            def add_bias(s):
                pool.wait_ge(xn_ready, s + 1)
                seq = X[:, bass.ds(s * SEQ_TILES, SEQ_TILES), :]
                pool.tensor_tensor(seq, seq, R["out_bias"][:, :].rearrange("p (o d) -> p o d", o=1)
                                   .to_broadcast([P, SEQ_TILES, D]), ALU.add).then_inc(bias_added, 1)

            def states(s):
                now(pool, scan_done, s)
                before(pool, stt_ready, s)
                settle(pool, R["settled"])
                pool.tensor_copy(state[:, 1:, :],
                                 after_chunk[:, :, 0:CHUNKS - 1].rearrange("p n c -> p c n")).then_inc(state_ready, 1)

            def step(s, p, first, last):
                add_bias(s)
                if not first:
                    out_power(s - 1)
                if not last:
                    norm.power(pool, s + 2, p)
                else:
                    next_norm.power(pool, 0, 0)
                    next_norm.power(pool, 1, 1)
                now(pool, cb_ready, s)
                before(pool, yoff_ready, s)
                pool.tensor_tensor(tiles(Cm, P), tiles(Cc, P),
                                   R["own_chunk"][0:NC, :].rearrange("p (o l) -> p o l", o=1)
                                   .to_broadcast([NC, SEQ_TILES, P]), ALU.mult).then_inc(cm_ready, 1)
                if first:
                    states(s)
                if not last:
                    spread_decays(s + 1)
                if not first:
                    states(s)

            spread_decays(0)
            run_steps(pool, step)
            out_power(B - 1)
            next_routing.softmax_power(pool, 0)

        @block.scalar
        def _(act):

            def x_high(s, p):
                now(act, xT_ready, s)
                act.activation(xh[p][:, PAD:], PXT[:, :], ACT.Copy).then_inc(xh_ready, 1)

            def dt_exp(s):
                now(act, neg_ready, s)
                act.activation(u[:, :], neg[:, :], ACT.Exp).then_inc(exp_ready, 1)

            def decays(s, p):
                now(act, total_ready, s)
                act.activation(ecd[p][:, :], PS[:, SUM0:SUM0 + 2 * TH], ACT.Exp).then_inc(decay_ready, 1)

            def carries(s):
                before(act, scan_done, s)
                act.activation(carry[:, :, 1:], PS[:, 257:256 + CHUNKS].rearrange("p (o c) -> p o c", o=1)
                               .to_broadcast([P, STATE, CHUNKS - 1]), ACT.Exp).then_inc(carry_ready, 1)

            def states_copy(s):
                now(act, stt_ready, s)
                before(act, yoff_ready, s)
                act.activation(STs[:, :], PSTT[0:NC, :], ACT.Copy).then_inc(states_copied, 1)

            def y_copy(s):
                now(act, yt_ready, s)
                before(act, o_ready, s)
                act.activation(yT[:, :], PYT[:, :], ACT.Copy).then_inc(yT_ready, 1)

            def x_out(s):
                now(act, x_ready, s)
                before(act, y_ready, s)
                act.activation(xc[:, :], PX[:, :], ACT.Silu, bias=R["cb_x"][:, 0:1]).then_inc(xc_ready, 1)

            def bc_out(s):
                now(act, bc_ready, s)
                before(act, cm_ready, s)
                act.activation(Cc[:, :], PBC[0:NC, :], ACT.Silu, bias=R["cb_bc"][0:NC, 0:1])
                act.activation(Bc[:, :], PBC[NC:NC + STATE, :], ACT.Silu, bias=R["cb_bc"][NC:NC + STATE, 0:1])\
                    .then_inc(cb_ready, 1)

            x_high(0, 0)
            weights.scalar_dt(act)
            weights.scalar_conv(act)
            weights.scalar_rate(act)
            dt_exp(0)
            x_out(0)
            weights.scalar_z(act)
            x_high(1, 1)
            bc_out(0)

            def exps(s):
                for g, (seg, m, done) in enumerate(((seg0_ready, m0_ready, e0_ready), (seg1_ready, m1_ready, e1_ready))):
                    now(act, seg, s)
                    before(act, m, s)
                    act.activation(Eg[g][:, :], PSEG[g][:, :], ACT.Exp).then_inc(done, 1)

            def spread_x(s):
                now(act, xdt_ready, s)
                for c in range(BLOCKS // 2, BLOCKS):
                    for b in range(BLOCKS):
                        dst, src = spread_block(act, c, b)
                        i = act.activation(dst, src, ACT.Copy)
                i.then_inc(xb_act, 1)

            def step(s, p, first, last):
                if first:
                    decays(0, 0)
                    carries(0)
                    dt_exp(1)
                    act.wait_ge(xb_cleared, 1)
                    spread_x(0)
                    exps(0)
                    return
                decays(s, p)
                carries(s)
                states_copy(s - 1)
                if not last:
                    x_high(s + 1, 1 - p)
                exps(s)
                if not last:
                    dt_exp(s + 1)
                x_out(s)
                y_copy(s - 1)
                bc_out(s)
                spread_x(s)
            run_steps(act, step)
            states_copy(B - 1)
            next_routing.x_high(act, 0, 0, NEXT_XT)
            y_copy(B - 1)

        @block.vector
        def _(dve):
            def heads(a, at):
                return a[:, at:at + TH].rearrange("p (h o) -> p h o", o=1).to_broadcast([P, TH, HDIM])

            def per_head(a):
                return a[:, :].rearrange("p (h o) -> p h o", o=HDIM)

            def x_low(s, p):
                now(dve, xh_ready, s)
                dve.tensor_tensor(xl[p][:, PAD:], PXT[:, :], xh[p][:, PAD:], ALU.subtract).then_inc(xl_ready, 1)

            class TimeSteps:

                def __init__(self, s, p):
                    self.s, self.p = s, p
                    self.own = Own(dve, own_time, s * TIME_OPS, TIME_OPS)

                def th(self, a):
                    return a[:, 0:TH].rearrange("p (t h) -> p t h", h=HEADS)

                def part(self, k):
                    return PS[:, 0:2 * TH].rearrange("p (t k h) -> p t k h", k=2, h=HEADS)[:, :, k, :]

                def row(self, a):
                    return a[:, :].rearrange("p (o h) -> p o h", o=1).to_broadcast([P, SEQ_TILES, HEADS])

                def biased(self):
                    now(dve, dt_ready, self.s)
                    return dve.tensor_tensor(self.th(v), self.part(1), self.row(R["dt_bias"]), ALU.add)

                def raw(self):
                    return dve.tensor_tensor(self.th(raw), self.part(0), self.th(v), ALU.add)

                def negative(self):
                    return dve.scalar_tensor_tensor(neg[:, :], raw[:, :], -1.0, raw[:, :], ALU.mult, ALU.min)\
                        .then_inc(neg_ready, 1)

                def positive(self):
                    dve.tensor_scalar(pos[:, :], raw[:, :], 0.0, None, ALU.max)

                def plus_two(self):
                    now(dve, exp_ready, self.s)
                    return dve.tensor_scalar(v[:, :], u[:, :], 2.0, None, ALU.add)

                def inverse(self):
                    return dve.reciprocal(w[:, :], v[:, :])

                def ratio(self):
                    return dve.tensor_tensor(v[:, :], u[:, :], w[:, :], ALU.mult)

                def square(self):
                    return dve.tensor_tensor(w[:, :], v[:, :], v[:, :], ALU.mult)

                def term(self, k):
                    if k == len(ARTANH) - 1:
                        return dve.tensor_scalar(q[:, :], w[:, :], ARTANH[k], None, ALU.mult)
                    return dve.scalar_tensor_tensor(q[:, :], q[:, :], ARTANH[k], w[:, :] if k else v[:, :], ALU.add, ALU.mult)

                def softplus(self):
                    return dve.scalar_tensor_tensor(dt[self.p][:, :], q[:, :], 2.0, pos[:, :], ALU.mult, ALU.add)

                def decay(self):
                    dve.tensor_tensor(self.th(at), self.th(dt[self.p]), self.row(R["decay_rate"]), ALU.mult)\
                        .then_inc(at_ready, 1)

            def block_decays(s):
                now(dve, cum_ready, s)
                dve.tensor_tensor(amask[:, :].rearrange("p (c b) -> p c b", b=BLOCKS),
                                  PS[:, 128:256].rearrange("p (c b) -> p c b", b=BLOCKS),
                                  R["own_block"].rearrange("p (o b) -> p o b", o=1)
                                  .to_broadcast([P, CHUNKS * HGROUPS, BLOCKS]), ALU.mult).then_inc(own_decay, 1)
                dve.tensor_tensor(totX[:, :].rearrange("p (t c) -> p t c", c=BLOCKS),
                                  PS[0:TH, 272:272 + BLOCKS].rearrange("p (o c) -> p o c", o=1)
                                  .to_broadcast([TH, SEQ_TILES, BLOCKS]),
                                  R["own_tile"][0:TH, :].rearrange("p (t c) -> p t c", c=BLOCKS), ALU.mult)\
                    .then_inc(totx_ready, 1)
                dve.wait_ge(own_decay, s + 1)
                before(dve, r1_ready, s)
                dve.tensor_reduce(aB[:, :], amask[:, :].rearrange("p (c b) -> p c b", b=BLOCKS), AX.X, ALU.add)\
                    .then_inc(ab_ready, 1)

            def states_part(s, p):
                now(dve, yoff_ready, s)
                dve.tensor_tensor(per_head(yo), per_head(PYO), heads(ecd[p], 0), ALU.mult).then_inc(yo_ready, 1)

            def y_sum(s):
                now(dve, y_ready, yo_ready, s)
                before(dve, yt_ready, s)
                dve.tensor_tensor(y[:, :], yo[:, :], PY[:, :], ALU.add).then_inc(yz_ready, 1)

            def y_stats(s, t):
                if t == 0:
                    now(dve, yz_ready, s)
                    settle(dve, R["settled"])
                i = dve.bn_stats(stats2[:, t, 0, :], y[:, tile(t)])
                if t == SEQ_TILES - 1:
                    i.then_inc(own_out, 1)

            def y_moments(s, t):
                if t == 0:
                    now(dve, zstats_done, s)
                    dve.wait_ge(own_out, s * OUT_OPS + 1)
                    settle(dve, R["settled"])
                i = dve.bn_aggr(mv2[:, t, :], stats2[:, t, :, :].rearrange("p k n -> p (k n)"))
                if t == SEQ_TILES - 1:
                    i.then_inc(own_out, 1)

            def y_variance(s):
                dve.wait_ge(own_out, s * OUT_OPS + 2)
                dve.tensor_scalar(ve2[:, :], mv2[:, :, 1], EPS, None, ALU.add).then_inc(ve2_ready, 1)

            def z_stats(s):
                now(dve, z_ready, s)
                for t in range(SEQ_TILES):
                    i = dve.bn_stats(stats2[:, t, 1, :], PZ[t // 2][:, (t % 2) * 2 * D:(t % 2) * 2 * D + HALF])
                i.then_inc(zstats_done, 1)

            def decayed(s, g, e, done):
                now(dve, e, s)
                dve.tensor_tensor(Mg[g][:, :, :, :].rearrange("p c t l -> p (c t l)"), Eg[g][:, :], PGR[:, :],
                                  ALU.mult).then_inc(done, 1)

            def residual(s):
                now(dve, o_ready, s)
                now(dve, rstd2_ready, s)
                now(dve, bias_added, s)
                for t in range(SEQ_TILES):
                    seq = X[:, bass.ds(s * SEQ_TILES + t, 1), :].rearrange("p o d -> p (o d)")
                    at_col = (t % 2) * 2 * D + HALF
                    i = dve.scalar_tensor_tensor(seq, PZ[t // 2][:, at_col:at_col + D], rstd2[:, t:t + 1], seq,
                                                 ALU.mult, ALU.add)
                i.then_inc(x_done, 1)

            weights.vector_skip(dve)
            x_low(0, 0)
            weights.vector_dt(dve)
            weights.vector_out(dve)
            weights.vector_conv(dve)
            weights.vector_rate(dve)
            g = TimeSteps(0, 0)
            link = g.own.link
            link(g.biased())
            link(g.raw())
            g.negative()
            g.positive()
            dve.wait_ge(weights.rate_ready, 1)
            for line in (g.plus_two, g.inverse, g.ratio, g.square):
                link(line())
            for k in range(len(ARTANH) - 1, -1, -1):
                link(g.term(k))
            link(g.softplus())
            g.decay()
            g.own.close()
            weights.vector_centre(dve)
            block_decays(0)
            weights.vector_z(dve)

            def xdt_product(s, p):
                now(dve, xt_ready, s)
                before(dve, xb_act, s)
                dve.tensor_tensor(per_head(xdt), per_head(PXCT), heads(dt[p], 0), ALU.mult).then_inc(xdt_ready, 1)

            def xdec_product(s, p):
                now(dve, xdt_ready, s)
                now(dve, decay_ready, s)
                before(dve, st_ready, s)
                dve.tensor_tensor(per_head(xdec), per_head(xdt), heads(ecd[p], TH), ALU.mult).then_inc(xdec_ready, 1)

            def b_of_chunks(s):
                now(dve, bt_ready, s)
                dve.tensor_tensor(Bm[:, :, :, :],
                                  PBT[:, BT0:BT0 + SEQ_TILES * STATE].rearrange("p (t o n) -> p t o n", t=SEQ_TILES, o=1)
                                  .to_broadcast([P, SEQ_TILES, BLOCKS, STATE]),
                                  R["own_block"].rearrange("p (a c o) -> p a c o", a=1, o=1)
                                  .to_broadcast([P, SEQ_TILES, BLOCKS, STATE]), ALU.mult).then_inc(bm_ready, 1)

            def g_masked(s):
                now(dve, g_ready, s)
                before(dve, g_spread, s)
                dve.tensor_tensor(Gm[:, :, :], tiles(PG, P),
                                  R["causal_block"].rearrange("p (o l) -> p o l", o=1).to_broadcast([P, SEQ_TILES, P]),
                                  ALU.mult).then_inc(gm_ready, 1)

            def spread_x(s):
                before(dve, y_ready, s)
                for c in range(BLOCKS // 2):
                    for b in range(BLOCKS):
                        spread_one(s, c, b)

            def spread_one(s, c, b):
                dst, src = spread_block(dve, c, b)
                i = dve.tensor_copy(dst, src)
                if (c, b) == (BLOCKS // 2 - 1, BLOCKS - 1):
                    i.then_inc(xb_dve, 1)

            def scan(s):
                now(dve, st_ready, s)
                now(dve, carry_ready, s)
                before(dve, state_ready, s)
                dve.tensor_tensor_scan(after_chunk[:, :, :].rearrange("p n c -> p (n c)"),
                                       carry[:, :, :].rearrange("p n c -> p (n c)"), PST[:, 0:STATE * CHUNKS],
                                       0.0, ALU.mult, ALU.add).then_inc(scan_done, 1)

            def step(s, p, first, last):
                copies = [(c, b) for c in range(BLOCKS // 2) for b in range(BLOCKS)]
                back = not first
                ahead = not last

                def apart(i, work, *args):
                    g.own.mark(i)
                    if first and work not in (norm.moments, norm.variance):
                        if copies:
                            spread_one(0, *copies.pop(0))
                    elif work in (y_stats, y_moments, y_variance):
                        work(s - 1, *args)
                    elif work:
                        work(dve, s + 2, p, *args)
                    g.own.ready()

                def time_lines():
                    apart(g.plus_two(), norm.moments, [0])
                    apart(g.inverse(), norm.moments, [1])
                    apart(g.ratio(), y_moments, 0)
                    apart(g.square(), y_moments, 1)
                    apart(g.term(7), y_moments, 2)
                    apart(g.term(6), y_moments, 3)
                    apart(g.term(5), norm.moments, [2])
                    apart(g.term(4), y_variance)
                    apart(g.term(3), norm.moments, [3])
                    apart(g.term(2), None)
                    apart(g.term(1), norm.variance)
                    apart(g.term(0), None)
                    apart(g.softplus(), None)
                    g.decay()
                    g.own.close()

                def finish():
                    now(dve, g_spread, s)
                    decayed(s, 0, e0_ready, m0_ready)
                    scan(s)
                    decayed(s, 1, e1_ready, m1_ready)
                    if first:
                        block_decays(1)
                    z_stats(s)
                    if ahead:
                        norm.apply(dve, s + 2, p)
                    else:
                        next_norm.first_apply(dve)

                if first:
                    x_low(1, 1)
                    norm.stats(dve, 2)
                    xdt_product(0, 0)
                    b_of_chunks(0)
                    g_masked(0)
                    g = TimeSteps(1, 1)
                    g.own.link(g.biased())
                    g.own.link(g.raw())
                    g.negative()
                    g.positive()
                    xdec_product(0, 0)
                    dve.wait_ge(xb_cleared, 1)
                    time_lines()
                    finish()
                    return
                if ahead:
                    x_low(s + 1, 1 - p)
                    norm.stats(dve, s + 2)
                if back:
                    states_part(s - 1, 1 - p)
                    y_sum(s - 1)
                if ahead:
                    g = TimeSteps(s + 1, 1 - p)
                    apart(g.biased(), y_stats, 0)
                    apart(g.raw(), y_stats, 1)
                    g.negative()
                    g.positive()
                    if back:
                        y_stats(s - 1, 2)
                        y_stats(s - 1, 3)
                    time_lines()
                else:
                    for t in range(SEQ_TILES):
                        y_stats(s - 1, t)
                    next_norm.stats(dve, 0)
                    for t in range(SEQ_TILES):
                        y_moments(s - 1, t)
                    next_norm.moments(dve, 0, 0)
                    y_variance(s - 1)
                    next_norm.variance(dve, 0, 0)
                    next_norm.stats(dve, 1)
                    next_norm.moments(dve, 1, 1)
                    next_norm.variance(dve, 1, 1)
                if back:
                    residual(s - 1)
                xdt_product(s, p)
                if ahead:
                    block_decays(s + 1)
                xdec_product(s, p)
                b_of_chunks(s)
                g_masked(s)
                spread_x(s)
                finish()
            run_steps(dve, step)
            last = B - 1
            next_routing.x_low(dve, 0, 0, NEXT_XT)
            states_part(last, 1)
            y_sum(last)
            g = Gates(next_routing, dve, 0, 0, NEXT_LOGITS)
            g.logits()
            y_stats(last, 0)
            y_stats(last, 1)
            g.largest(0)
            y_stats(last, 2)
            g.equal(0)
            y_stats(last, 3)
            g.order()
            y_moments(last, 0)
            g.first_of()
            y_moments(last, 1)
            g.mark(0)
            y_moments(last, 2)
            g.remove()
            y_moments(last, 3)
            g.largest(1)
            y_variance(last)
            g.equal(1)
            g.distance()
            g.order()
            g.first_of()
            g.mark(1)
            residual(last)
            next_routing.begun = g

        @block.tensor
        def _(pe):
            def four(out, src, ident, done):
                for t in range(SEQ_TILES):
                    i = pe.transpose(out(t), src(t), ident)
                i.then_inc(done, 1)

            def x_turn(s, p):
                pe.wait_ge(xn_ready, s + 1)
                four(lambda t: PXT[:, tile(t)], lambda t: xn[p][:, t, :], R["ident"], xT_ready)

            def times(s, p):
                now(pe, xl_ready, s)
                before(pe, carry_ready, s)
                before(pe, ab_ready, s)
                for t in range(SEQ_TILES):
                    out, tt = PS[:, t * 2 * HEADS:(t + 1) * 2 * HEADS], slice(PAD + t * P, PAD + (t + 1) * P)
                    pe.matmul(out, xh[p][:, tt], R["wdt_parts"][:, :], start=(t == 0), stop=False, skip_group_check=True)
                    i = pe.matmul(out, xl[p][:, tt], R["wdt_parts"][:, :], start=False, stop=True, skip_group_check=True)
                i.then_inc(dt_ready, 1)

            def sums(s):
                now(pe, at_ready, s)
                pe.matmul(PS[:, SUM0:SUM0 + TH], R["upto"], at[:, :], start=True, stop=True)
                pe.matmul(PS[:, SUM0 + TH:SUM0 + 2 * TH], R["after"], at[:, :], start=True, stop=True)
                for c in range(BLOCKS):
                    pe.matmul(PS[:, 128 + c * TH:128 + (c + 1) * TH], R["spread_one"][:, tile(c)], at[:, :],
                              start=True, stop=True)
                pe.matmul(PS[0:TH, 272:272 + BLOCKS], at[:, :], R["own_block"], start=True, stop=True).then_inc(cum_ready, 1)

            def totals(s):
                now(pe, totx_ready, s)
                pe.matmul(PS[:, 256:256 + CHUNKS], R["own_head"][0:TH, :], totX[:, :], start=True, stop=True)\
                    .then_inc(total_ready, 1)

            def conv(out, w, p, done, taps=range(TAPS)):
                for k in taps:
                    i = split_mm(pe, out, R[f"{w}_hi"][:, tile(k)], R[f"{w}_lo"][:, tile(k)], xh[p][:, k:k + L],
                                 xl[p][:, k:k + L], k == 0, k == TAPS - 1)
                if k == TAPS - 1:
                    i.then_inc(done, 1)

            def segment(s, g, done):
                for k in range(2):
                    i = pe.matmul(PSEG[g][:, :], R["after_r"][:, :], Rg[g][k][:, :, :].rearrange("p c l -> p (c l)"),
                                  start=(k == 0), stop=(k == 1))
                i.then_inc(done, 1)

            def segments(s, first):
                now(pe, r0_ready, s)
                before(pe, gm_ready, s)
                segment(s, 0, seg0_ready)
                now(pe, r1_ready, s)
                if not first:
                    before(pe, yT_ready, s - 1)
                segment(s, 1, seg1_ready)

            def states_turn(s):
                now(pe, state_ready, s)
                now(pe, m1_ready, s)
                settle(pe, R["settled"])
                four(lambda t: PSTT[0:NC, tile(t)],
                     lambda t: state[:, t * BLOCKS:(t + 1) * BLOCKS, :].rearrange("p c n -> p (c n)"),
                     R["ident"], stt_ready)

            def states_out(s):
                now(pe, states_copied, s)
                now(pe, cm_ready, s)
                for t in range(SEQ_TILES):
                    i = pe.matmul(PYO[:, tile(t)], Cm[:, tile(t)], STs[:, tile(t)], start=True, stop=True)
                i.then_inc(yoff_ready, 1)

            def y_turn(s):
                now(pe, yz_ready, s)
                four(lambda t: PYT[:, tile(t)], lambda t: y[:, tile(t)], R["ident"], yt_ready)

            def output(s):
                now(pe, yT_ready, s)
                for t in range(SEQ_TILES):
                    at_col = (t % 2) * 2 * D + HALF
                    i = pe.matmul(PZ[t // 2][:, at_col:at_col + D], yT[:, tile(t)], R["wo_y"][:, :], start=False, stop=True,
                                  skip_group_check=True)
                i.then_inc(o_ready, 1)

            def z_and_output(s, p):
                before(pe, x_done, s)
                for t in range(SEQ_TILES):
                    tt = slice(PAD + t * P, PAD + (t + 1) * P)
                    out = PZ[t // 2][:, (t % 2) * 2 * D:(t % 2 + 1) * 2 * D]
                    pe.matmul(out, xh[p][:, tt], R["wz_hi"][:, :], start=(t % 2 == 0), stop=False, skip_group_check=True)
                    pe.matmul(out, xh[p][:, tt], R["wz_lo"][:, :], start=False, stop=False, skip_group_check=True)
                    i = pe.matmul(out, xl[p][:, tt], R["wz_hi"][:, :], start=False, stop=True, skip_group_check=True)
                i.then_inc(z_ready, 1)

            x_turn(0, 0)
            pe.wait_ge(weights.taps_ready, 1)
            weights.turn(pe)
            pe.wait_ge(weights.dt_split, 1)
            times(0, 0)
            pe.wait_ge(weights.conv_split, 1)
            pe.wait_ge(pads_cleared, 1)
            conv(PX[:, :], "wx", 0, x_ready)
            sums(0)
            weights.centre(pe)
            now(pe, xc_ready, 0)
            x_turn(1, 1)
            weights.z_to_output(pe)
            conv(PBC[:, :], "wbc", 0, bc_ready)
            totals(0)

            def xc_turn(s):
                now(pe, xc_ready, s)
                four(lambda t: PXCT[:, tile(t)], lambda t: xc[:, tile(t)], R["ident"], xt_ready)

            def groups(s):
                now(pe, cb_ready, s)
                settle(pe, R["settled"])
                four(lambda t: PBT[:, BT0 + t * STATE:BT0 + (t + 1) * STATE], lambda t: Bc[:, tile(t)],
                     R["ident"][0:STATE, 0:STATE], bt_ready)
                now(pe, xdt_ready, s)
                for t in range(SEQ_TILES):
                    i = pe.matmul(PG[:, tile(t)], Bc[:, tile(t)], Cc[0:STATE, tile(t)], start=True, stop=True)
                i.then_inc(g_ready, 1)

            def chunk_parts(s):
                now(pe, gm_ready, s)
                for c in range(BLOCKS):
                    i = pe.matmul(PGR[:, tile(c)], R["spread"], Gm[:, :, c * CHUNK:(c + 1) * CHUNK], start=True, stop=True)
                i.then_inc(g_spread, 1)
                now(pe, xdec_ready, s)
                now(pe, bm_ready, s)
                for t in range(SEQ_TILES):
                    out = PST[:, 0:STATE * CHUNKS].rearrange("p (n c) -> p c n", c=CHUNKS)[:, t * BLOCKS:(t + 1) * BLOCKS, :]
                    i = pe.matmul(out, xdec[:, tile(t)], Bm[:, t, :, :], start=True, stop=True)
                i.then_inc(st_ready, 1)
                before(pe, yz_ready, s)
                for t in range(SEQ_TILES):
                    pe.matmul(PY[:, tile(t)], xc[:, tile(t)], R["skip"][:, :], start=(t == 0), stop=False,
                              skip_group_check=True)

            def own_part(s):
                now(pe, xb_dve, s)
                now(pe, xb_act, s)
                for g, m in ((0, m0_ready), (1, m1_ready)):
                    now(pe, m, s)
                    for t in range(SEQ_TILES):
                        for c in range(BLOCKS):
                            at_col = t * P + g * BLOCKS * HDIM
                            i = pe.matmul(PY[c * CHUNK:(c + 1) * CHUNK, at_col:at_col + BLOCKS * HDIM],
                                          Mg[g][:, c, t, :], XB[:, t, c, g, :], start=False, stop=True,
                                          skip_group_check=True)
                i.then_inc(y_ready, 1)

            def step(s, p, first, last):
                if first:
                    pe.wait_ge(weights.centred, 1)
                    pe.wait_ge(weights.weights_ready, 1)
                    xc_turn(0)
                    z_and_output(0, 0)
                    now(pe, xl_ready, 1)
                    groups(0)
                    times(1, 1)
                    now(pe, gm_ready, 0)
                    segments(0, first)
                    chunk_parts(0)
                    sums(1)
                    totals(1)
                    own_part(0)
                    return
                states_turn(s - 1)
                if not last:
                    before(pe, scan_done, s)
                    x_turn(s + 1, 1 - p)
                segments(s, first)
                states_out(s - 1)
                if not last:
                    times(s + 1, 1 - p)
                conv(PX[:, :], "wx", p, x_ready)
                now(pe, e1_ready, s)
                y_turn(s - 1)
                before(pe, yo_ready, s)
                conv(PBC[:, :], "wbc", p, bc_ready, range(TAPS - 1))
                output(s - 1)
                conv(PBC[:, :], "wbc", p, bc_ready, [TAPS - 1])
                now(pe, e0_ready, s)
                xc_turn(s)
                if not last:
                    sums(s + 1)
                groups(s)
                z_and_output(s, p)
                if not last:
                    totals(s + 1)
                chunk_parts(s)
                own_part(s)
            run_steps(pe, step)
            states_turn(B - 1)
            now(pe, gm_ready, B - 1)
            next_routing.x_turn(pe, 0, 0, NEXT_XT)
            states_out(B - 1)
            next_routing.router(pe, 0, 0, NEXT_LOGITS)
            y_turn(B - 1)
            output(B - 1)


def program(nc, ins, out):
    with ExitStack() as ctx:
        R = {"all_phases": ctx}
        allocate(nc, R, ins, ctx)
        norms = [Norm(nc, R, ctx, tag) for tag in ("ffn1", "mamba", "ffn2")]
        loading, weights = Loading(nc, R, ins, ctx), MambaWeights(nc, R, ins, ctx)
        routings = [Routing(nc, R, ctx, tag, norm) for tag, norm in (("ffn1", norms[0]), ("ffn2", norms[2]))]
        signals = MambaSignals(nc, ctx)
        ffn_phase(nc, "ffn1", R, norms[0], routings[0], norms[1], loading, weights, signals, None)
        mamba_phase(nc, R, signals, norms[1], norms[2], routings[1], weights)
        ffn_phase(nc, "ffn2", R, norms[2], routings[1], None, None, None, None, out.rearrange("b (t p) d -> b p t d", p=P))


def kernel(**inputs):
    import numpy as np
    import concourse.bacc as bacc
    from concourse.bass_utils import run_bass_kernel_spmd

    nc = bacc.Bacc("TRN2", target_bir_lowering=False, num_devices=1)
    arrays = {name: np.ascontiguousarray(a) for name, a in inputs.items()}
    arrays["constants"] = constants()
    ins = {name: nc.dram_tensor(name, a.shape, mybir.dt.from_np(a.dtype), kind="ExternalInput").ap()
           for name, a in arrays.items()}
    out = nc.dram_tensor("out", (B, L, D), F32, kind="ExternalOutput").ap()
    program(nc, ins, out)
    return run_bass_kernel_spmd(nc, [arrays], core_ids=[0]).results[0]["out"]
```
